# Optimizing a Trainium2 kernel written in Bass

```python
import numpy as np
import jax
import jax.numpy as jnp

def _softmax(x, axis=-1):
    return jax.nn.softmax(x, axis=axis)

def _gelu(x):
    return jax.nn.gelu(x, approximate=True)

def _silu(x):
    return jax.nn.silu(x)

def _sigmoid(x):
    return jax.nn.sigmoid(x)

def _layernorm(x, axis=-1, eps=1e-05):
    m = jnp.mean(x, axis=axis, keepdims=True)
    v = jnp.var(x, axis=axis, keepdims=True)
    return (x - m) / jnp.sqrt(v + eps)

def _scatter_add(tgt, idx, src, axis=0):
    return tgt.at[idx].add(src)

def _segment_sum(src, seg, n):
    return jax.ops.segment_sum(src, seg, n)
kernel_name = 'mk_xattn_seq_d4_seqx_r8_894973'

def setup_inputs(seed: int=0):
    np.random.seed(seed)
    _w = jnp.asarray

    def _rec_inputs():
        import jax
        import jax.numpy as jnp
        _rk = jax.random.key(seed)
        x = 7.22e-05 + 1 * jax.random.normal(jax.random.fold_in(_rk, 1), (8, 256, 128), jnp.float32)
        _lenS = 256 - jax.random.randint(jax.random.fold_in(_rk, 7), (8,), 0, max(1, 256 // 4) + 1, jnp.int32)
        _lenS2 = 512 - jax.random.randint(jax.random.fold_in(_rk, 8), (8,), 0, max(1, 512 // 4) + 1, jnp.int32)
        _ctx_768P = jax.random.normal(jax.random.fold_in(_rk, 11), (8, 16, 96), jnp.float32)
        _ctx_768c = jax.random.dirichlet(jax.random.fold_in(_rk, 511), 0.3 * jnp.ones((16,), jnp.float32), (8, 512))
        _ctx_768t = jnp.einsum('bsk,bkd->bsd', _ctx_768c, _ctx_768P)
        _ctx_768t = _ctx_768t * jax.lax.rsqrt(jnp.mean(jnp.square(_ctx_768t)) + 1e-12) * 0.953939
        ctx_768 = 0.000651243 + 0.998673 * (_ctx_768t + 0.3 * jax.random.normal(jax.random.fold_in(_rk, 611), (8, 512, 96), jnp.float32))
        return (x, ctx_768)
    x, ctx_768 = _rec_inputs()

    def _L0_xattn_setup():
        import jax, jax.numpy as jnp
        import numpy as np
        DIM = 128
        HEADS = 16
        D_HEAD = 64
        INNER = HEADS * D_HEAD
        CTX_DIM = 96
        FF_INNER = 4 * DIM
        EPS = 1e-05
        SCALE = D_HEAD ** (-0.5)

        def _layer_norm(x, g, b):
            m = jnp.mean(x, axis=-1, keepdims=True)
            v = jnp.mean(jnp.square(x - m), axis=-1, keepdims=True)
            return (x - m) * jax.lax.rsqrt(v + EPS) * g + b

        def _attention(x, ctx, wq, wk, wv, wo, bo):
            B, S, _ = x.shape
            T = ctx.shape[1]
            q = (x @ wq).reshape(B, S, HEADS, D_HEAD).transpose(0, 2, 1, 3)
            k = (ctx @ wk).reshape(B, T, HEADS, D_HEAD).transpose(0, 2, 1, 3)
            v = (ctx @ wv).reshape(B, T, HEADS, D_HEAD).transpose(0, 2, 1, 3)
            attn = jnp.einsum('bhid,bhjd->bhij', q, k) * SCALE
            attn = jax.nn.softmax(attn, axis=-1)
            out = jnp.einsum('bhij,bhjd->bhid', attn, v)
            out = out.transpose(0, 2, 1, 3).reshape(B, S, INNER)
            return out @ wo + bo
        key = jax.random.key(seed)
        ks = jax.random.split(key, 20)
        rn = lambda k, shape, s=0.02: jax.random.normal(k, shape, dtype=jnp.float32) * s
        inp = {'hidden_states': jax.random.normal(ks[0], (4, 256, DIM), dtype=jnp.float32), 'context': jax.random.normal(ks[1], (4, 77, CTX_DIM), dtype=jnp.float32), 'wq1': rn(ks[2], (DIM, INNER)), 'wk1': rn(ks[3], (DIM, INNER)), 'wv1': rn(ks[4], (DIM, INNER)), 'wo1': rn(ks[5], (INNER, DIM)), 'bo1': jnp.zeros((DIM,), jnp.float32), 'wq2': rn(ks[6], (DIM, INNER)), 'wk2': rn(ks[7], (CTX_DIM, INNER)), 'wv2': rn(ks[8], (CTX_DIM, INNER)), 'wo2': rn(ks[9], (INNER, DIM)), 'bo2': jnp.zeros((DIM,), jnp.float32), 'w_ff1': rn(ks[10], (DIM, 2 * FF_INNER)), 'b_ff1': jnp.zeros((2 * FF_INNER,), jnp.float32), 'w_ff2': rn(ks[11], (FF_INNER, DIM)), 'b_ff2': jnp.zeros((DIM,), jnp.float32), 'ln1_g': jnp.ones((DIM,), jnp.float32), 'ln1_b': jnp.zeros((DIM,), jnp.float32), 'ln2_g': jnp.ones((DIM,), jnp.float32), 'ln2_b': jnp.zeros((DIM,), jnp.float32), 'ln3_g': jnp.ones((DIM,), jnp.float32), 'ln3_b': jnp.zeros((DIM,), jnp.float32)}
        return inp
    _L0_xattn_all = _L0_xattn_setup()
    _L0_xattn_in = {k: v for k, v in _L0_xattn_all.items() if k in ('wq1', 'wk1', 'wv1', 'wo1', 'bo1', 'wq2', 'wk2', 'wv2', 'wo2', 'bo2', 'w_ff1', 'b_ff1', 'w_ff2', 'b_ff2', 'ln1_g', 'ln1_b', 'ln2_g', 'ln2_b', 'ln3_g', 'ln3_b')}
    del _L0_xattn_all

    def _L1_xattn_setup():
        import jax, jax.numpy as jnp
        import numpy as np
        D_TEXT, D_AUDIO, D_HID = (128, 96, 128)
        EPS = 1e-05

        def layer_norm(x, gamma, beta):
            mu = jnp.mean(x, axis=-1, keepdims=True)
            var = jnp.mean(jnp.square(x - mu), axis=-1, keepdims=True)
            return (x - mu) * jax.lax.rsqrt(var + EPS) * gamma + beta
        key = jax.random.key(seed)
        ks = jax.random.split(key, 8)
        B, L, S = (16, 128, 256)

        def xavier(k, shape):
            bound = np.sqrt(6.0 / (shape[0] + shape[1]))
            return jax.random.uniform(k, shape, jnp.float32, -bound, bound)
        return {'H_l': jax.random.normal(ks[0], (B, L, D_TEXT), jnp.float32), 'H_a': jax.random.normal(ks[1], (B, S, D_AUDIO), jnp.float32), 'W_text': xavier(ks[2], (D_TEXT, D_HID)), 'b_text': jnp.zeros((D_HID,), jnp.float32), 'W_audio': xavier(ks[3], (D_AUDIO, D_HID)), 'b_audio': jnp.zeros((D_HID,), jnp.float32), 'W_out': xavier(ks[4], (D_HID, D_HID)), 'b_out': jnp.zeros((D_HID,), jnp.float32), 'g1': jnp.ones((D_HID,), jnp.float32), 'beta1': jnp.zeros((D_HID,), jnp.float32), 'g2': jnp.ones((D_HID,), jnp.float32), 'beta2': jnp.zeros((D_HID,), jnp.float32), 'g_out': jnp.ones((D_HID,), jnp.float32), 'beta_out': jnp.zeros((D_HID,), jnp.float32)}
    _L1_xattn_all = _L1_xattn_setup()
    _L1_xattn_in = {k: v for k, v in _L1_xattn_all.items() if k in ('W_text', 'b_text', 'W_audio', 'b_audio', 'W_out', 'b_out', 'g1', 'beta1', 'g2', 'beta2', 'g_out', 'beta_out')}
    del _L1_xattn_all

    def _L2_xattn_setup():
        import jax, jax.numpy as jnp
        import numpy as np
        B, S, L = (2, 256, 64)
        WIDTH, HEADS, CTX = (128, 16, 96)
        HD = WIDTH // HEADS
        EPS = 1e-05

        def _layernorm(x, g, b):
            m = jnp.mean(x, axis=-1, keepdims=True)
            v = jnp.mean(jnp.square(x - m), axis=-1, keepdims=True)
            return (x - m) * jax.lax.rsqrt(v + EPS) * g + b

        def _mha(q_in, kv_in, wq, bq, wk, bk, wv, bv, wo, bo):
            b = q_in.shape[0]
            q = (q_in @ wq.T + bq).reshape(b, -1, HEADS, HD).transpose(0, 2, 1, 3)
            k = (kv_in @ wk.T + bk).reshape(b, -1, HEADS, HD).transpose(0, 2, 1, 3)
            v = (kv_in @ wv.T + bv).reshape(b, -1, HEADS, HD).transpose(0, 2, 1, 3)
            scores = jnp.einsum('bhqd,bhkd->bhqk', q, k) * HD ** (-0.5)
            p = jax.nn.softmax(scores, axis=-1)
            o = jnp.einsum('bhqk,bhkd->bhqd', p, v)
            o = o.transpose(0, 2, 1, 3).reshape(b, -1, WIDTH)
            return o @ wo.T + bo
        key = jax.random.key(seed)
        ks = jax.random.split(key, 32)

        def xav(k, shape, gain=1.0):
            fan_out, fan_in = shape
            a = gain * np.sqrt(6.0 / (fan_in + fan_out))
            return jax.random.uniform(k, shape, jnp.float32, -a, a)
        g2 = 1.0 / np.sqrt(2.0)
        inp = {'x': jax.random.normal(ks[0], (B, S, WIDTH), jnp.float32), 'context': jax.random.normal(ks[1], (B, L, CTX), jnp.float32), 'ln1_g': jnp.ones((WIDTH,), jnp.float32), 'ln1_b': jnp.zeros((WIDTH,), jnp.float32), 'ln2_g': jnp.ones((WIDTH,), jnp.float32), 'ln2_b': jnp.zeros((WIDTH,), jnp.float32), 'ln3_g': jnp.ones((WIDTH,), jnp.float32), 'ln3_b': jnp.zeros((WIDTH,), jnp.float32), 'sa_wq': xav(ks[2], (WIDTH, WIDTH), g2), 'sa_bq': jnp.zeros((WIDTH,), jnp.float32), 'sa_wk': xav(ks[3], (WIDTH, WIDTH), g2), 'sa_bk': jnp.zeros((WIDTH,), jnp.float32), 'sa_wv': xav(ks[4], (WIDTH, WIDTH), g2), 'sa_bv': jnp.zeros((WIDTH,), jnp.float32), 'sa_wo': xav(ks[5], (WIDTH, WIDTH), 1.0), 'sa_bo': jnp.zeros((WIDTH,), jnp.float32), 'ca_wq': xav(ks[6], (WIDTH, WIDTH), g2), 'ca_bq': jnp.zeros((WIDTH,), jnp.float32), 'ca_wk': xav(ks[7], (WIDTH, CTX), g2), 'ca_bk': jnp.zeros((WIDTH,), jnp.float32), 'ca_wv': xav(ks[8], (WIDTH, CTX), g2), 'ca_bv': jnp.zeros((WIDTH,), jnp.float32), 'ca_wo': xav(ks[9], (WIDTH, WIDTH), 1.0), 'ca_bo': jnp.zeros((WIDTH,), jnp.float32), 'mlp_w1': 0.02 * jax.random.normal(ks[10], (4 * WIDTH, WIDTH), jnp.float32), 'mlp_b1': jnp.zeros((4 * WIDTH,), jnp.float32), 'mlp_w2': 0.02 * jax.random.normal(ks[11], (WIDTH, 4 * WIDTH), jnp.float32), 'mlp_b2': jnp.zeros((WIDTH,), jnp.float32)}
        return inp
    _L2_xattn_all = _L2_xattn_setup()
    _L2_xattn_in = {k: v for k, v in _L2_xattn_all.items() if k in ('ln1_g', 'ln1_b', 'ln2_g', 'ln2_b', 'ln3_g', 'ln3_b', 'sa_wq', 'sa_bq', 'sa_wk', 'sa_bk', 'sa_wv', 'sa_bv', 'sa_wo', 'sa_bo', 'ca_wq', 'ca_bq', 'ca_wk', 'ca_bk', 'ca_wv', 'ca_bv', 'ca_wo', 'ca_bo', 'mlp_w1', 'mlp_b1', 'mlp_w2', 'mlp_b2')}
    del _L2_xattn_all

    def _L3_xattn_setup():
        import jax, jax.numpy as jnp
        import numpy as np
        EPS_RMS = 1e-05
        EPS_L2 = 1e-12
        MAX_SEQ_LEN = 512
        D_Q, D_KV, N_HEADS = (128, 96, 16)
        HEAD_DIM = D_Q // N_HEADS

        def _rope_tables(head_dim, max_len):
            inv_freq = 1.0 / 10000.0 ** (np.arange(0, head_dim, 2, dtype=np.float32) / head_dim)
            t = np.arange(max_len, dtype=np.float32)
            freqs = np.einsum('i,j->ij', t, inv_freq)
            emb = np.concatenate([freqs, freqs], axis=-1)
            return (jnp.asarray(np.cos(emb)), jnp.asarray(np.sin(emb)))

        def _rotate(x, cos, sin):
            T = x.shape[1]
            c = cos[:T][None, :, None, :]
            s = sin[:T][None, :, None, :]
            x1, x2 = jnp.split(x, 2, axis=-1)
            return x * c + jnp.concatenate([-x2, x1], axis=-1) * s
        key = jax.random.key(seed)
        ks = jax.random.split(key, 6)
        B, T_dec, T_enc = (4, 64, 256)
        x = jax.random.normal(ks[0], (B, T_dec, D_Q), dtype=jnp.float32)
        encoder_out = jax.random.normal(ks[1], (B, T_enc, D_KV), dtype=jnp.float32)
        sq = 1.0 / np.sqrt(D_Q)
        skv = 1.0 / np.sqrt(D_KV)
        norm_w = jnp.ones((D_Q,), dtype=jnp.float32)
        wq = jax.random.normal(ks[2], (D_Q, D_Q), dtype=jnp.float32) * sq
        wkv = jax.random.normal(ks[3], (D_KV, 2 * D_Q), dtype=jnp.float32) * skv
        wout = jax.random.normal(ks[4], (D_Q, D_Q), dtype=jnp.float32) * sq
        return {'x': x, 'encoder_out': encoder_out, 'norm_w': norm_w, 'wq': wq, 'wkv': wkv, 'wout': wout}
    _L3_xattn_all = _L3_xattn_setup()
    _L3_xattn_in = {k: v for k, v in _L3_xattn_all.items() if k in ('norm_w', 'wq', 'wkv', 'wout')}
    del _L3_xattn_all
    return {'x': x, 'ctx_768': ctx_768, 'L0_xattn_wq1': _L0_xattn_in['wq1'], 'L0_xattn_wk1': _L0_xattn_in['wk1'], 'L0_xattn_wv1': _L0_xattn_in['wv1'], 'L0_xattn_wo1': _L0_xattn_in['wo1'], 'L0_xattn_bo1': _L0_xattn_in['bo1'], 'L0_xattn_wq2': _L0_xattn_in['wq2'], 'L0_xattn_wk2': _L0_xattn_in['wk2'], 'L0_xattn_wv2': _L0_xattn_in['wv2'], 'L0_xattn_wo2': _L0_xattn_in['wo2'], 'L0_xattn_bo2': _L0_xattn_in['bo2'], 'L0_xattn_w_ff1': _L0_xattn_in['w_ff1'], 'L0_xattn_b_ff1': _L0_xattn_in['b_ff1'], 'L0_xattn_w_ff2': _L0_xattn_in['w_ff2'], 'L0_xattn_b_ff2': _L0_xattn_in['b_ff2'], 'L0_xattn_ln1_g': _L0_xattn_in['ln1_g'], 'L0_xattn_ln1_b': _L0_xattn_in['ln1_b'], 'L0_xattn_ln2_g': _L0_xattn_in['ln2_g'], 'L0_xattn_ln2_b': _L0_xattn_in['ln2_b'], 'L0_xattn_ln3_g': _L0_xattn_in['ln3_g'], 'L0_xattn_ln3_b': _L0_xattn_in['ln3_b'], 'L1_xattn_W_text': _L1_xattn_in['W_text'], 'L1_xattn_b_text': _L1_xattn_in['b_text'], 'L1_xattn_W_audio': _L1_xattn_in['W_audio'], 'L1_xattn_b_audio': _L1_xattn_in['b_audio'], 'L1_xattn_W_out': _L1_xattn_in['W_out'], 'L1_xattn_b_out': _L1_xattn_in['b_out'], 'L1_xattn_g1': _L1_xattn_in['g1'], 'L1_xattn_beta1': _L1_xattn_in['beta1'], 'L1_xattn_g2': _L1_xattn_in['g2'], 'L1_xattn_beta2': _L1_xattn_in['beta2'], 'L1_xattn_g_out': _L1_xattn_in['g_out'], 'L1_xattn_beta_out': _L1_xattn_in['beta_out'], 'L2_xattn_ln1_g': _L2_xattn_in['ln1_g'], 'L2_xattn_ln1_b': _L2_xattn_in['ln1_b'], 'L2_xattn_ln2_g': _L2_xattn_in['ln2_g'], 'L2_xattn_ln2_b': _L2_xattn_in['ln2_b'], 'L2_xattn_ln3_g': _L2_xattn_in['ln3_g'], 'L2_xattn_ln3_b': _L2_xattn_in['ln3_b'], 'L2_xattn_sa_wq': _L2_xattn_in['sa_wq'], 'L2_xattn_sa_bq': _L2_xattn_in['sa_bq'], 'L2_xattn_sa_wk': _L2_xattn_in['sa_wk'], 'L2_xattn_sa_bk': _L2_xattn_in['sa_bk'], 'L2_xattn_sa_wv': _L2_xattn_in['sa_wv'], 'L2_xattn_sa_bv': _L2_xattn_in['sa_bv'], 'L2_xattn_sa_wo': _L2_xattn_in['sa_wo'], 'L2_xattn_sa_bo': _L2_xattn_in['sa_bo'], 'L2_xattn_ca_wq': _L2_xattn_in['ca_wq'], 'L2_xattn_ca_bq': _L2_xattn_in['ca_bq'], 'L2_xattn_ca_wk': _L2_xattn_in['ca_wk'], 'L2_xattn_ca_bk': _L2_xattn_in['ca_bk'], 'L2_xattn_ca_wv': _L2_xattn_in['ca_wv'], 'L2_xattn_ca_bv': _L2_xattn_in['ca_bv'], 'L2_xattn_ca_wo': _L2_xattn_in['ca_wo'], 'L2_xattn_ca_bo': _L2_xattn_in['ca_bo'], 'L2_xattn_mlp_w1': _L2_xattn_in['mlp_w1'], 'L2_xattn_mlp_b1': _L2_xattn_in['mlp_b1'], 'L2_xattn_mlp_w2': _L2_xattn_in['mlp_w2'], 'L2_xattn_mlp_b2': _L2_xattn_in['mlp_b2'], 'L3_xattn_norm_w': _L3_xattn_in['norm_w'], 'L3_xattn_wq': _L3_xattn_in['wq'], 'L3_xattn_wkv': _L3_xattn_in['wkv'], 'L3_xattn_wout': _L3_xattn_in['wout']}

def reference(x, ctx_768, L0_xattn_wq1, L0_xattn_wk1, L0_xattn_wv1, L0_xattn_wo1, L0_xattn_bo1, L0_xattn_wq2, L0_xattn_wk2, L0_xattn_wv2, L0_xattn_wo2, L0_xattn_bo2, L0_xattn_w_ff1, L0_xattn_b_ff1, L0_xattn_w_ff2, L0_xattn_b_ff2, L0_xattn_ln1_g, L0_xattn_ln1_b, L0_xattn_ln2_g, L0_xattn_ln2_b, L0_xattn_ln3_g, L0_xattn_ln3_b, L1_xattn_W_text, L1_xattn_b_text, L1_xattn_W_audio, L1_xattn_b_audio, L1_xattn_W_out, L1_xattn_b_out, L1_xattn_g1, L1_xattn_beta1, L1_xattn_g2, L1_xattn_beta2, L1_xattn_g_out, L1_xattn_beta_out, L2_xattn_ln1_g, L2_xattn_ln1_b, L2_xattn_ln2_g, L2_xattn_ln2_b, L2_xattn_ln3_g, L2_xattn_ln3_b, L2_xattn_sa_wq, L2_xattn_sa_bq, L2_xattn_sa_wk, L2_xattn_sa_bk, L2_xattn_sa_wv, L2_xattn_sa_bv, L2_xattn_sa_wo, L2_xattn_sa_bo, L2_xattn_ca_wq, L2_xattn_ca_bq, L2_xattn_ca_wk, L2_xattn_ca_bk, L2_xattn_ca_wv, L2_xattn_ca_bv, L2_xattn_ca_wo, L2_xattn_ca_bo, L2_xattn_mlp_w1, L2_xattn_mlp_b1, L2_xattn_mlp_w2, L2_xattn_mlp_b2, L3_xattn_norm_w, L3_xattn_wq, L3_xattn_wkv, L3_xattn_wout):
    import jax
    import jax.numpy as jnp

    def _L0_xattn_ref(hidden_states, context, wq1, wk1, wv1, wo1, bo1, wq2, wk2, wv2, wo2, bo2, w_ff1, b_ff1, w_ff2, b_ff2, ln1_g, ln1_b, ln2_g, ln2_b, ln3_g, ln3_b):
        import jax, jax.numpy as jnp
        import numpy as np
        DIM = 128
        HEADS = 16
        D_HEAD = 64
        INNER = HEADS * D_HEAD
        CTX_DIM = 96
        FF_INNER = 4 * DIM
        EPS = 1e-05
        SCALE = D_HEAD ** (-0.5)

        def _layer_norm(x, g, b):
            m = jnp.mean(x, axis=-1, keepdims=True)
            v = jnp.mean(jnp.square(x - m), axis=-1, keepdims=True)
            return (x - m) * jax.lax.rsqrt(v + EPS) * g + b

        def _attention(x, ctx, wq, wk, wv, wo, bo):
            B, S, _ = x.shape
            T = ctx.shape[1]
            q = (x @ wq).reshape(B, S, HEADS, D_HEAD).transpose(0, 2, 1, 3)
            k = (ctx @ wk).reshape(B, T, HEADS, D_HEAD).transpose(0, 2, 1, 3)
            v = (ctx @ wv).reshape(B, T, HEADS, D_HEAD).transpose(0, 2, 1, 3)
            attn = jnp.einsum('bhid,bhjd->bhij', q, k) * SCALE
            attn = jax.nn.softmax(attn, axis=-1)
            out = jnp.einsum('bhij,bhjd->bhid', attn, v)
            out = out.transpose(0, 2, 1, 3).reshape(B, S, INNER)
            return out @ wo + bo
        h = hidden_states
        h = h + _attention(_layer_norm(h, ln1_g, ln1_b), _layer_norm(h, ln1_g, ln1_b), wq1, wk1, wv1, wo1, bo1)
        h = h + _attention(_layer_norm(h, ln2_g, ln2_b), context, wq2, wk2, wv2, wo2, bo2)
        x = _layer_norm(h, ln3_g, ln3_b) @ w_ff1 + b_ff1
        lin, gate = jnp.split(x, 2, axis=2)
        h = h + lin * jax.nn.gelu(gate) @ w_ff2 + b_ff2
        return h

    def _L1_xattn_ref(H_l, H_a, W_text, b_text, W_audio, b_audio, W_out, b_out, g1, beta1, g2, beta2, g_out, beta_out):
        import jax, jax.numpy as jnp
        import numpy as np
        D_TEXT, D_AUDIO, D_HID = (128, 96, 128)
        EPS = 1e-05

        def layer_norm(x, gamma, beta):
            mu = jnp.mean(x, axis=-1, keepdims=True)
            var = jnp.mean(jnp.square(x - mu), axis=-1, keepdims=True)
            return (x - mu) * jax.lax.rsqrt(var + EPS) * gamma + beta
        text_p = jnp.einsum('bld,dh->blh', H_l, W_text) + b_text
        audio_p = jnp.einsum('bsd,dh->bsh', H_a, W_audio) + b_audio
        Q = layer_norm(text_p, g1, beta1)
        K = layer_norm(audio_p, g2, beta2)
        V = audio_p
        scale = 1.0 / np.sqrt(D_HID).astype(np.float32)
        scores = jnp.einsum('blh,bsh->bls', Q, K) * scale
        alpha = jax.nn.softmax(scores, axis=-1)
        H_hyper = jnp.einsum('bls,bsh->blh', alpha, V)
        H_hyper = jnp.einsum('blh,hk->blk', H_hyper, W_out) + b_out
        return layer_norm(H_hyper + H_l, g_out, beta_out)

    def _L2_xattn_ref(x, context, ln1_g, ln1_b, ln2_g, ln2_b, ln3_g, ln3_b, sa_wq, sa_bq, sa_wk, sa_bk, sa_wv, sa_bv, sa_wo, sa_bo, ca_wq, ca_bq, ca_wk, ca_bk, ca_wv, ca_bv, ca_wo, ca_bo, mlp_w1, mlp_b1, mlp_w2, mlp_b2):
        import jax, jax.numpy as jnp
        import numpy as np
        B, S, L = (2, 256, 64)
        WIDTH, HEADS, CTX = (128, 16, 96)
        HD = WIDTH // HEADS
        EPS = 1e-05

        def _layernorm(x, g, b):
            m = jnp.mean(x, axis=-1, keepdims=True)
            v = jnp.mean(jnp.square(x - m), axis=-1, keepdims=True)
            return (x - m) * jax.lax.rsqrt(v + EPS) * g + b

        def _mha(q_in, kv_in, wq, bq, wk, bk, wv, bv, wo, bo):
            b = q_in.shape[0]
            q = (q_in @ wq.T + bq).reshape(b, -1, HEADS, HD).transpose(0, 2, 1, 3)
            k = (kv_in @ wk.T + bk).reshape(b, -1, HEADS, HD).transpose(0, 2, 1, 3)
            v = (kv_in @ wv.T + bv).reshape(b, -1, HEADS, HD).transpose(0, 2, 1, 3)
            scores = jnp.einsum('bhqd,bhkd->bhqk', q, k) * HD ** (-0.5)
            p = jax.nn.softmax(scores, axis=-1)
            o = jnp.einsum('bhqk,bhkd->bhqd', p, v)
            o = o.transpose(0, 2, 1, 3).reshape(b, -1, WIDTH)
            return o @ wo.T + bo
        h = _layernorm(x, ln1_g, ln1_b)
        x = x + _mha(h, h, sa_wq, sa_bq, sa_wk, sa_bk, sa_wv, sa_bv, sa_wo, sa_bo)
        h = _layernorm(x, ln2_g, ln2_b)
        x = x + _mha(h, context, ca_wq, ca_bq, ca_wk, ca_bk, ca_wv, ca_bv, ca_wo, ca_bo)
        h = _layernorm(x, ln3_g, ln3_b)
        h = jax.nn.gelu(h @ mlp_w1.T + mlp_b1, approximate=False) @ mlp_w2.T + mlp_b2
        return x + h

    def _L3_xattn_ref(x, encoder_out, norm_w, wq, wkv, wout):
        import jax, jax.numpy as jnp
        import numpy as np
        EPS_RMS = 1e-05
        EPS_L2 = 1e-12
        MAX_SEQ_LEN = 512
        D_Q, D_KV, N_HEADS = (128, 96, 16)
        HEAD_DIM = D_Q // N_HEADS

        def _rope_tables(head_dim, max_len):
            inv_freq = 1.0 / 10000.0 ** (np.arange(0, head_dim, 2, dtype=np.float32) / head_dim)
            t = np.arange(max_len, dtype=np.float32)
            freqs = np.einsum('i,j->ij', t, inv_freq)
            emb = np.concatenate([freqs, freqs], axis=-1)
            return (jnp.asarray(np.cos(emb)), jnp.asarray(np.sin(emb)))

        def _rotate(x, cos, sin):
            T = x.shape[1]
            c = cos[:T][None, :, None, :]
            s = sin[:T][None, :, None, :]
            x1, x2 = jnp.split(x, 2, axis=-1)
            return x * c + jnp.concatenate([-x2, x1], axis=-1) * s
        B, T_dec, _ = x.shape
        T_enc = encoder_out.shape[1]
        cos, sin = _rope_tables(HEAD_DIM, MAX_SEQ_LEN)
        residual = x
        xn = x * jax.lax.rsqrt(jnp.mean(x * x, axis=-1, keepdims=True) + EPS_RMS) * norm_w
        q = (xn @ wq).reshape(B, T_dec, N_HEADS, HEAD_DIM)
        kv = (encoder_out @ wkv).reshape(B, T_enc, 2, N_HEADS, HEAD_DIM)
        k, v = (kv[:, :, 0], kv[:, :, 1])
        q = _rotate(q, cos, sin)
        k = _rotate(k, cos, sin)
        q = q / jnp.maximum(jnp.linalg.norm(q, axis=-1, keepdims=True), EPS_L2)
        k = k / jnp.maximum(jnp.linalg.norm(k, axis=-1, keepdims=True), EPS_L2)
        scale = jnp.sqrt(jnp.float32(HEAD_DIM))
        logits = jnp.einsum('bqhd,bkhd->bhqk', q, k) * scale
        attn = jax.nn.softmax(logits, axis=-1)
        out = jnp.einsum('bhqk,bkhd->bqhd', attn, v).reshape(B, T_dec, D_Q)
        return residual + out @ wout
    x = _L0_xattn_ref(x, ctx_768, L0_xattn_wq1, L0_xattn_wk1, L0_xattn_wv1, L0_xattn_wo1, L0_xattn_bo1, L0_xattn_wq2, L0_xattn_wk2, L0_xattn_wv2, L0_xattn_wo2, L0_xattn_bo2, L0_xattn_w_ff1, L0_xattn_b_ff1, L0_xattn_w_ff2, L0_xattn_b_ff2, L0_xattn_ln1_g, L0_xattn_ln1_b, L0_xattn_ln2_g, L0_xattn_ln2_b, L0_xattn_ln3_g, L0_xattn_ln3_b)
    x = _L1_xattn_ref(x, ctx_768, L1_xattn_W_text, L1_xattn_b_text, L1_xattn_W_audio, L1_xattn_b_audio, L1_xattn_W_out, L1_xattn_b_out, L1_xattn_g1, L1_xattn_beta1, L1_xattn_g2, L1_xattn_beta2, L1_xattn_g_out, L1_xattn_beta_out)
    x = _L2_xattn_ref(x, ctx_768, L2_xattn_ln1_g, L2_xattn_ln1_b, L2_xattn_ln2_g, L2_xattn_ln2_b, L2_xattn_ln3_g, L2_xattn_ln3_b, L2_xattn_sa_wq, L2_xattn_sa_bq, L2_xattn_sa_wk, L2_xattn_sa_bk, L2_xattn_sa_wv, L2_xattn_sa_bv, L2_xattn_sa_wo, L2_xattn_sa_bo, L2_xattn_ca_wq, L2_xattn_ca_bq, L2_xattn_ca_wk, L2_xattn_ca_bk, L2_xattn_ca_wv, L2_xattn_ca_bv, L2_xattn_ca_wo, L2_xattn_ca_bo, L2_xattn_mlp_w1, L2_xattn_mlp_b1, L2_xattn_mlp_w2, L2_xattn_mlp_b2)
    x = _L3_xattn_ref(x, ctx_768, L3_xattn_norm_w, L3_xattn_wq, L3_xattn_wkv, L3_xattn_wout)
    return x

_drawn_inputs = setup_inputs


def setup_inputs(seed=0):
    import zlib

    import numpy as np

    out = dict(_drawn_inputs(seed))
    spreads = {'L0_xattn_bo1': (0.0, 0.314),
     'L0_xattn_bo2': (0.0, 0.272),
     'L0_xattn_b_ff1': (0.0, 0.8),
     'L0_xattn_b_ff2': (0.0, 0.539),
     'L0_xattn_ln1_g': (1.0, 0.6),
     'L0_xattn_ln1_b': (0.0, 0.681),
     'L0_xattn_ln2_g': (1.0, 0.6),
     'L0_xattn_ln2_b': (0.0, 2.0),
     'L0_xattn_ln3_g': (1.0, 0.6),
     'L0_xattn_ln3_b': (0.0, 0.8),
     'L1_xattn_b_text': (0.0, 2.0),
     'L1_xattn_b_audio': (0.0, 0.426),
     'L1_xattn_b_out': (0.0, 0.472),
     'L1_xattn_g1': (1.0, 0.6),
     'L1_xattn_beta1': (0.0, 1.807),
     'L1_xattn_g2': (1.0, 0.6),
     'L1_xattn_beta2': (0.0, 2.0),
     'L1_xattn_g_out': (1.0, 0.2),
     'L1_xattn_beta_out': (0.0, 0.1),
     'L2_xattn_ln1_g': (1.0, 0.2),
     'L2_xattn_ln1_b': (0.0, 0.1),
     'L2_xattn_ln2_g': (1.0, 0.6),
     'L2_xattn_ln2_b': (0.0, 0.8),
     'L2_xattn_ln3_g': (1.0, 0.6),
     'L2_xattn_ln3_b': (0.0, 0.8),
     'L2_xattn_sa_bq': (0.0, 0.8),
     'L2_xattn_sa_bk': (0.0, 2.0),
     'L2_xattn_sa_bv': (0.0, 0.1),
     'L2_xattn_sa_bo': (0.0, 0.1),
     'L2_xattn_ca_bq': (0.0, 0.8),
     'L2_xattn_ca_bk': (0.0, 2.0),
     'L2_xattn_ca_bv': (0.0, 0.1),
     'L2_xattn_ca_bo': (0.0, 0.1),
     'L2_xattn_mlp_b1': (0.0, 0.41),
     'L2_xattn_mlp_b2': (0.0, 0.1),
     'L3_xattn_norm_w': (1.0, 0.6)}
    factors = {'L0_xattn_wq1': 8.0,
     'L0_xattn_wk1': 8.0,
     'L0_xattn_wv1': 3.659,
     'L0_xattn_wo1': 3.9,
     'L0_xattn_wq2': 8.0,
     'L0_xattn_wk2': 8.0,
     'L0_xattn_w_ff1': 4.812,
     'L0_xattn_w_ff2': 4.827}
    for name, (base, spread) in spreads.items():
        noise = np.random.default_rng([zlib.crc32(name.encode()), seed]).standard_normal(out[name].shape)
        drawn = base * np.exp(spread * noise) if base else spread * noise
        out[name] = jnp.asarray(drawn.astype(out[name].dtype))
    for name, factor in factors.items():
        out[name] = (out[name] * factor).astype(out[name].dtype)
    return out
```

```python
from contextlib import ExitStack

import numpy as np

import concourse.bass as bass
from concourse import mybir

F32 = mybir.dt.float32
F32R = mybir.dt.float32r
ACT = mybir.ActivationFunctionType
ALU = mybir.AluOpType
AX = mybir.AxisListType

B, S, D = 8, 256, 128
T, C = 512, 96
H = 16
E0 = 64
E2 = 8
INNER = H * E0
FF = 4 * D
P = 128
QB = S // P
TB = T // P
PAIRS = H // 2
QUADS = H // 4
EPS = 1e-5
EPS_L2 = 1e-12
ENGINES = 5


class Semaphores:

    def __init__(self, nc, ctx):
        self.nc, self.ctx, self.by_name = nc, ctx, {}

    def __getitem__(self, name):
        if name not in self.by_name:
            self.by_name[name] = self.ctx.enter_context(self.nc.semaphore(name))
        return self.by_name[name]

    def ids(self):
        ids = sorted(s.num for s in self.by_name.values())
        assert ids == list(range(ids[0], ids[0] + len(ids)))
        return range(ids[0], ids[0] + len(ids))


class Attention:

    def __init__(self, name, heads, group, keys, t_rows=0):
        self.name, self.heads, self.group, self.keys, self.t_rows = name, heads, group, keys, t_rows
        self.kb = keys // P
        self.fills = keys // (2 * P)
        self.groups = heads // group
        self.slots = 2 * group
        self.rows = P // group
        self.before = {}

    def counts(self):
        t = self.heads if self.t_rows else 0
        fills = self.heads * self.fills
        return {"t": t, "t_hi": t, "t_lo": t, "scores": self.heads, "max": self.heads, "exp": QB * self.heads,
                "turned": fills, "turned_copied0": (fills + 1) // 2, "turned_copied1": fills // 2,
                "rinv": self.groups, "heads": self.groups, "scale": self.groups, "out_scaled": self.groups}

    def at(self, what, n):
        return self.before[what] + n


SELF0 = Attention("self0", H, 2, S, D)
CROSS0 = Attention("cross0", H, 2, T, C)
CROSS1 = Attention("cross1", 1, 1, T)
SELF2 = Attention("self2", H, 4, S)
CROSS2 = Attention("cross2", H, 4, T)
PHASES = (SELF0, CROSS0, CROSS1, SELF2, CROSS2)
for _k, _phase in enumerate(PHASES):
    _phase.before = {what: sum(q.counts()[what] for q in PHASES[:_k]) for what in _phase.counts()}
NORMS = ("ln1", "ln2", "ln3", "audio", "text", "out1", "m1", "m2", "m3", "rms")
TURNED = tuple(n for n in NORMS if n != "out1")


def program(nc, A, y_out):
    ctx = ExitStack()
    with ctx:
        def sb(name, shape, dt=F32):
            return ctx.enter_context(nc.sbuf_tensor(name, shape, dt))

        def ps(name, cols):
            return ctx.enter_context(nc.psum_tensor(name, [P, cols], F32))

        ident = sb("ident", [P, P])
        sum_rows = sb("sum_rows", [P, P])
        rope_cos = sb("rope_cos", [P, TB, E2])
        rope_sin = sb("rope_sin", [P, TB, E2])
        minus_half = sb("minus_half", [P, TB])
        m_hi = [sb("m1_hi", [P, H, D], F32R), sb("m2_hi", [P, H, C], F32R)]
        m_lo = [sb("m1_lo", [P, H, D], F32R), sb("m2_lo", [P, H, C], F32R)]
        split = {}
        for name, rows, cols in (("wv1", D, INNER), ("wv2", C, INNER), ("wff1", D, 2 * FF), ("wtext", D, D),
                                 ("waudio", C, D), ("wsa", D, 3 * D), ("wcaq", D, D), ("wcakv", C, 2 * D),
                                 ("wl3q", D, D), ("wl3kv", C, 2 * D), ("wmlp1", D, FF)):
            split[name] = (sb(name + "_hi", [rows, cols], F32R), sb(name + "_lo", [rows, cols], F32R))
        wo = [sb("wo1", [P, PAIRS, D]), sb("wo2", [P, PAIRS, D])]
        wff2 = sb("wff2", [P, FF // P, D])
        wout1 = sb("wout1", [P, D])
        wmlp2 = sb("wmlp2", [P, FF // P, D])
        wo_pad = [sb("wo_sa", [P, QUADS, D]), sb("wo_ca", [P, QUADS, D]), sb("wo_l3", [P, QUADS, D])]
        rows_of = {}
        for name, cols in (("bo1", D), ("bo2", D), ("bff2", D), ("btext", D), ("baudio", D), ("bout", D),
                           ("gout", D), ("betaout", D), ("bsa", 3 * D), ("bcaq", D), ("bcakv", 2 * D),
                           ("bosa", D), ("boca", D), ("bmlp2", D)):
            rows_of[name] = sb("row_" + name, [P, cols])
        cols_of = {}
        for name, n in (("ln1g", 1), ("ln1b", 1), ("ln2g", 1), ("ln2b", 1), ("ln3g", 1), ("ln3b", 1),
                        ("bff1", 2 * FF // P), ("g1", 1), ("beta1", 1), ("g2", 1), ("beta2", 1),
                        ("m1g", 1), ("m1b", 1), ("m2g", 1), ("m2b", 1), ("m3g", 1), ("m3b", 1),
                        ("bmlp1", FF // P), ("normw", 1)):
            cols_of[name] = sb("col_" + name, [P, n])

        x = sb("x", [P, QB, D])
        ctx_nat = sb("ctx_nat", [P, TB, C])
        ctx_hi, ctx_lo = sb("ctx_hi", [C, T], F32R), sb("ctx_lo", [C, T], F32R)
        stats = sb("stats", [P, TB, 6])
        moments = sb("moments", [P, TB, 2])
        var_eps = sb("var_eps", [P, TB])
        rstd = sb("rstd", [P, TB])
        xhat = sb("xhat", [P, TB, D])
        xz = sb("xz", [P, T])
        x_hi, x_lo = sb("x_hi", [P, S], F32R), sb("x_lo", [P, S], F32R)
        t_hi, t_lo = sb("t_hi", [P, 2, S], F32R), sb("t_lo", [P, 2, S], F32R)
        v = sb("v", [P, TB * INNER])
        v0 = v[:, :].rearrange("p (b n) -> p b n", b=TB)
        v1 = v[:, 0:TB * D].rearrange("p (b n) -> p b n", b=TB)
        k_stack = v[:, 0:TB * H * 32].rearrange("p (b h c) -> p b h c", b=TB, h=H)
        q_stack = v[:, 2048:2048 + QB * H * 32].rearrange("p (b h c) -> p b h c", b=QB, h=H)
        rope_tmp = v[:, 3072:3072 + TB * D].rearrange("p (b h c) -> p b h c", b=TB, h=H)
        rope_prod = v[:, 3584:3584 + TB * D].rearrange("p (b h c) -> p b h c", b=TB, h=H)
        probs = sb("probs", [P, 2, QB, T])
        probs_t = sb("probs_t", [P, 8, TB, S])
        sums = sb("sums", [P, QB, H])
        rinv = sb("rinv", [P, QB, P])
        inv = sb("inv", [P, QB, 4])
        nmax = sb("nmax", [P, H, QB])
        scale_t = sb("scale_t", [P, 2, S])
        out_t = sb("out_t", [P, PAIRS, S])
        gate = out_t[:, 4:6, :]
        prod = out_t[:, 0:4, :]
        q_mask = sb("q_mask", [P, QUADS, 4, S], F32R)
        k_t = sb("k_t", [P, QUADS, T], F32R)
        k1_hi, k1_lo = k_t[:, 0, :], k_t[:, 1, :]
        v_pad = sb("v_pad", [P, TB, H, 32])
        nat_q = sb("nat_q", [P, QB, D])
        nat_kv = sb("nat_kv", [P, TB, 2 * D])
        ss = sb("ss", [P, TB, H])
        norm = sb("norm", [P, TB, H])
        dummy = sb("table_probe", [P, 1])

        raw_at, raw = [0], {}
        raw_tile = probs_t[:, :, :, :].rearrange("p a b c -> p (a b c)")

        def raw_view(name, rows, cols):
            raw[name] = raw_tile[0:rows, raw_at[0]:raw_at[0] + cols]
            raw_at[0] += cols

        wqt = [v[:, 0:PAIRS * D].rearrange("p (j n) -> p j n", j=PAIRS),
               v[:, 1024:1024 + PAIRS * D].rearrange("p (j n) -> p j n", j=PAIRS)]
        wkt = [v[:, 2048:2048 + PAIRS * D].rearrange("p (j n) -> p j n", j=PAIRS),
               v[:, 3072:3072 + PAIRS * C].rearrange("p (j n) -> p j n", j=PAIRS)]
        for name, (hi, _) in split.items():
            raw_view(name, hi.shape[0], hi.shape[1])

        S0, S1 = ps("scores0", 1024), ps("scores1", 1024)
        PT = [ps("pt0", 512), ps("pt1", 512)]
        O = ps("heads_out", 512)
        X = ps("small", 512)
        SC = [S0, S1]

        sem = Semaphores(nc, ctx)
        batch_open = ctx.enter_context(nc.semaphore("batch_open"))

        def f32r(ap):
            return ap.bitcast(F32R)

        def f32(ap):
            return ap.bitcast(F32)

        def three_products(out, a, b):
            (a_hi, a_lo), (b_hi, b_lo) = a, b
            nc.tensor.matmul(out, a_hi, b_hi, start=True, stop=False)
            nc.tensor.matmul(out, a_lo, b_hi, start=False, stop=False)
            return nc.tensor.matmul(out, a_hi, b_lo, start=False, stop=True)

        SINGLE = [("ident", ident[:, :]), ("sum_rows", sum_rows[:, :]), ("rope_cos", rope_cos[:, :, :]),
                  ("rope_sin", rope_sin[:, :, :])]
        RAW = ([("wqt0", wqt[0]), ("wkt0", wkt[0]), ("wqt1", wqt[1]), ("wkt1", wkt[1])]
               + [(n, raw[n]) for n in ("wv1", "wv2", "wff1", "wtext", "waudio", "wcaq", "wl3q", "wl3kv", "wmlp1")]
               + [(n, raw["wsa"][:, k * D:(k + 1) * D]) for k, n in enumerate(("sawq", "sawk", "sawv"))]
               + [(n, raw["wcakv"][:, k * D:(k + 1) * D]) for k, n in enumerate(("cawk", "cawv"))])
        KEPT = ([("wo1", wo[0][:, :, :]), ("wo2", wo[1][:, :, :]), ("wff2", wff2[:, :, :]), ("wout1", wout1[:, :]),
                 ("wmlp2", wmlp2[:, :, :])]
                + [(n, t[:, :]) for n, t in cols_of.items()]
                + [(n, rows_of[n][:, :]) for n in rows_of if n not in ("bsa", "bcakv")]
                + [(n, rows_of["bsa"][:, k * D:(k + 1) * D]) for k, n in enumerate(("sabq", "sabk", "sabv"))]
                + [(n, rows_of["bcakv"][:, k * D:(k + 1) * D]) for k, n in enumerate(("cabk", "cabv"))])
        n_raw, n_kept = len(RAW) + len(SINGLE), len(KEPT)

        def setup_end(eng):
            eng.drain().then_inc(sem["setup_done"], 1)
            eng.wait_ge(sem["setup_done"], ENGINES)

        def batch_end(eng, b):
            eng.drain().then_inc(sem["batch_done"], 1)
            eng.wait_ge(batch_open, b + 1)

        block = ctx.enter_context(nc.Block())

        @block.tensor
        def _(pe):
            pe.wait_ge(sem["raw_loaded"], 16 * n_raw)
            for fill in range(4):
                layer, half = fill // 2, fill % 2
                width = (D, C)[layer]
                if fill >= 2:
                    pe.wait_ge(sem["m_split"], 2 * (fill - 1))
                for jj in range(4):
                    for i in range(2):
                        rows = slice(64 * i, 64 * i + 64)
                        last = nc.tensor.matmul(SC[fill % 2][:, 512 * i + jj * width:512 * i + (jj + 1) * width],
                                                wqt[layer][rows, 4 * half + jj, :],
                                                wkt[layer][rows, 4 * half + jj, 0:width], start=True, stop=True)
                last.then_inc(sem["m_made"], 1)
            setup_end(pe)

            def transpose(out, in_):
                return nc.tensor.transpose(out, in_, ident[:, :])

            def norm_transposes(n, ready):
                pe.wait_ge(sem[ready], 2)
                for qb in range(QB):
                    last = transpose(X[:, qb * P:(qb + 1) * P], xhat[:, qb, :])
                last.then_inc(sem["norm_turned"], 1)

            def x_blocks(qb):
                s = slice(qb * P, (qb + 1) * P)
                return x_hi[:, s], x_lo[:, s]

            def c_blocks(kb):
                s = slice(kb * P, (kb + 1) * P)
                return ctx_hi[:, s], ctx_lo[:, s]

            def halves(name, s=slice(None)):
                hi, lo = split[name]
                return hi[:, s], lo[:, s]

            def value_fill(name, fill, left, w):
                kb, half = fill // 2, fill % 2
                bank = SC[(fill // 2) % 2][:, 512 * half:512 * half + 512]
                three_products(bank, left(kb), halves(w, slice(512 * half, 512 * half + 512))).then_inc(sem[f"{name}_v"], 1)

            def queries_times_m(ph, layer, h):
                if h >= 1:
                    pe.wait_ge(sem["attention_t_lo"], ph.at("t_lo", h))
                three_products(X[0:ph.t_rows, 0:S], (m_hi[layer][:, h, :], m_lo[layer][:, h, :]),
                               (x_hi[:, :], x_lo[:, :])).then_inc(sem["attention_t"], 1)

            def scores(ph, layer, h):
                if h >= 2:
                    pe.wait_ge(sem["attention_exp"], ph.at("exp", QB * (h - 1)))
                if layer < 2:
                    pe.wait_ge(sem["attention_t_hi"], ph.at("t_hi", h + 1))
                    pe.wait_ge(sem["attention_t_lo"], ph.at("t_lo", h + 1))
                for qb in range(QB):
                    out = SC[h % 2][:, qb * 512:qb * 512 + ph.keys]
                    q = slice(qb * P, (qb + 1) * P)
                    if layer < 2:
                        left = (t_hi[0:ph.t_rows, h % 2, q], t_lo[0:ph.t_rows, h % 2, q])
                        right = (x_hi[:, :], x_lo[:, :]) if ph is SELF0 else (ctx_hi[:, :], ctx_lo[:, :])
                        last = three_products(out, left, right)
                    elif layer == 2:
                        last = three_products(out, (x_hi[:, q], x_lo[:, q]), (k1_hi, k1_lo))
                    else:
                        last = nc.tensor.matmul(out, q_mask[:, h // 4, h % 4, q], k_t[:, h // 4, 0:ph.keys],
                                                start=True, stop=True)
                last.then_inc(sem["attention_scores"], 1)

            def turn_probs(ph, h):
                pe.wait_ge(sem["attention_exp"], ph.at("exp", QB * (h + 1)))
                for j in range(ph.fills):
                    n = h * ph.fills + j
                    if n >= 2:
                        pe.wait_ge(sem[f"attention_turned_copied{n % 2}"], ph.at(f"turned_copied{n % 2}", n // 2))
                    for k in range(2):
                        for qb in range(QB):
                            kb = 2 * j + k
                            last = transpose(PT[n % 2][:, k * S + qb * P:k * S + (qb + 1) * P],
                                             probs[:, h % 2, qb, kb * P:(kb + 1) * P])
                    last.then_inc(sem["attention_turned"], 1)

            def head_outputs(ph, g, values):
                n = (g + 1) * ph.group * ph.fills
                pe.wait_ge(sem["attention_turned_copied0"], ph.at("turned_copied0", (n + 1) // 2))
                if n >= 2:
                    pe.wait_ge(sem["attention_turned_copied1"], ph.at("turned_copied1", n // 2))
                if g >= 1:
                    pe.wait_ge(sem["attention_out_scaled"], ph.at("out_scaled", g))
                w = ph.rows
                for kb in range(ph.kb):
                    for i in range(ph.group):
                        h = g * ph.group + i
                        nc.tensor.matmul(O[w * i:w * i + w, 0:S], values(kb, h), probs_t[:, h % ph.slots, kb, :],
                                         start=(kb == 0), stop=(kb == ph.kb - 1))
                pe.wait_ge(sem["attention_rinv"], ph.at("rinv", g + 1))
                for qb in range(QB):
                    last = transpose(O[:, S + qb * P:S + (qb + 1) * P], rinv[:, qb, :])
                last.then_inc(sem["attention_heads"], 1)

            def attention(ph, layer, values):
                if layer < 2:
                    queries_times_m(ph, layer, 0)
                    queries_times_m(ph, layer, 1)
                scores(ph, layer, 0)
                if layer < 2:
                    queries_times_m(ph, layer, 2)
                if ph.heads > 1:
                    scores(ph, layer, 1)
                for h in range(ph.heads):
                    if h + 2 < ph.heads:
                        scores(ph, layer, h + 2)
                    turn_probs(ph, h)
                    if layer < 2 and h + 3 < ph.heads:
                        queries_times_m(ph, layer, h + 3)
                    if h % ph.group == 0 and h >= ph.group:
                        head_outputs(ph, h // ph.group - 1, values)
                head_outputs(ph, ph.groups - 1, values)

            def project_out(ready, n_ready, n, blocks, left, weights):
                pe.wait_ge(sem[ready], n_ready)
                for qb in range(QB):
                    for j in range(blocks):
                        last = nc.tensor.matmul(X[:, qb * P:(qb + 1) * P], left[:, j, qb * P:(qb + 1) * P],
                                                weights(j), start=(j == 0), stop=(j == blocks - 1))
                last.then_inc(sem[f"{n}_projected"], 1)

            def turn_stacks(n, kb_count):
                pe.wait_ge(sem[f"{n}_q_stacked"], 1)
                pe.wait_ge(sem[f"{n}_q_stacked_act"], 1)
                for g in range(QUADS):
                    for qb in range(QB):
                        last = transpose(S0[:, g * S + qb * P:g * S + (qb + 1) * P],
                                         q_stack[:, qb, 4 * g:4 * g + 4, :])
                last.then_inc(sem[f"{n}_q_turned"], 1)
                pe.wait_ge(sem[f"{n}_k_stacked"], 1)
                pe.wait_ge(sem[f"{n}_k_stacked_act"], 1)
                for r in range(kb_count // 2):
                    if r == 1:
                        pe.wait_ge(sem[f"{n}_k_copied"], 1)
                    for g in range(QUADS):
                        for k in range(2):
                            last = transpose(S1[:, g * S + k * P:g * S + (k + 1) * P],
                                             k_stack[:, 2 * r + k, 4 * g:4 * g + 4, :])
                    last.then_inc(sem[f"{n}_k_turned"], 1)
                pe.wait_ge(sem[f"{n}_q_masked_act"], 2)
                pe.wait_ge(sem[f"{n}_q_masked_dve"], 2)
                pe.wait_ge(sem[f"{n}_k_copied"], kb_count // 2)

            with pe.Fori(0, B) as b:
                pe.wait_ge(sem["ctx_loaded"], 16)
                for kb in range(TB):
                    last = transpose(S0[0:C, kb * P:(kb + 1) * P], ctx_nat[:, kb, :])
                last.then_inc(sem["ctx_turned"], 1)

                norm_transposes("ln1", "ln1_hat")
                pe.wait_ge(sem["norm_split"], TURNED.index("ln1") + 1)
                pe.wait_ge(sem["ctx_lo"], 1)
                for fill in range(4):
                    value_fill("self0", fill, x_blocks, "wv1")
                pe.wait_ge(sem["self0_v_act"], 2)
                pe.wait_ge(sem["self0_v_dve"], 2)
                attention(SELF0, 0, lambda kb, h: v0[:, kb, h * E0:(h + 1) * E0])
                project_out("attention_out_scaled", SELF0.at("out_scaled", PAIRS), "self0", PAIRS, out_t, lambda j: wo[0][:, j, :])

                for fill in range(4):
                    value_fill("cross0", fill, c_blocks, "wv2")
                norm_transposes("ln2", "ln2_hat")
                for fill in range(4, 8):
                    pe.wait_ge(sem["cross0_v_act"], (fill - 4) // 2 + 1)
                    pe.wait_ge(sem["cross0_v_dve"], (fill - 4) // 2 + 1)
                    value_fill("cross0", fill, c_blocks, "wv2")
                pe.wait_ge(sem["norm_split"], TURNED.index("ln2") + 1)
                pe.wait_ge(sem["cross0_v_act"], 4)
                pe.wait_ge(sem["cross0_v_dve"], 4)
                attention(CROSS0, 1, lambda kb, h: v0[:, kb, h * E0:(h + 1) * E0])
                project_out("attention_out_scaled", CROSS0.at("out_scaled", PAIRS), "cross0", PAIRS, out_t, lambda j: wo[1][:, j, :])

                norm_transposes("ln3", "ln3_hat")
                pe.wait_ge(sem["norm_split"], TURNED.index("ln3") + 1)
                for j in range(4):
                    if j >= 2:
                        pe.wait_ge(sem["gelu"], j - 1)
                    three_products(S0[:, 512 * (j % 2):512 * (j % 2) + S],
                                   halves("wff1", slice(FF + j * P, FF + (j + 1) * P)),
                                   (x_hi[:, :], x_lo[:, :])).then_inc(sem["gate"], 1)
                    if j >= 2:
                        pe.wait_ge(sem["gated"], j - 1)
                    three_products(S1[:, 512 * (j % 2):512 * (j % 2) + S],
                                   halves("wff1", slice(j * P, (j + 1) * P)),
                                   (x_hi[:, :], x_lo[:, :])).then_inc(sem["linear"], 1)
                project_out("gated", 4, "ff", 4, prod, lambda j: wff2[:, j, :])

                for kb in range(TB):
                    last = three_products(S0[:, kb * D:(kb + 1) * D], c_blocks(kb), halves("waudio"))
                last.then_inc(sem["audio"], 1)
                pe.wait_ge(sem["audio_hat"], TB)
                for kb in range(TB):
                    last = transpose(S1[:, kb * P:(kb + 1) * P], xhat[:, kb, :])
                last.then_inc(sem["norm_turned"], 1)
                pe.wait_ge(sem["x_ff"], 1)
                for qb in range(QB):
                    last = transpose(X[:, qb * P:(qb + 1) * P], x[:, qb, :])
                last.then_inc(sem["x1_turned"], 1)
                pe.wait_ge(sem["x1_split"], 1)
                for qb in range(QB):
                    last = three_products(O[:, qb * P:(qb + 1) * P], x_blocks(qb), halves("wtext"))
                last.then_inc(sem["text"], 1)
                norm_transposes("text", "text_hat")
                pe.wait_ge(sem["norm_split"], TURNED.index("text") + 1)
                pe.wait_ge(sem["norm_split"], TURNED.index("audio") + 1)
                attention(CROSS1, 2, lambda kb, h: v1[:, kb, :])
                project_out("attention_out_scaled", CROSS1.at("out_scaled", 1), "cross1", 1, out_t, lambda j: wout1[:, :])

                norm_transposes("m1", "m1_hat")
                pe.wait_ge(sem["norm_split"], TURNED.index("m1") + 1)
                for qb in range(QB):
                    last = three_products(S0[:, 512 * qb:512 * qb + 3 * D], x_blocks(qb), halves("wsa"))
                last.then_inc(sem["self2_qkv"], 1)
                turn_stacks("self2", QB)
                attention(SELF2, 3, lambda kb, h: v_pad[:, kb, h, :])
                project_out("attention_out_scaled", SELF2.at("out_scaled", QUADS), "self2", QUADS, out_t, lambda j: wo_pad[0][:, j, :])

                for kb in range(TB):
                    last = three_products(S1[:, kb * 2 * D:(kb + 1) * 2 * D], c_blocks(kb), halves("wcakv"))
                last.then_inc(sem["cross2_kv"], 1)
                norm_transposes("m2", "m2_hat")
                pe.wait_ge(sem["norm_split"], TURNED.index("m2") + 1)
                for qb in range(QB):
                    last = three_products(S0[:, 512 * qb:512 * qb + D], x_blocks(qb), halves("wcaq"))
                last.then_inc(sem["cross2_q"], 1)
                turn_stacks("cross2", TB)
                attention(CROSS2, 3, lambda kb, h: v_pad[:, kb, h, :])
                project_out("attention_out_scaled", CROSS2.at("out_scaled", QUADS), "cross2", QUADS, out_t, lambda j: wo_pad[1][:, j, :])

                norm_transposes("m3", "m3_hat")
                pe.wait_ge(sem["norm_split"], TURNED.index("m3") + 1)
                for j in range(4):
                    three_products(SC[j // 2][:, 512 * (j % 2):512 * (j % 2) + S],
                                   halves("wmlp1", slice(j * P, (j + 1) * P)), (x_hi[:, :], x_lo[:, :])).then_inc(sem["up"], 1)
                project_out("gelu2", 4, "mlp", 4, prod, lambda j: wmlp2[:, j, :])

                for kb in range(TB):
                    last = three_products(S1[:, kb * 2 * D:(kb + 1) * 2 * D], c_blocks(kb), halves("wl3kv"))
                last.then_inc(sem["l3_kv"], 1)
                norm_transposes("rms", "rms_hat")
                pe.wait_ge(sem["norm_split"], TURNED.index("rms") + 1)
                for qb in range(QB):
                    last = three_products(S0[:, 512 * qb:512 * qb + D], x_blocks(qb), halves("wl3q"))
                last.then_inc(sem["l3_q"], 1)
                turn_stacks("l3", TB)

                def key_major_scores(h):
                    if h >= 2:
                        pe.wait_ge(sem["l3_exp"], h - 1)
                    for kb in range(TB):
                        last = nc.tensor.matmul(SC[h % 2][:, kb * S:(kb + 1) * S],
                                                k_t[:, h // 4, kb * P:(kb + 1) * P],
                                                q_mask[:, h // 4, h % 4, :], start=True, stop=True)
                    last.then_inc(sem["l3_scores"], 1)

                def quad_outputs(g):
                    pe.wait_ge(sem["l3_exp"], 4 * g + 4)
                    if g >= 1:
                        pe.wait_ge(sem["l3_scaled"], g)
                    for kb in range(TB):
                        for i in range(4):
                            h = 4 * g + i
                            last = nc.tensor.matmul(O[32 * i:32 * i + 32, 0:S], v_pad[:, kb, h, :],
                                                    probs_t[:, h % 8, kb, :], start=(kb == 0), stop=(kb == TB - 1))
                    last.then_inc(sem["l3_heads"], 1)

                def quad_sums(g):
                    pe.wait_ge(sem["l3_heads_copied"], g + 1)
                    nc.tensor.matmul(O[:, S:2 * S], sum_rows[:, :], scale_t[:, g % 2, :],
                                     start=True, stop=True).then_inc(sem["l3_sums"], 1)

                key_major_scores(0)
                for h in range(H):
                    if h + 1 < H:
                        key_major_scores(h + 1)
                    if h % 4 == 0 and h >= 4:
                        quad_outputs(h // 4 - 1)
                    if h % 4 == 1 and h >= 4:
                        quad_sums(h // 4 - 1)
                quad_outputs(QUADS - 1)
                quad_sums(QUADS - 1)
                project_out("l3_scaled", QUADS, "l3", QUADS, out_t, lambda j: wo_pad[2][:, j, :])
                batch_end(pe, b)

        @block.scalar
        def _(act):
            def copy(out, in_, scale=1.0):
                return nc.scalar.activation(out, in_, ACT.Copy, scale=scale)

            for name, dst in KEPT:
                act.dma_start(dst, A[name]).then_inc(sem["kept_loaded"], 16)
            act.wait_ge(sem["raw_loaded"], 16 * n_raw)
            act.wait_ge(sem["raw_scaled"], 1)
            for name in split:
                copy(split[name][0][:, :], raw[name]).then_inc(sem["w_hi"], 1)
            for fill in range(4):
                layer, half = fill // 2, fill % 2
                width = (D, C)[layer]
                act.wait_ge(sem["m_made"], fill + 1)
                for i in range(2):
                    out = m_hi[layer][:, :, :].rearrange("p (j i) n -> p j i n", i=2)[:, 4 * half:4 * half + 4, i, :]
                    src = SC[fill % 2][:, 512 * i:512 * i + 4 * width].rearrange("p (j n) -> p j n", j=4)
                    copy(out, src, scale=E0 ** -0.5).then_inc(sem["m_hi"], 1)
            setup_end(act)

            def affine(n, g, beta, cols=S, bank=None):
                act.wait_ge(sem["norm_turned"], TURNED.index(n) + 1)
                nc.scalar.activation(xz[:, 0:cols], (X if bank is None else bank)[:, 0:cols], ACT.Identity,
                                     bias=cols_of[beta][:, 0:1] if beta else 0.0,
                                     scale=cols_of[g][:, 0:1]).then_inc(sem["norm_affine"], 1)

            def value_copy(name, fill):
                act.wait_ge(sem[f"{name}_v"], fill + 1)
                kb, half = fill // 2, fill % 2
                copy(v0[:, kb, 512 * half:512 * half + 512],
                     SC[(fill // 2) % 2][:, 512 * half:512 * half + 512]).then_inc(sem[f"{name}_v_act"], 1)

            def t_high(ph, h):
                act.wait_ge(sem["attention_t"], ph.at("t", h + 1))
                if h >= 2:
                    act.wait_ge(sem["attention_scores"], ph.at("scores", h - 1))
                copy(t_hi[0:ph.t_rows, h % 2, :], X[0:ph.t_rows, 0:S]).then_inc(sem["attention_t_hi"], 1)

            def exps(ph, h):
                act.wait_ge(sem["attention_max"], ph.at("max", h + 1))
                if h >= 2:
                    act.wait_ge(sem["attention_turned"], ph.at("turned", (h - 1) * ph.fills))
                for qb in range(QB):
                    nc.scalar.activation(probs[:, h % 2, qb, 0:ph.keys], SC[h % 2][:, qb * 512:qb * 512 + ph.keys],
                                         ACT.Exp, bias=nmax[:, h, qb:qb + 1],
                                         accum_out=sums[:, qb, h:h + 1]).then_inc(sem["attention_exp"], 1)

            def turned_copy(ph, n):
                h, j = n // ph.fills, n % ph.fills
                act.wait_ge(sem["attention_turned"], ph.at("turned", n + 1))
                if h >= ph.slots:
                    act.wait_ge(sem["attention_heads"], ph.at("heads", (h - ph.slots) // ph.group + 1))
                copy(probs_t[:, h % ph.slots, 2 * j:2 * j + 2, :],
                     PT[0][:, :].rearrange("p (k q) -> p k q", k=2)).then_inc(sem["attention_turned_copied0"], 1)

            def scale_copy(ph, g):
                act.wait_ge(sem["attention_heads"], ph.at("heads", g + 1))
                if g >= 2:
                    act.wait_ge(sem["attention_out_scaled"], ph.at("out_scaled", g - 1))
                copy(scale_t[:, g % 2, :], O[:, S:2 * S]).then_inc(sem["attention_scale"], 1)

            def attention(ph, has_t):
                if has_t:
                    t_high(ph, 0)
                    t_high(ph, 1)
                    t_high(ph, 2)
                exps(ph, 0)
                for h in range(ph.heads):
                    if h + 1 < ph.heads:
                        exps(ph, h + 1)
                    for n in range(h * ph.fills, (h + 1) * ph.fills):
                        if n % 2 == 0:
                            turned_copy(ph, n)
                    if has_t and h + 3 < ph.heads:
                        t_high(ph, h + 3)
                    if h % ph.group == 0 and h >= ph.group:
                        scale_copy(ph, h // ph.group - 1)
                scale_copy(ph, ph.groups - 1)

            def stack_high(n, kb_count):
                act.wait_ge(sem[f"{n}_q_nat"], 1)
                q4 = nat_q[:, :, :].rearrange("p b (h c) -> p b h c", h=H)
                copy(f32r(q_stack[:, :, :, 0:8]), q4).then_inc(sem[f"{n}_q_high"], 1)
                copy(f32r(q_stack[:, :, :, 8:16]), q4).then_inc(sem[f"{n}_q_stacked_act"], 1)
                act.wait_ge(sem[f"{n}_kv_nat"], 1)
                kv = nat_kv[:, 0:kb_count, 0:D].rearrange("p b (h c) -> p b h c", h=H)
                copy(f32r(k_stack[:, 0:kb_count, :, 0:8]), kv).then_inc(sem[f"{n}_k_high"], 1)
                copy(f32r(k_stack[:, 0:kb_count, :, 16:24]), kv).then_inc(sem[f"{n}_k_stacked_act"], 1)
                vv = nat_kv[:, 0:kb_count, D:2 * D].rearrange("p b (h c) -> p b h c", h=H)
                copy(v_pad[:, 0:kb_count, :, 0:8], vv).then_inc(sem[f"{n}_v_padded"], 1)
                act.wait_ge(sem[f"{n}_q_turned"], 1)
                for i in (0, 1):
                    r = slice(32 * i, 32 * i + 32)
                    copy(q_mask[r, :, i, :], S0[r, :].rearrange("p (g q) -> p g q", g=QUADS)).then_inc(sem[f"{n}_q_masked_act"], 1)

            def table_for(func):
                nc.scalar.activation(dummy[:, :], ident[:, 0:1], func)

            with act.Fori(0, B) as b:
                act.wait_ge(sem["ctx_turned"], 1)
                copy(ctx_hi[:, :], S0[0:C, 0:T]).then_inc(sem["ctx_hi"], 1)
                affine("ln1", "ln1g", "ln1b")
                for fill in (0, 2):
                    value_copy("self0", fill)
                attention(SELF0, True)
                for fill in (0, 2):
                    value_copy("cross0", fill)
                affine("ln2", "ln2g", "ln2b")
                for fill in (4, 6):
                    value_copy("cross0", fill)
                attention(CROSS0, True)

                table_for(ACT.Gelu_apprx_tanh)
                affine("ln3", "ln3g", "ln3b")
                for j in range(4):
                    act.wait_ge(sem["gate"], j + 1)
                    if j >= 2:
                        act.wait_ge(sem["gated"], j - 1)
                    nc.scalar.activation(gate[:, j % 2, :], S0[:, 512 * (j % 2):512 * (j % 2) + S],
                                         ACT.Gelu_apprx_tanh, bias=cols_of["bff1"][:, 4 + j:5 + j]).then_inc(sem["gelu"], 1)

                table_for(ACT.Exp)
                affine("audio", "g2", "beta2", cols=T, bank=S1)
                act.wait_ge(sem["x1_turned"], 1)
                copy(x_hi[:, :], X[:, 0:S]).then_inc(sem["x1_high"], 1)
                act.wait_ge(sem["norm_split"], TURNED.index("audio") + 1)
                affine("text", "g1", "beta1")
                attention(CROSS1, False)

                affine("m1", "m1g", "m1b")
                stack_high("self2", QB)
                attention(SELF2, False)
                affine("m2", "m2g", "m2b")
                stack_high("cross2", TB)
                attention(CROSS2, False)

                table_for(ACT.Gelu)
                affine("m3", "m3g", "m3b")
                for j in range(4):
                    act.wait_ge(sem["up"], j + 1)
                    nc.scalar.activation(prod[:, j, :], SC[j // 2][:, 512 * (j % 2):512 * (j % 2) + S],
                                         ACT.Gelu, bias=cols_of["bmlp1"][:, j:j + 1]).then_inc(sem["gelu2"], 1)

                table_for(ACT.Sqrt)
                affine("rms", "normw", None)
                for name, blocks in (("l3_kv_nat", TB), ("l3_q_nat", QB)):
                    act.wait_ge(sem[f"{name}_squares"], 1)
                    nc.scalar.activation(norm[:, 0:blocks, :], ss[:, 0:blocks, :],
                                         ACT.Sqrt).then_inc(sem[f"{name}_root"], 1)
                table_for(ACT.Exp)
                stack_high("l3", TB)
                for h in range(H):
                    act.wait_ge(sem["l3_scores"], h + 1)
                    if h >= 8:
                        act.wait_ge(sem["l3_heads"], (h - 8) // 4 + 1)
                    nc.scalar.activation(probs_t[:, h % 8, :, :],
                                         SC[h % 2][:, :].rearrange("p (k q) -> p k q", k=TB),
                                         ACT.Exp, scale=float(np.sqrt(np.float32(E2)))).then_inc(sem["l3_exp"], 1)
                batch_end(act, b)

        @block.vector
        def _(dve):
            chain = {"setup_chain": 0, "batch_chain": 0}

            def then(ins, name="batch_chain"):
                ins.then_inc(sem[name], 1)
                chain[name] += 1
                dve.wait_ge(sem[name], chain[name])

            def low_part(out, full, high):
                return nc.vector.tensor_tensor(out, full, f32(high), ALU.subtract)

            dve.wait_ge(sem["kept_loaded"], 16 * n_kept)
            dve.wait_ge(sem["raw_loaded"], 16 * n_raw)
            q_scale = float(E2) ** -0.5
            then(nc.vector.tensor_scalar(raw["wsa"][:, 0:D], raw["wsa"][:, 0:D], q_scale, None, ALU.mult), "setup_chain")
            nc.vector.tensor_scalar(raw["wcaq"], raw["wcaq"], q_scale, None, ALU.mult).then_inc(sem["raw_scaled"], 1)
            then(nc.vector.tensor_scalar(rows_of["bsa"][:, 0:D], rows_of["bsa"][:, 0:D], q_scale, None, ALU.mult), "setup_chain")
            then(nc.vector.tensor_scalar(rows_of["bcaq"][:, :], rows_of["bcaq"][:, :], q_scale, None, ALU.mult), "setup_chain")
            for name in ("g1", "beta1"):
                then(nc.vector.tensor_scalar(cols_of[name][:, :], cols_of[name][:, :], float(D) ** -0.5, None,
                                             ALU.mult), "setup_chain")
            dve.wait_ge(sem["raw_scaled"], 1)
            for n, name in enumerate(split):
                dve.wait_ge(sem["w_hi"], n + 1)
                low_part(split[name][1][:, :], raw[name], split[name][0][:, :]).then_inc(sem["w_lo"], 1)
            for fill in range(4):
                layer, half = fill // 2, fill % 2
                width = (D, C)[layer]
                dve.wait_ge(sem["m_hi"], 2 * fill + 2)
                for i in range(2):
                    view = lambda m: m[:, :, :].rearrange("p (j i) n -> p j i n", i=2)[:, 4 * half:4 * half + 4, i, :]
                    src = SC[fill % 2][:, 512 * i:512 * i + 4 * width].rearrange("p (j n) -> p j n", j=4)
                    nc.vector.scalar_tensor_tensor(view(m_lo[layer]), src, E0 ** -0.5, f32(view(m_hi[layer])),
                                                   op0=ALU.mult, op1=ALU.subtract).then_inc(sem["m_split"], 1)
            setup_end(dve)

            def normalise(n, src, blocks, hat_name):
                for k in range(blocks):
                    ins = nc.vector.bn_stats(stats[:, k, :], src[:, k, :])
                then(ins)
                for k in range(blocks):
                    ins = nc.vector.bn_aggr(moments[:, k, :], stats[:, k, :])
                then(ins)
                nc.vector.tensor_scalar(var_eps[:, 0:blocks], moments[:, 0:blocks, 1], EPS, None, ALU.add).then_inc(sem["var"], 1)
                dve.wait_ge(sem["rstd"], NORMS.index(n) + 1)
                for k in range(blocks):
                    nc.vector.tensor_scalar(xhat[:, k, :], src[:, k, :], moments[:, k, 0:1], rstd[:, k:k + 1],
                                            ALU.subtract, ALU.mult).then_inc(sem[hat_name], 1)
                dve.wait_ge(sem[hat_name], blocks)

            def split_x(n, hi=None, lo=None, cols=S):
                hi, lo = (x_hi[:, :], x_lo[:, :]) if hi is None else (hi, lo)
                dve.wait_ge(sem["norm_affine"], TURNED.index(n) + 1)
                then(nc.vector.tensor_copy(hi, xz[:, 0:cols]))
                low_part(lo, xz[:, 0:cols], hi).then_inc(sem["norm_split"], 1)

            def add_row(dst, row):
                then(nc.vector.tensor_tensor(dst, dst, rows_of[row][:, :].unsqueeze(1).to_broadcast([P, QB, D]),
                                             ALU.add))

            def add_projected(n, done=None):
                dve.wait_ge(sem[f"{n}_projected"], 1)
                ins = nc.vector.tensor_tensor(x[:, :, :], X[:, 0:S].rearrange("p (b n) -> p b n", b=QB), x[:, :, :],
                                              ALU.add)
                if done:
                    ins.then_inc(sem[done], 1)
                    dve.wait_ge(sem[done], 1)
                else:
                    then(ins)

            def value_copy(name, fill):
                dve.wait_ge(sem[f"{name}_v"], fill + 1)
                kb, half = fill // 2, fill % 2
                nc.vector.tensor_copy(v0[:, kb, 512 * half:512 * half + 512],
                                      SC[(fill // 2) % 2][:, 512 * half:512 * half + 512]).then_inc(sem[f"{name}_v_dve"], 1)

            def maximum(ph, h):
                dve.wait_ge(sem["attention_scores"], ph.at("scores", h + 1))
                src = SC[h % 2][:, :].rearrange("p (b k) -> p b k", b=QB)[:, :, 0:ph.keys]
                nc.vector.tensor_reduce(nmax[:, h, :], src, AX.X, ALU.max, negate=True).then_inc(sem["attention_max"], 1)

            def t_low(ph, h):
                dve.wait_ge(sem["attention_t_hi"], ph.at("t_hi", h + 1))
                low_part(t_lo[0:ph.t_rows, h % 2, :], X[0:ph.t_rows, 0:S], t_hi[0:ph.t_rows, h % 2, :]).then_inc(sem["attention_t_lo"], 1)

            def turned_copy(ph, n):
                h, j = n // ph.fills, n % ph.fills
                dve.wait_ge(sem["attention_turned"], ph.at("turned", n + 1))
                if h >= ph.slots:
                    dve.wait_ge(sem["attention_heads"], ph.at("heads", (h - ph.slots) // ph.group + 1))
                nc.vector.tensor_copy(probs_t[:, h % ph.slots, 2 * j:2 * j + 2, :],
                                      PT[1][:, :].rearrange("p (k q) -> p k q", k=2)).then_inc(sem["attention_turned_copied1"], 1)

            def inverse_sums(ph, g):
                dve.wait_ge(sem["attention_exp"], ph.at("exp", QB * ph.group * (g + 1)))
                s = inv[:, :, 0:ph.group]
                then(nc.vector.reciprocal(s, sums[:, :, g * ph.group:(g + 1) * ph.group]))
                nc.vector.tensor_copy(rinv[:, :, :].rearrange("p b (h c) -> p b h c", h=ph.group),
                                      s.unsqueeze(3).to_broadcast([P, QB, ph.group, ph.rows])
                                      ).then_inc(sem["attention_rinv"], 1)

            def scale_out(ph, g):
                dve.wait_ge(sem["attention_scale"], ph.at("scale", g + 1))
                nc.vector.tensor_tensor(out_t[:, g, :], O[:, 0:S], scale_t[:, g % 2, :], ALU.mult).then_inc(sem["attention_out_scaled"], 1)

            def attention(ph, has_t):
                if has_t:
                    t_low(ph, 0)
                    t_low(ph, 1)
                maximum(ph, 0)
                if has_t:
                    t_low(ph, 2)
                if ph.heads > 1:
                    maximum(ph, 1)
                for h in range(ph.heads):
                    if h + 2 < ph.heads:
                        maximum(ph, h + 2)
                    if h % ph.group == 0 and h >= ph.group:
                        inverse_sums(ph, h // ph.group - 1)
                    for n in range(h * ph.fills, (h + 1) * ph.fills):
                        if n % 2 == 1:
                            turned_copy(ph, n)
                    if has_t and h + 3 < ph.heads:
                        t_low(ph, h + 3)
                    if h % ph.group == 0 and h >= ph.group:
                        scale_out(ph, h // ph.group - 1)
                inverse_sums(ph, ph.groups - 1)
                scale_out(ph, ph.groups - 1)

            def stack_low(n, kb_count):
                q4 = nat_q[:, :, :].rearrange("p b (h c) -> p b h c", h=H)
                dve.wait_ge(sem[f"{n}_q_high"], 1)
                nc.vector.tensor_tensor(f32r(q_stack[:, :, :, 16:24]), q4, q_stack[:, :, :, 0:8], ALU.subtract).then_inc(sem[f"{n}_q_stacked"], 1)
                kv = nat_kv[:, 0:kb_count, 0:D].rearrange("p b (h c) -> p b h c", h=H)
                dve.wait_ge(sem[f"{n}_k_high"], 1)
                nc.vector.tensor_tensor(f32r(k_stack[:, 0:kb_count, :, 8:16]), kv,
                                        k_stack[:, 0:kb_count, :, 0:8], ALU.subtract).then_inc(sem[f"{n}_k_stacked"], 1)
                dve.wait_ge(sem[f"{n}_q_turned"], 1)
                for i in (2, 3):
                    r = slice(32 * i, 32 * i + 32)
                    nc.vector.tensor_copy(q_mask[r, :, i, :], S0[r, :].rearrange("p (g q) -> p g q", g=QUADS)).then_inc(sem[f"{n}_q_masked_dve"], 1)
                for r in range(kb_count // 2):
                    dve.wait_ge(sem[f"{n}_k_turned"], r + 1)
                    nc.vector.tensor_copy(k_t[:, :, r * S:(r + 1) * S],
                                          S1[:, :].rearrange("p (g q) -> p g q", g=QUADS)).then_inc(sem[f"{n}_k_copied"], 1)

            def clear_stack_pads():
                nc.vector.memset(q_stack[:, :, :, 24:32], 0.0).then_inc(sem["q_pads"], 1)
                nc.vector.memset(k_stack[:, :, :, 24:32], 0.0).then_inc(sem["k_pads"], 1)
                dve.wait_ge(sem["q_pads"], 1)
                dve.wait_ge(sem["k_pads"], 1)

            def rope_and_normalise(y, blocks, last_name):
                y4 = y.rearrange("p b (h c) -> p b h c", h=H)
                cos = rope_cos[:, 0:blocks, :].unsqueeze(2).to_broadcast([P, blocks, H, E2])
                sin = rope_sin[:, 0:blocks, :].unsqueeze(2).to_broadcast([P, blocks, H, E2])
                tmp, pr = rope_tmp[:, 0:blocks], rope_prod[:, 0:blocks]
                half = E2 // 2
                nc.vector.tensor_tensor(tmp[:, :, :, 0:half], y4[:, :, :, half:E2], sin[:, :, :, 0:half], ALU.mult)
                nc.vector.tensor_tensor(tmp[:, :, :, half:E2], y4[:, :, :, 0:half], sin[:, :, :, half:E2], ALU.mult)
                then(nc.vector.tensor_tensor(pr, y4, cos, ALU.mult))
                then(nc.vector.tensor_tensor(tmp, tmp, pr, ALU.add))
                then(nc.vector.tensor_tensor(pr, tmp, tmp, ALU.mult))
                then(nc.vector.tensor_reduce(ss[:, 0:blocks, :], pr, AX.X, ALU.add))
                nc.vector.tensor_scalar(ss[:, 0:blocks, :], ss[:, 0:blocks, :], EPS_L2 ** 2, None,
                                        ALU.max).then_inc(sem[f"{last_name}_squares"], 1)
                dve.wait_ge(sem[f"{last_name}_root"], 1)
                then(nc.vector.reciprocal(norm[:, 0:blocks, :], norm[:, 0:blocks, :]))
                nc.vector.tensor_tensor(y4, tmp, norm[:, 0:blocks, :].unsqueeze(3).to_broadcast([P, blocks, H, E2]),
                                        ALU.mult).then_inc(sem[last_name], 1)
                dve.wait_ge(sem[last_name], 1)

            with dve.Fori(0, B) as b:
                dve.wait_ge(sem["x_loaded"], 16)
                normalise("ln1", x, QB, "ln1_hat")
                add_row(x[:, :, :], "bo1")
                dve.wait_ge(sem["ctx_hi"], 1)
                low_part(ctx_lo[:, :], S0[0:C, 0:T], ctx_hi[:, :]).then_inc(sem["ctx_lo"], 1)
                split_x("ln1")
                for fill in (1, 3):
                    value_copy("self0", fill)
                attention(SELF0, True)
                add_projected("self0")

                normalise("ln2", x, QB, "ln2_hat")
                for fill in (1, 3):
                    value_copy("cross0", fill)
                split_x("ln2")
                for fill in (5, 7):
                    value_copy("cross0", fill)
                add_row(x[:, :, :], "bo2")
                attention(CROSS0, True)
                add_projected("cross0")

                normalise("ln3", x, QB, "ln3_hat")
                add_row(x[:, :, :], "bff2")
                split_x("ln3")
                for j in range(4):
                    dve.wait_ge(sem["linear"], j + 1)
                    dve.wait_ge(sem["gelu"], j + 1)
                    nc.vector.scalar_tensor_tensor(prod[:, j, :], S1[:, 512 * (j % 2):512 * (j % 2) + S],
                                                   cols_of["bff1"][:, j:j + 1], gate[:, j % 2, :],
                                                   op0=ALU.add, op1=ALU.mult).then_inc(sem["gated"], 1)
                add_projected("ff", "x_ff")

                dve.wait_ge(sem["audio"], 1)
                then(nc.vector.tensor_tensor(v1, S0[:, 0:T].rearrange("p (b n) -> p b n", b=TB),
                                             rows_of["baudio"][:, :].unsqueeze(1).to_broadcast([P, TB, D]), ALU.add))
                normalise("audio", v1, TB, "audio_hat")
                split_x("audio", k1_hi, k1_lo, T)
                dve.wait_ge(sem["x1_high"], 1)
                low_part(x_lo[:, :], X[:, 0:S], x_hi[:, :]).then_inc(sem["x1_split"], 1)
                dve.wait_ge(sem["text"], 1)
                then(nc.vector.tensor_tensor(nat_q[:, :, :], O[:, 0:S].rearrange("p (b n) -> p b n", b=QB),
                                             rows_of["btext"][:, :].unsqueeze(1).to_broadcast([P, QB, D]), ALU.add))
                normalise("text", nat_q, QB, "text_hat")
                split_x("text")
                add_row(x[:, :, :], "bout")
                attention(CROSS1, False)
                add_projected("cross1")
                normalise("out1", x, QB, "out1_hat")
                for k in range(QB):
                    then(nc.vector.tensor_tensor(x[:, k, :], xhat[:, k, :], rows_of["gout"][:, :], ALU.mult))
                add_row(x[:, :, :], "betaout")

                normalise("m1", x, QB, "m1_hat")
                add_row(x[:, :, :], "bosa")
                clear_stack_pads()
                split_x("m1")
                dve.wait_ge(sem["self2_qkv"], 1)
                src = S0[:, :].rearrange("p (b n) -> p b n", b=QB)
                bsa = rows_of["bsa"][:, :].unsqueeze(1)
                nc.vector.tensor_tensor(nat_q[:, :, :], src[:, :, 0:D], bsa[:, :, 0:D].to_broadcast([P, QB, D]),
                                        ALU.add).then_inc(sem["self2_q_nat"], 1)
                nc.vector.tensor_tensor(nat_kv[:, 0:QB, :], src[:, :, D:3 * D],
                                        bsa[:, :, D:3 * D].to_broadcast([P, QB, 2 * D]), ALU.add).then_inc(sem["self2_kv_nat"], 1)
                stack_low("self2", QB)
                attention(SELF2, False)
                add_projected("self2")

                normalise("m2", x, QB, "m2_hat")
                add_row(x[:, :, :], "boca")
                dve.wait_ge(sem["cross2_kv"], 1)
                bkv = rows_of["bcakv"][:, :].unsqueeze(1).to_broadcast([P, TB, 2 * D])
                nc.vector.tensor_tensor(nat_kv[:, :, :], S1[:, :].rearrange("p (b n) -> p b n", b=TB), bkv,
                                        ALU.add).then_inc(sem["cross2_kv_nat"], 1)
                split_x("m2")
                dve.wait_ge(sem["cross2_q"], 1)
                nc.vector.tensor_tensor(nat_q[:, :, :], src[:, :, 0:D],
                                        rows_of["bcaq"][:, :].unsqueeze(1).to_broadcast([P, QB, D]), ALU.add).then_inc(sem["cross2_q_nat"], 1)
                stack_low("cross2", TB)
                attention(CROSS2, False)
                add_projected("cross2")

                normalise("m3", x, QB, "m3_hat")
                add_row(x[:, :, :], "bmlp2")
                split_x("m3")
                add_projected("mlp")

                then(nc.vector.tensor_tensor(xhat[:, 0:QB, :], x[:, :, :], x[:, :, :], ALU.mult))
                then(nc.vector.tensor_reduce(moments[:, 0:QB, 0], xhat[:, 0:QB, :], AX.X, ALU.add))
                nc.vector.tensor_scalar(var_eps[:, 0:QB], moments[:, 0:QB, 0], 1.0 / D, EPS, ALU.mult, ALU.add).then_inc(sem["var"], 1)
                dve.wait_ge(sem["rstd"], NORMS.index("rms") + 1)
                for k in range(QB):
                    nc.vector.tensor_scalar(xhat[:, k, :], x[:, k, :], rstd[:, k:k + 1], None, ALU.mult).then_inc(sem["rms_hat"], 1)
                dve.wait_ge(sem["l3_kv"], 1)
                then(nc.vector.tensor_copy(nat_kv[:, :, :], S1[:, :].rearrange("p (b n) -> p b n", b=TB)))
                split_x("rms")
                rope_and_normalise(nat_kv[:, :, 0:D], TB, "l3_kv_nat")
                dve.wait_ge(sem["l3_q"], 1)
                then(nc.vector.tensor_copy(nat_q[:, :, :], src[:, :, 0:D]))
                rope_and_normalise(nat_q[:, :, :], QB, "l3_q_nat")
                stack_low("l3", TB)
                for g in range(QUADS):
                    dve.wait_ge(sem["l3_heads"], g + 1)
                    nc.vector.tensor_copy(scale_t[:, g % 2, :], O[:, 0:S]).then_inc(sem["l3_heads_copied"], 1)
                    dve.wait_ge(sem["l3_sums"], g + 1)
                    then(nc.vector.reciprocal(out_t[:, QUADS + g % 2, :], O[:, S:2 * S]))
                    nc.vector.tensor_tensor(out_t[:, g, :], scale_t[:, g % 2, :], out_t[:, QUADS + g % 2, :],
                                            ALU.mult).then_inc(sem["l3_scaled"], 1)
                add_projected("l3", "y_ready")
                batch_end(dve, b)

        @block.gpsimd
        def _(pool):
            nc.gpsimd.memset(minus_half[:, :], -0.5)
            for k in range(3):
                nc.gpsimd.memset(wo_pad[k][:, :, :], 0.0).then_inc(sem["pads_clear"], 1)
            nc.gpsimd.memset(f32(q_mask[:, :, :, :]), 0.0)
            nc.gpsimd.memset(v_pad[:, :, :, :], 0.0).then_inc(sem["pads_clear"], 1)
            pool.wait_ge(sem["pads_clear"], 4)
            nc.gpsimd.memset(v_pad[:, :, :, E2:E2 + 1], 1.0)
            setup_end(pool)

            def power(n, blocks):
                pool.wait_ge(sem["var"], NORMS.index(n) + 1)
                nc.gpsimd.tensor_tensor(rstd[:, 0:blocks], var_eps[:, 0:blocks], minus_half[:, 0:blocks],
                                        ALU.pow).then_inc(sem["rstd"], 1)

            with pool.Fori(0, B) as b:
                for n in NORMS:
                    power(n, TB if n == "audio" else QB)
                batch_end(pool, b)

        @block.sync
        def _(sp):
            for name, dst in SINGLE + RAW:
                sp.dma_start(dst, A[name]).then_inc(sem["raw_loaded"], 16)
            sp.wait_ge(sem["pads_clear"], 4)
            for k, name in enumerate(("sawo", "cawo", "l3wo")):
                for i in range(4):
                    sp.dma_start(wo_pad[k][32 * i:32 * i + E2, :, :], A[name][i]).then_inc(sem["wo_loaded"], 16)
            sp.wait_ge(sem["wo_loaded"], 16 * 12)
            setup_end(sp)
            with sp.Fori(0, B) as b:
                sp.dma_start(x[:, :, :], A["x"][:, bass.ds(b * QB, QB), :]).then_inc(sem["x_loaded"], 16)
                sp.dma_start(ctx_nat[:, :, :], A["ctx"][:, bass.ds(b * TB, TB), :]).then_inc(sem["ctx_loaded"], 16)
                sp.wait_ge(sem["y_ready"], 1)
                sp.dma_start(y_out[:, bass.ds(b * QB, QB), :], x[:, :, :]).then_inc(sem["y_stored"], 16)
                sp.wait_ge(sem["batch_done"], ENGINES - 1)
                sp.wait_ge(sem["y_stored"], 16)
                sp.sem_clear(sem.ids()).then_inc(batch_open, 1)


def rope_tables():
    inv = 1.0 / 10000.0 ** (np.arange(0, E2, 2, dtype=np.float32) / E2)
    freqs = np.einsum("i,j->ij", np.arange(T, dtype=np.float32), inv)
    emb = np.concatenate([freqs, freqs], axis=-1)
    sign = np.concatenate([-np.ones(E2 // 2, np.float32), np.ones(E2 // 2, np.float32)])
    by_partition = lambda t: t.astype(np.float32).reshape(TB, P, E2).transpose(1, 0, 2)
    return by_partition(np.cos(emb)), by_partition(np.sin(emb) * sign)


def layout(a):
    l0, l1, l2, l3 = (f"L{n}_xattn_" for n in range(4))
    cols = lambda v: v.reshape(-1, P).T
    out = {"x": a["x"], "ctx": a["ctx_768"]}
    out["ident"] = np.eye(P, dtype=np.float32)
    sum_rows = np.zeros((P, P), np.float32)
    for i in range(4):
        sum_rows[32 * i + E2, 32 * i:32 * i + 32] = 1.0
    out["sum_rows"] = sum_rows
    out["rope_cos"], out["rope_sin"] = rope_tables()
    for n in (1, 2):
        out[f"wqt{n - 1}"] = a[f"{l0}wq{n}"].T
        out[f"wkt{n - 1}"] = a[f"{l0}wk{n}"].T
        out[f"wv{n}"] = a[f"{l0}wv{n}"]
        out[f"wo{n}"] = a[f"{l0}wo{n}"]
        out[f"bo{n}"] = a[f"{l0}bo{n}"]
    for n in (1, 2, 3):
        out[f"ln{n}g"], out[f"ln{n}b"] = cols(a[f"{l0}ln{n}_g"]), cols(a[f"{l0}ln{n}_b"])
        out[f"m{n}g"], out[f"m{n}b"] = cols(a[f"{l2}ln{n}_g"]), cols(a[f"{l2}ln{n}_b"])
    out["wff1"], out["wff2"] = a[l0 + "w_ff1"], a[l0 + "w_ff2"]
    out["bff1"], out["bff2"] = cols(a[l0 + "b_ff1"]), a[l0 + "b_ff2"]
    out["wtext"], out["waudio"], out["wout1"] = a[l1 + "W_text"], a[l1 + "W_audio"], a[l1 + "W_out"]
    out["btext"], out["baudio"], out["bout"] = a[l1 + "b_text"], a[l1 + "b_audio"], a[l1 + "b_out"]
    for n in ("g1", "beta1", "g2", "beta2"):
        out[n] = cols(a[l1 + n])
    out["gout"], out["betaout"] = a[l1 + "g_out"], a[l1 + "beta_out"]
    for k in "qkv":
        out[f"saw{k}"], out[f"caw{k}"] = a[f"{l2}sa_w{k}"].T, a[f"{l2}ca_w{k}"].T
        out[f"sab{k}"], out[f"cab{k}"] = a[f"{l2}sa_b{k}"], a[f"{l2}ca_b{k}"]
    out["wcaq"], out["bcaq"] = out.pop("cawq"), out.pop("cabq")
    out["sawo"], out["cawo"], out["l3wo"] = a[l2 + "sa_wo"].T, a[l2 + "ca_wo"].T, a[l3 + "wout"]
    out["bosa"], out["boca"] = a[l2 + "sa_bo"], a[l2 + "ca_bo"]
    out["wmlp1"], out["wmlp2"] = a[l2 + "mlp_w1"].T, a[l2 + "mlp_w2"].T
    out["bmlp1"], out["bmlp2"] = cols(a[l2 + "mlp_b1"]), a[l2 + "mlp_b2"]
    out["wl3q"], out["wl3kv"], out["normw"] = a[l3 + "wq"], a[l3 + "wkv"], cols(a[l3 + "norm_w"])
    return {n: np.ascontiguousarray(v) for n, v in out.items()}


VIEWS = {"x": "b (q p) n -> p (b q) n", "ctx": "b (q p) n -> p (b q) n"}
VIEWS |= dict.fromkeys(("wqt0", "wkt0", "wqt1", "wkt1", "wo1", "wo2", "wff2", "wmlp2"), "(j p) n -> p j n")
VIEWS |= dict.fromkeys(("sawo", "cawo", "l3wo"), "(g i c) n -> i c g n")
SIZES = {"(j p) n -> p j n": {"p": P}, "(g i c) n -> i c g n": {"i": 4, "c": E2}, VIEWS["x"]: {"p": P}}
ROWS = ("bo1", "bo2", "bff2", "btext", "baudio", "bout", "gout", "betaout", "sabq", "sabk", "sabv", "bcaq",
        "cabk", "cabv", "bosa", "boca", "bmlp2")


def kernel(**inputs):
    from concourse import bacc
    from concourse.bass_utils import run_bass_kernel_spmd

    arrays = layout({n: np.asarray(v) for n, v in inputs.items()})
    nc = bacc.Bacc("TRN2", target_bir_lowering=False, num_devices=1, dynamic_dma_scratch_size=1024)
    A = {}
    for name, a in arrays.items():
        ap = nc.dram_tensor(name + "_dram", a.shape, mybir.dt.from_np(a.dtype), kind="ExternalInput").ap()
        if name in VIEWS:
            ap = ap.rearrange(VIEWS[name], **SIZES[VIEWS[name]])
        elif name in ROWS:
            ap = ap.partition_broadcast(P)
        A[name] = ap
    y = nc.dram_tensor("y_dram", arrays["x"].shape, F32, kind="ExternalOutput").ap().rearrange(VIEWS["x"], p=P)
    program(nc, A, y)
    r = run_bass_kernel_spmd(nc, [{n + "_dram": a for n, a in arrays.items()}], core_ids=[0])
    return r.results[0]["y_dram"]
```

```python
from contextlib import ExitStack

import numpy as np

import concourse.bass as bass
from concourse import mybir

F32 = mybir.dt.float32
F32R = mybir.dt.float32r
ACT = mybir.ActivationFunctionType
ALU = mybir.AluOpType
AX = mybir.AxisListType

B, S, D = 8, 256, 128
T, C = 512, 96
H = 16
E0 = 64
E2 = 8
INNER = H * E0
FF = 4 * D
P = 128
QB = S // P
TB = T // P
PAIRS = H // 2
QUADS = H // 4
STREAMS = 2
PROBS_SLOTS = 5
EPS = 1e-5
EPS_L2 = 1e-12
ENGINES = 5


class Semaphores:

    def __init__(self, nc, ctx):
        self.nc, self.ctx, self.by_name = nc, ctx, {}

    def __getitem__(self, name):
        if name not in self.by_name:
            self.by_name[name] = self.ctx.enter_context(self.nc.semaphore(name))
        return self.by_name[name]

    def ids(self):
        ids = sorted(s.num for s in self.by_name.values())
        assert ids == list(range(ids[0], ids[0] + len(ids)))
        return range(ids[0], ids[0] + len(ids))


class Attention:

    def __init__(self, name, s, group, keys, t_rows=0, masked=False, key_major=False):
        self.name, self.s, self.group, self.keys, self.t_rows = name, s, group, keys, t_rows
        self.masked, self.key_major = masked, key_major
        self.kb = keys // P
        self.per_head = keys // S
        self.units = H * self.per_head
        self.groups = H // group
        self.slots = min(2 * group, PROBS_SLOTS)
        self.rows = P // group
        self.before = {}

    def counts(self):
        t = H if self.t_rows else 0
        qm = 0 if self.key_major else 1
        return {"t": t, "t_hi": t, "t_lo": t, "mask": H if self.masked else 0, "scores": self.units,
                "max": self.units * qm, "exp": self.units, "turned": self.units * qm,
                "copied0": self.units // 2 * qm, "copied1": self.units // 2 * qm, "rinv": self.groups * qm,
                "heads": self.groups, "scale": self.groups, "out_scaled": self.groups}

    def at(self, what, n):
        return self.before[what] + n

    def ends_group(self, u):
        n = self.group * self.per_head
        return u // n - 1 if u % n == 0 and u else None


MAKE = {"self0": lambda s: Attention("self0", s, 2, S, t_rows=D),
        "cross0": lambda s: Attention("cross0", s, 2, T, t_rows=C),
        "self2": lambda s: Attention("self2", s, 4, S, masked=True),
        "cross2": lambda s: Attention("cross2", s, 4, T, masked=True),
        "l3": lambda s: Attention("l3", s, 4, T, masked=True, key_major=True)}

CHAINS = {
    "start": "ctx stats hat ln1 split v0 v1 v2 v3",
    "mid0": "audio wo stats hat v0 astats ln2 v1 split v2 ahat v3 audio_t v4 asplit v5 v6 v7",
    "mid1": "wo stats hat ln3 gate l0 l1 down x1_t x1_lo text "
            "tstats that text_t tsplit s0 e0 s1 e1 p0 p1 pv sc wout ostats ohat mstats mhat m1_t msplit "
            "qkv0 qkv1 high low qt0 qt1 kt0 kt1",
    "mid2": "wo stats hat kv0 kv1 m2_t msplit q high low qt0 qt1 kt0 kt1 kt2 kt3",
    "mid3": "wo stats hat m3_t up down squares rmshat kv0 kv1 krope rms_t rsplit q qrope root unit high "
            "low qt0 qt1 kt0 kt1 kt2 kt3",
    "end": "wo",
}
FILLS = {
    "start": "ctx ln1 v0 v1 v2 v3",
    "mid0": "audio wo v0 ln2 v1 v2 v3 audio_t v4 v5 v6 v7",
    "mid1": "wo ln3 g0 g1 l0 l1 down x1_t text text_t s0 s1 p0 p1 pv wout m1_t qkv0 qkv1 "
            "qt0 qt1 kt0 kt1",
    "mid2": "wo kv0 kv1 m2_t q qt0 qt1 kt0 kt1 kt2 kt3",
    "mid3": "wo m3_t up0 up1 down kv0 kv1 rms_t q qt0 qt1 kt0 kt1 kt2 kt3",
    "end": "wo",
}
NORMS = {"start": "ln1", "mid0": "ln2 audio", "mid1": "ln3 text out1 m1", "mid2": "m2", "mid3": "m3 rms", "end": ""}

SPLITS = {"start": "ln1", "mid0": "ln2 audio", "mid1": "text m1", "mid2": "m2", "mid3": "rms", "end": ""}


PAIR = [("self0", 0, [("start", 1)]), ("self0", 1, [("mid0", 0)]), ("cross0", 0, [("mid0", 1)]),
        ("cross0", 1, [("mid1", 0)]), ("self2", 0, [("mid1", 1)]), ("self2", 1, [("mid2", 0)]),
        ("cross2", 0, [("mid2", 1)]), ("cross2", 1, [("mid3", 0)]), ("l3", 0, [("mid3", 1)])]
SEGMENTS = {
    "first": [("", 0, [("start", 0)])],
    "loop": PAIR + [("l3", 1, [("end", 0), ("start", 0)]), ("", 0, [("end", 1)])],
    "last": PAIR + [("l3", 1, [("end", 0)]), ("", 0, [("end", 1)])],
}
LOOPS = B // STREAMS - 1

TOTAL = {"l1_max": 2, "pads": 2, "l3_heads_copied": QUADS}
CHAIN_OF = {"ctx_high": "start", "x1_high": "mid1", "l1_max": "mid1", "l1_rinv": "mid1", "l1_scale": "mid1",
            "pads": "mid1", "squares": "mid3", "root": "mid3", "l3_heads_copied": "l3"}

ORDER = []
PHASES = {}
FILL = {}
NORM = {}
SPLIT = {}


def enter(segment):
    for table in (ORDER, PHASES, FILL, NORM, SPLIT):
        table.clear()
    total = {}
    for phase, ps, chains in SEGMENTS[segment]:
        if phase:
            ph = PHASES[phase, ps] = MAKE[phase](ps)
            ph.before = dict.fromkeys(ph.counts(), 0) | total
            total = {what: ph.before[what] + n for what, n in ph.counts().items()}
            ORDER.append((phase, ps))
        for chain, s in chains:
            ORDER.append((chain, s))
            for table, of_chain in ((FILL, FILLS), (NORM, NORMS), (SPLIT, SPLITS)):
                for content in of_chain[chain].split():
                    table[chain, s, content] = len(table) + 1


def rank(s, name):
    return [key[1] for key in ORDER if key[0] == name].index(s)


def precedes(first, second):
    return first in ORDER and ORDER.index(first) < ORDER.index(second)


def early_t(ph):
    return (range(2, 4) if ph.per_head == 1 else (2,)) if ph.t_rows else ()


def next_t(ph, u):
    ahead = u + (4 if ph.per_head == 1 else 5)
    return ahead // ph.per_head if ph.t_rows and ahead < ph.units and ahead % ph.per_head == 0 else None


W = {}


def due(steps, units):
    at, seen = {}, 0.0
    total = sum(W.get(step, 1.0) for step in steps)
    for step in steps:
        at[step] = int(seen * units / total)
        seen += W.get(step, 1.0)
    return at


def run_rounds(segment, attention, chain):
    for phase, ps, chains in SEGMENTS[segment]:
        units = PHASES[phase, ps].units if phase else 1
        at = due([(name, s, step) for name, s in chains for step in CHAINS[name].split()], units)
        work = ((name, s, step) for name, s in chains for step in chain(name, s))
        emitted = attention(PHASES[phase, ps]) if phase else iter((None,))
        ahead = next(work, None)
        for u in range(units):
            next(emitted)
            while ahead is not None and at[ahead] <= u:
                ahead = next(work, None)
        assert ahead is None and next(emitted, "over") == "over"


def program(nc, A, y_out):
    ctx = ExitStack()
    with ctx:
        def sb(name, shape, dt=F32):
            return ctx.enter_context(nc.sbuf_tensor(name, shape, dt))

        def ps(name, cols=512):
            return ctx.enter_context(nc.psum_tensor(name, [P, cols], F32))

        def f32r(ap):
            return ap.bitcast(F32R)

        def f32(ap):
            return ap.bitcast(F32)

        def per_stream(name, shape, dt=F32):
            return [sb(f"{name}_{s}", shape, dt) for s in range(STREAMS)]

        ident = sb("ident", [P, P])
        sum_rows = sb("sum_rows", [P, P])
        rope_cos = sb("rope_cos", [P, TB, E2])
        rope_sin = sb("rope_sin", [P, TB, E2])
        minus_half = sb("minus_half", [P, TB])
        m_hi = [sb("m1_hi", [P, H, D], F32R), sb("m2_hi", [P, H, C], F32R)]
        m_lo = [sb("m1_lo", [P, H, D], F32R), sb("m2_lo", [P, H, C], F32R)]
        split = {}
        for name, rows, cols in (("wv1", D, INNER), ("wv2", C, INNER), ("wtext", D, D),
                                 ("waudio", C, D), ("wsa", D, 3 * D), ("wcaq", D, D), ("wcakv", C, 2 * D),
                                 ("wl3q", D, D), ("wl3kv", C, 2 * D)):
            split[name] = (sb(name + "_hi", [rows, cols], F32R), sb(name + "_lo", [rows, cols], F32R))
        wo = [sb("wo1", [P, PAIRS, D]), sb("wo2", [P, PAIRS, D])]
        wff1 = sb("wff1", [D, 2 * FF])
        wff2 = sb("wff2", [P, FF // P, D])
        wout1 = sb("wout1", [P, D])
        wmlp1 = sb("wmlp1", [D, FF])
        wmlp2 = sb("wmlp2", [P, FF // P, D])
        wo_pad = [sb("wo_sa", [P, QUADS, D]), sb("wo_ca", [P, QUADS, D]), sb("wo_l3", [P, QUADS, D])]
        rows_of = {}
        for name, cols in (("bo1", D), ("bo2", D), ("bff2", D), ("btext", D), ("baudio", D), ("bout", D),
                           ("gout", D), ("betaout", D), ("bsa", 3 * D), ("bcaq", D), ("bcakv", 2 * D),
                           ("bosa", D), ("boca", D), ("bmlp2", D)):
            rows_of[name] = sb("row_" + name, [P, cols])
        cols_of = {}
        for name, n in (("ln1g", 1), ("ln1b", 1), ("ln2g", 1), ("ln2b", 1), ("ln3g", 1), ("ln3b", 1),
                        ("bff1", 2 * FF // P), ("g1", 1), ("beta1", 1), ("g2", 1), ("beta2", 1),
                        ("m1g", 1), ("m1b", 1), ("m2g", 1), ("m2b", 1), ("m3g", 1), ("m3b", 1),
                        ("bmlp1", FF // P), ("normw", 1)):
            cols_of[name] = sb("col_" + name, [P, n])

        x = per_stream("x", [P, QB, D])
        ctx_hi, ctx_lo = per_stream("ctx_hi", [C, T], F32R), per_stream("ctx_lo", [C, T], F32R)
        x_hi, x_lo = per_stream("x_hi", [P, S], F32R), per_stream("x_lo", [P, S], F32R)
        v = per_stream("v", [P, TB * INNER])
        out_t = per_stream("out_t", [P, PAIRS, S])
        q_t = per_stream("q_t", [P, QUADS, S], F32R)
        k_t = per_stream("k_t", [P, QUADS, T], F32R)
        v0 = [t[:, :].rearrange("p (b n) -> p b n", b=TB) for t in v]
        probs1 = [t[:, 512:1536].rearrange("p (b k) -> p b k", b=QB) for t in v]
        probs1_t = [t[:, 1536:2560].rearrange("p (k q) -> p k q", k=TB) for t in v]
        l1_rinv = [t[:, 2560:2816].rearrange("p (b n) -> p b n", b=QB) for t in v]
        l1_scale = [t[:, 2816:3072] for t in v]
        k_stack = [t[:, 0:2048].rearrange("p (b h c) -> p b h c", b=TB, h=H) for t in v]
        v_pad = [t[:, 2048:4096].rearrange("p (b h c) -> p b h c", b=TB, h=H) for t in v]
        hidden = [t[:, 0:4, :] for t in out_t]
        q_stack = [t[:, 0:4, :].rearrange("p a c -> p (a c)").rearrange("p (b h c) -> p b h c", b=QB, h=H)
                   for t in out_t]
        rope_tmp = [t[:, 4:6, :].rearrange("p a c -> p (a c)").rearrange("p (b h c) -> p b h c", b=TB, h=H)
                    for t in out_t]
        rope_prod = [t[:, 6:8, :].rearrange("p a c -> p (a c)").rearrange("p (b h c) -> p b h c", b=TB, h=H)
                     for t in out_t]
        ctx_nat = [t[:, 0:2, :].rearrange("p a c -> p (a c)")[:, 0:TB * C].rearrange("p (b n) -> p b n", b=TB)
                   for t in out_t]
        k1_hi, k1_lo = [t[:, 0, :] for t in k_t], [t[:, 1, :] for t in k_t]

        stats = sb("stats", [P, TB, 6])
        moments = sb("moments", [P, TB, 2])
        var_eps = sb("var_eps", [P, TB])
        rstd = sb("rstd", [P, TB])
        xhat = sb("xhat", [P, TB, D])
        xz = sb("xz", [P, T])
        nat_q = xhat[:, TB - QB:TB, :]
        nat_kv = sb("nat_kv", [P, TB, 2 * D])
        ss = sb("ss", [P, TB + QB, H])
        norm = sb("norm", [P, TB + QB, H])
        l1_nmax = sb("l1_nmax", [P, QB])
        l1_sums = sb("l1_sums", [P, QB])
        t_hi, t_lo = sb("t_hi", [P, 2, S], F32R), sb("t_lo", [P, 2, S], F32R)
        probs = sb("probs", [P, 3, 512])
        probs_t = sb("probs_t", [P, PROBS_SLOTS, TB, S])
        v1 = [probs_t[:, PROBS_SLOTS - 1, 2 * s:2 * s + 2, :].rearrange("p a q -> p (a q)").rearrange(
            "p (b n) -> p b n", b=TB) for s in range(STREAMS)]
        sums = sb("sums", [P, QB, H])
        inv = sb("inv", [P, QB, 4])
        rinv = sb("rinv", [P, QB, P])
        nmax = sb("nmax", [P, H * QB])
        scale_t = sb("scale_t", [P, 2, S])
        q_mask = sb("q_mask", [P, 4, S], F32R)
        table_probe = sb("table_probe", [P, 1])

        raw_at, raw = 0, {}
        raw_tile = probs_t[:, :, :, :].rearrange("p a b c -> p (a b c)")
        for name, (hi, _) in split.items():
            rows, cols = hi.shape
            raw[name] = raw_tile[0:rows, raw_at:raw_at + cols]
            raw_at += cols
        wqt = [v[0][:, 0:PAIRS * D].rearrange("p (j n) -> p j n", j=PAIRS),
               v[0][:, 1024:1024 + PAIRS * D].rearrange("p (j n) -> p j n", j=PAIRS)]
        wkt = [v[0][:, 2048:2048 + PAIRS * D].rearrange("p (j n) -> p j n", j=PAIRS),
               v[0][:, 3072:3072 + PAIRS * C].rearrange("p (j n) -> p j n", j=PAIRS)]

        SC = [ps(f"scores{k}") for k in range(3)]
        PT = [ps("turned0"), ps("turned1")]
        O = ps("heads_out")
        X = ps("queries_m")
        Y = ps("chain_bank")

        sem = Semaphores(nc, ctx)
        segments_over = ctx.enter_context(nc.semaphore("segments_over"))

        def nth(name, s, n=1):
            return TOTAL.get(name, 1) * rank(s, CHAIN_OF[name]) + n

        def each_layer(s, chain):
            before = [key for key in ORDER if key[0] in ("mid1", "mid2", "mid3")]
            return before.index((chain, s)) + 1

        def heads4(ap):
            return ap.rearrange("p b (h c) -> p b h c", h=H)

        def three_products(out, a, b):
            (a_hi, a_lo), (b_hi, b_lo) = a, b
            nc.tensor.matmul(out, a_hi, b_hi, start=True, stop=False)
            nc.tensor.matmul(out, a_lo, b_hi, start=False, stop=False)
            return nc.tensor.matmul(out, a_hi, b_lo, start=False, stop=True)

        def probs_block(ph, k):
            kb, qb = (k // 2, k % 2) if ph.per_head == 1 else (k, 0)
            return slice(qb * S + kb * P, qb * S + (kb + 1) * P)

        def turned_place(ph, u):
            h, part = u // ph.per_head, u % ph.per_head
            if ph.per_head == 1:
                return probs_t[:, h % ph.slots, 0:2, :]
            return probs_t[:, h % ph.slots, :, part * P:(part + 1) * P]

        def turned_in_bank(ph, bank):
            return PT[bank][:, :].rearrange("p (k q) -> p k q", k=2 if ph.per_head == 1 else TB)

        def keys_in_bank(kb_count):
            return Y[:, :].rearrange("p (g k) -> p g k", g=1 if kb_count == TB else 2)

        def keys_turned(s, r, kb_count):
            return k_t[s][:, r:r + 1, :] if kb_count == TB else k_t[s][:, 2 * r:2 * r + 2, 0:S]

        CONSTANTS = [("ident", ident[:, :]), ("sum_rows", sum_rows[:, :]), ("rope_cos", rope_cos[:, :, :]),
                     ("rope_sin", rope_sin[:, :, :])]
        RAW = ([("wqt0", wqt[0]), ("wkt0", wkt[0]), ("wqt1", wqt[1]), ("wkt1", wkt[1])]
               + [(n, raw[n]) for n in ("wv1", "wv2", "wtext", "waudio", "wcaq", "wl3q", "wl3kv")]
               + [(n, raw["wsa"][:, k * D:(k + 1) * D]) for k, n in enumerate(("sawq", "sawk", "sawv"))]
               + [(n, raw["wcakv"][:, k * D:(k + 1) * D]) for k, n in enumerate(("cawk", "cawv"))])
        KEPT = ([("wo1", wo[0][:, :, :]), ("wo2", wo[1][:, :, :]), ("wff1", wff1[:, :]), ("wff2", wff2[:, :, :]),
                 ("wout1", wout1[:, :]), ("wmlp1", wmlp1[:, :]), ("wmlp2", wmlp2[:, :, :])]
                + [(n, t[:, :]) for n, t in cols_of.items()]
                + [(n, rows_of[n][:, :]) for n in rows_of if n not in ("bsa", "bcakv")]
                + [(n, rows_of["bsa"][:, k * D:(k + 1) * D]) for k, n in enumerate(("sabq", "sabk", "sabv"))]
                + [(n, rows_of["bcakv"][:, k * D:(k + 1) * D]) for k, n in enumerate(("cabk", "cabv"))])
        n_raw, n_kept = len(RAW) + len(CONSTANTS), len(KEPT)

        def setup_end(eng):
            eng.drain().then_inc(sem["setup_done"], 1)
            eng.wait_ge(sem["setup_done"], ENGINES)

        def segment_end(eng, ends):
            eng.drain().then_inc(sem["segment_done"], 1)
            eng.wait_ge(segments_over, ends)

        block = ctx.enter_context(nc.Block())

        @block.tensor
        def _(pe):
            pe.wait_ge(sem["raw_loaded"], 16 * n_raw)
            for fill in range(4):
                layer, half = fill // 2, fill % 2
                width = (D, C)[layer]
                for jj in range(4):
                    for i in range(2):
                        bank = (SC[0], SC[1], PT[0], PT[1], O, X, Y, SC[2])[2 * fill + i]
                        rows = slice(64 * i, 64 * i + 64)
                        last = nc.tensor.matmul(bank[:, jj * width:(jj + 1) * width],
                                                wqt[layer][rows, 4 * half + jj, :],
                                                wkt[layer][rows, 4 * half + jj, 0:width], start=True, stop=True)
                last.then_inc(sem["m_made"], 1)
            setup_end(pe)

            def transpose(out, in_):
                return nc.tensor.transpose(out, in_, ident[:, :])

            def fill_bank(key):
                if FILL[key] > 1:
                    pe.wait_ge(sem["bank_read"], FILL[key] - 1)

            def block_of(pair, k):
                cols = slice(k * P, (k + 1) * P)
                return pair[0][:, cols], pair[1][:, cols]

            def halves(name, cols=slice(None)):
                hi, lo = split[name]
                return hi[:, cols], lo[:, cols]

            def turn_tokens(key, src, blocks):
                fill_bank(key)
                for k in range(blocks):
                    last = transpose(Y[:, k * P:(k + 1) * P], src[:, k, :])
                last.then_inc(sem["bank_filled"], 1)

            def turn_normalised(chain, s, norm_name, content, blocks=QB):
                pe.wait_ge(sem["hat"], NORM[chain, s, norm_name])
                turn_tokens((chain, s, content), xhat, blocks)

            def values(chain, s, k, left, w):
                kb, half = k // 2, k % 2
                fill_bank((chain, s, f"v{k}"))
                three_products(Y[:, :], block_of(left, kb),
                               halves(w, slice(512 * half, 512 * half + 512))).then_inc(sem["bank_filled"], 1)

            def project_out(chain, s, content, blocks, left, weights, phase=None):
                fill_bank((chain, s, content))
                for qb in range(QB):
                    for j in range(blocks):
                        if phase and qb == 0:
                            pe.wait_ge(sem["attention_out_scaled"], PHASES[phase, s].at("out_scaled", j + 1))
                        last = nc.tensor.matmul(Y[:, qb * P:(qb + 1) * P], left[:, j, qb * P:(qb + 1) * P],
                                                weights(j), start=(j == 0), stop=(j == blocks - 1))
                last.then_inc(sem["bank_filled"], 1)

            def keys_values(chain, s, r, w):
                fill_bank((chain, s, f"kv{r}"))
                for k in range(2):
                    last = three_products(Y[:, k * 2 * D:(k + 1) * 2 * D],
                                          block_of((ctx_hi[s], ctx_lo[s]), 2 * r + k), halves(w))
                last.then_inc(sem["bank_filled"], 1)

            def queries(chain, s, w):
                fill_bank((chain, s, "q"))
                for qb in range(QB):
                    last = three_products(Y[:, qb * D:(qb + 1) * D], block_of((x_hi[s], x_lo[s]), qb), halves(w))
                last.then_inc(sem["bank_filled"], 1)

            def turn_stacks(chain, s, kb_count):
                pe.wait_ge(sem["stacked"], each_layer(s, chain))
                pe.wait_ge(sem["high"], each_layer(s, chain))
                for r in range(2):
                    yield f"qt{r}"
                    fill_bank((chain, s, f"qt{r}"))
                    for g in range(2):
                        for qb in range(QB):
                            last = transpose(Y[:, g * S + qb * P:g * S + (qb + 1) * P],
                                             q_stack[s][:, qb, 8 * r + 4 * g:8 * r + 4 * g + 4, :])
                    last.then_inc(sem["bank_filled"], 1)
                for r in range(kb_count):
                    yield f"kt{r}"
                    fill_bank((chain, s, f"kt{r}"))
                    for k in range(4):
                        quad, kb = (r, k) if kb_count == TB else (2 * r + k // 2, k % 2)
                        last = transpose(Y[:, k * P:(k + 1) * P], k_stack[s][:, kb, 4 * quad:4 * quad + 4, :])
                    last.then_inc(sem["bank_filled"], 1)

            def chain(name, s):
                xs, cs = (x_hi[s], x_lo[s]), (ctx_hi[s], ctx_lo[s])
                if name == "start":
                    yield "ctx"
                    pe.wait_ge(sem[f"ctx_loaded{s}"], 16)
                    fill_bank((name, s, "ctx"))
                    for kb in range(TB):
                        last = transpose(Y[0:C, kb * P:(kb + 1) * P], ctx_nat[s][:, kb, :])
                    last.then_inc(sem["bank_filled"], 1)
                    yield "ln1"
                    turn_normalised(name, s, "ln1", "ln1")
                    for k in range(4):
                        yield f"v{k}"
                        pe.wait_ge(sem["split"], SPLIT[name, s, "ln1"])
                        values(name, s, k, xs, "wv1")
                elif name == "mid0":
                    yield "audio"
                    fill_bank((name, s, "audio"))
                    for kb in range(TB):
                        last = three_products(Y[:, kb * D:(kb + 1) * D], block_of(cs, kb), halves("waudio"))
                    last.then_inc(sem["bank_filled"], 1)
                    yield "wo"
                    project_out(name, s, "wo", PAIRS, out_t[s], lambda j: wo[0][:, j, :], "self0")
                    yield "v0"
                    values(name, s, 0, cs, "wv2")
                    yield "ln2"
                    turn_normalised(name, s, "ln2", "ln2")
                    for k in range(1, 8):
                        if k == 4:
                            yield "audio_t"
                            turn_normalised(name, s, "audio", "audio_t", TB)
                        yield f"v{k}"
                        values(name, s, k, cs, "wv2")
                elif name == "mid1":
                    yield "wo"
                    project_out(name, s, "wo", PAIRS, out_t[s], lambda j: wo[1][:, j, :], "cross0")
                    yield "ln3"
                    turn_normalised(name, s, "ln3", "ln3")
                    for part, at in (("g", FF), ("l", 0)):
                        for r in range(2):
                            if part == "l" or r == 0:
                                yield f"l{r}" if part == "l" else "gate"
                            fill_bank((name, s, f"{part}{r}"))
                            for k in range(2):
                                cols = slice(at + (2 * r + k) * P, at + (2 * r + k + 1) * P)
                                last = nc.tensor.matmul(Y[:, k * S:(k + 1) * S], wff1[:, cols], xz[:, 0:S],
                                                        start=True, stop=True)
                            last.then_inc(sem["bank_filled"], 1)
                    yield "down"
                    project_out(name, s, "down", 4, hidden[s], lambda j: wff2[:, j, :])
                    yield "x1_t"
                    turn_tokens((name, s, "x1_t"), x[s], QB)
                    yield "text"
                    fill_bank((name, s, "text"))
                    for qb in range(QB):
                        last = three_products(Y[:, qb * P:(qb + 1) * P], block_of(xs, qb), halves("wtext"))
                    last.then_inc(sem["bank_filled"], 1)
                    yield "text_t"
                    turn_normalised(name, s, "text", "text_t")
                    for qb in range(QB):
                        yield f"s{qb}"
                        pe.wait_ge(sem["split"], SPLIT[name, s, "text"])
                        fill_bank((name, s, f"s{qb}"))
                        three_products(Y[:, :], block_of(xs, qb), (k1_hi[s], k1_lo[s])
                                       ).then_inc(sem["bank_filled"], 1)
                    for qb in range(QB):
                        yield f"p{qb}"
                        fill_bank((name, s, f"p{qb}"))
                        for kb in range(TB):
                            last = transpose(Y[:, kb * P:(kb + 1) * P], probs1[s][:, qb, kb * P:(kb + 1) * P])
                        last.then_inc(sem["bank_filled"], 1)
                    yield "pv"
                    fill_bank((name, s, "pv"))
                    for kb in range(TB):
                        nc.tensor.matmul(Y[:, 0:S], v1[s][:, kb, :], probs1_t[s][:, kb, :],
                                         start=(kb == 0), stop=(kb == TB - 1))
                    pe.wait_ge(sem["l1_rinv"], nth("l1_rinv", s))
                    for qb in range(QB):
                        last = transpose(Y[:, S + qb * P:S + (qb + 1) * P], l1_rinv[s][:, qb, :])
                    last.then_inc(sem["bank_filled"], 1)
                    yield "wout"
                    project_out(name, s, "wout", 1, out_t[s], lambda j: wout1[:, :])
                    yield "m1_t"
                    turn_normalised(name, s, "m1", "m1_t")
                    for qb in range(QB):
                        yield f"qkv{qb}"
                        pe.wait_ge(sem["split"], SPLIT[name, s, "m1"])
                        fill_bank((name, s, f"qkv{qb}"))
                        three_products(Y[:, 0:3 * D], block_of(xs, qb), halves("wsa")
                                       ).then_inc(sem["bank_filled"], 1)
                    yield "low"
                    yield from turn_stacks(name, s, QB)
                elif name == "mid2":
                    yield "wo"
                    project_out(name, s, "wo", QUADS, out_t[s], lambda j: wo_pad[0][:, j, :], "self2")
                    for r in range(2):
                        yield f"kv{r}"
                        keys_values(name, s, r, "wcakv")
                    yield "m2_t"
                    turn_normalised(name, s, "m2", "m2_t")
                    yield "q"
                    pe.wait_ge(sem["split"], SPLIT[name, s, "m2"])
                    queries(name, s, "wcaq")
                    yield "low"
                    yield from turn_stacks(name, s, TB)
                elif name == "mid3":
                    yield "wo"
                    project_out(name, s, "wo", QUADS, out_t[s], lambda j: wo_pad[1][:, j, :], "cross2")
                    yield "m3_t"
                    turn_normalised(name, s, "m3", "m3_t")
                    yield "up"
                    for r in range(2):
                        fill_bank((name, s, f"up{r}"))
                        for k in range(2):
                            last = nc.tensor.matmul(Y[:, k * S:(k + 1) * S],
                                                    wmlp1[:, (2 * r + k) * P:(2 * r + k + 1) * P], xz[:, 0:S],
                                                    start=True, stop=True)
                        last.then_inc(sem["bank_filled"], 1)
                    yield "down"
                    project_out(name, s, "down", 4, hidden[s], lambda j: wmlp2[:, j, :])
                    for r in range(2):
                        yield f"kv{r}"
                        keys_values(name, s, r, "wl3kv")
                    yield "rms_t"
                    turn_normalised(name, s, "rms", "rms_t")
                    yield "q"
                    pe.wait_ge(sem["split"], SPLIT[name, s, "rms"])
                    queries(name, s, "wl3q")
                    yield "low"
                    yield from turn_stacks(name, s, TB)
                else:
                    yield "wo"
                    project_out(name, s, "wo", QUADS, out_t[s], lambda j: wo_pad[2][:, j, :], "l3")

            def queries_times_m(ph, h):
                layer = 0 if ph.name == "self0" else 1
                if ph.at("t_lo", h) > 0:
                    pe.wait_ge(sem["attention_t_lo"], ph.at("t_lo", h))
                three_products(X[0:ph.t_rows, 0:S], (m_hi[layer][:, h, :], m_lo[layer][:, h, :]),
                               (x_hi[ph.s][:, :], x_lo[ph.s][:, :])).then_inc(sem["attention_t"], 1)

            def scores(ph, u):
                h, part, s = u // ph.per_head, u % ph.per_head, ph.s
                if ph.at("exp", u - 2) > 0:
                    pe.wait_ge(sem["attention_exp"], ph.at("exp", u - 2))
                if ph.masked:
                    pe.wait_ge(sem["attention_mask"], ph.at("mask", h + 1))
                else:
                    pe.wait_ge(sem["attention_t_lo"], ph.at("t_lo", h + 1))
                bank = SC[ph.at("scores", u) % 3]
                if ph.key_major:
                    for k in range(2):
                        kb = 2 * part + k
                        last = nc.tensor.matmul(bank[:, k * S:(k + 1) * S], k_t[s][:, h // 4, kb * P:(kb + 1) * P],
                                                q_mask[:, h % 4, :], start=True, stop=True)
                else:
                    for k, qb in enumerate(range(QB) if ph.per_head == 1 else (part,)):
                        out, q = bank[:, k * S:k * S + ph.keys], slice(qb * P, (qb + 1) * P)
                        if ph.masked:
                            last = nc.tensor.matmul(out, q_mask[:, h % 4, q], k_t[s][:, h // 4, 0:ph.keys],
                                                    start=True, stop=True)
                        else:
                            right = (x_hi[s], x_lo[s]) if ph.name == "self0" else (ctx_hi[s], ctx_lo[s])
                            last = three_products(out, (t_hi[0:ph.t_rows, h % 2, q], t_lo[0:ph.t_rows, h % 2, q]),
                                                  (right[0][:, :], right[1][:, :]))
                last.then_inc(sem["attention_scores"], 1)

            def turn_probs(ph, u):
                pe.wait_ge(sem["attention_exp"], ph.at("exp", u + 1))
                n = ph.at("turned", u)
                if n >= 2:
                    pe.wait_ge(sem[f"attention_copied{n % 2}"], n // 2)
                for k in range(4):
                    last = transpose(PT[n % 2][:, k * P:(k + 1) * P],
                                     probs[:, n % 3, probs_block(ph, k)])
                last.then_inc(sem["attention_turned"], 1)

            def head_outputs(ph, g):
                s, w = ph.s, ph.rows
                n = (g + 1) * ph.group * ph.per_head
                if ph.key_major:
                    pe.wait_ge(sem["attention_exp"], ph.at("exp", n))
                else:
                    pe.wait_ge(sem["attention_copied0"], ph.at("copied0", n // 2))
                    pe.wait_ge(sem["attention_copied1"], ph.at("copied1", n // 2))
                if ph.at("out_scaled", g) > 0:
                    pe.wait_ge(sem["attention_out_scaled"], ph.at("out_scaled", g))
                for kb in range(ph.kb):
                    for i in range(ph.group):
                        h = g * ph.group + i
                        stationary = v_pad[s][:, kb, h, :] if ph.masked else v0[s][:, kb, h * E0:(h + 1) * E0]
                        last = nc.tensor.matmul(O[w * i:w * i + w, 0:S], stationary,
                                                probs_t[:, h % ph.slots, kb, :], start=(kb == 0),
                                                stop=(kb == ph.kb - 1))
                if not ph.key_major:
                    pe.wait_ge(sem["attention_rinv"], ph.at("rinv", g + 1))
                    for qb in range(QB):
                        last = transpose(O[:, S + qb * P:S + (qb + 1) * P], rinv[:, qb, :])
                last.then_inc(sem["attention_heads"], 1)

            def quad_sums(ph, g):
                pe.wait_ge(sem["l3_heads_copied"], nth("l3_heads_copied", ph.s, g + 1))
                nc.tensor.matmul(O[:, S:2 * S], sum_rows[:, :], scale_t[:, g % 2, :], start=True,
                                 stop=True).then_inc(sem["attention_scale"], 1)

            def attention(ph):
                chain, content = {"self0": ("start", "v3"), "cross0": ("mid0", "v7"), "self2": ("mid1", "kt1"),
                                  "cross2": ("mid2", "kt3"), "l3": ("mid3", "kt3")}[ph.name]
                if precedes((chain, ph.s), (ph.name, ph.s)):
                    pe.wait_ge(sem["bank_read"], FILL[chain, ph.s, content])
                    if ph.name == "cross0":
                        pe.wait_ge(sem["split"], SPLIT["mid0", ph.s, "audio"])
                    if ph.masked:
                        pe.wait_ge(sem["v_padded"], each_layer(ph.s, chain))
                if ph.t_rows:
                    queries_times_m(ph, 0)
                    queries_times_m(ph, 1)
                scores(ph, 0)
                scores(ph, 1)
                for h in early_t(ph):
                    queries_times_m(ph, h)
                for u in range(ph.units):
                    if u + 2 < ph.units:
                        scores(ph, u + 2)
                    if not ph.key_major:
                        turn_probs(ph, u)
                    if next_t(ph, u):
                        queries_times_m(ph, next_t(ph, u))
                    g = ph.ends_group(u)
                    if g is not None:
                        head_outputs(ph, g)
                    if ph.key_major and ph.ends_group(u - 2) is not None:
                        quad_sums(ph, ph.ends_group(u - 2))
                    if u == ph.units - 1:
                        head_outputs(ph, ph.groups - 1)
                        if ph.key_major:
                            quad_sums(ph, ph.groups - 1)
                    yield

            def segment(name, ends):
                enter(name)
                run_rounds(name, attention, chain)
                segment_end(pe, ends)

            segment("first", 1)
            with pe.Fori(0, LOOPS) as b:
                segment("loop", b + 2)
            segment("last", LOOPS + 2)

        @block.scalar
        def _(act):
            def copy(out, in_, scale=1.0):
                return nc.scalar.activation(out, in_, ACT.Copy, scale=scale)

            act.wait_ge(sem["raw_loaded"], 16 * n_raw)
            act.wait_ge(sem["raw_scaled"], 1)
            for name in split:
                copy(split[name][0][:, :], raw[name]).then_inc(sem["w_hi"], 1)
            for fill in range(4):
                layer, half = fill // 2, fill % 2
                width = (D, C)[layer]
                act.wait_ge(sem["m_made"], fill + 1)
                for i in range(2):
                    bank = (SC[0], SC[1], PT[0], PT[1], O, X, Y, SC[2])[2 * fill + i]
                    out = m_hi[layer][:, :, :].rearrange("p (j i) n -> p j i n", i=2)[:, 4 * half:4 * half + 4, i, :]
                    copy(out, bank[:, 0:4 * width].rearrange("p (j n) -> p j n", j=4),
                         scale=E0 ** -0.5).then_inc(sem["m_hi"], 1)
            setup_end(act)

            def affine(chain, s, norm_name, content, g, beta, cols=S):
                act.wait_ge(sem["bank_filled"], FILL[chain, s, content])
                nc.scalar.activation(xz[:, 0:cols], Y[:, 0:cols], ACT.Identity,
                                     bias=cols_of[beta][:, 0:1] if beta else 0.0,
                                     scale=cols_of[g][:, 0:1]).then_inc(sem["bank_read"], 1)

            def value_copy(chain, s, k):
                act.wait_ge(sem["bank_filled"], FILL[chain, s, f"v{k}"])
                copy(v0[s][:, k // 2, 512 * (k % 2):512 * (k % 2) + 512], Y[:, :]).then_inc(sem["bank_read"], 1)

            def stack_high(chain, s, kb_count):
                act.wait_ge(sem["natural"], each_layer(s, chain))
                copy(f32r(q_stack[s][:, :, :, 0:8]), heads4(nat_q[:, :, :]))
                keys = heads4(nat_kv[:, 0:kb_count, 0:D])
                copy(f32r(k_stack[s][:, 0:kb_count, :, 0:8]), keys).then_inc(sem["high_once"], 1)
                copy(f32r(q_stack[s][:, :, :, 8:16]), heads4(nat_q[:, :, :]))
                copy(f32r(k_stack[s][:, 0:kb_count, :, 16:24]), keys).then_inc(sem["high"], 1)
                if chain == "mid1":
                    act.wait_ge(sem["pads"], nth("pads", s, 2))
                copy(v_pad[s][:, 0:kb_count, :, 0:8],
                     heads4(nat_kv[:, 0:kb_count, D:2 * D])).then_inc(sem["v_padded"], 1)

            def turned_stacks(chain, s, kb_count):
                yield "qt0"
                act.wait_ge(sem["bank_filled"], FILL[chain, s, "qt0"])
                copy(q_t[s][:, 0:2, :], Y[:, :].rearrange("p (g q) -> p g q", g=2)).then_inc(sem["bank_read"], 1)
                for r in range(0, kb_count, 2):
                    yield f"kt{r}"
                    act.wait_ge(sem["bank_filled"], FILL[chain, s, f"kt{r}"])
                    copy(keys_turned(s, r, kb_count), keys_in_bank(kb_count)).then_inc(sem["bank_read"], 1)

            def table_for(func):
                nc.scalar.activation(table_probe[:, :], ident[:, 0:1], func)

            def chain(name, s):
                if name == "start":
                    yield "ctx"
                    act.wait_ge(sem["bank_filled"], FILL[name, s, "ctx"])
                    copy(ctx_hi[s][:, :], Y[0:C, :]).then_inc(sem["ctx_high"], 1)
                    yield "ln1"
                    affine(name, s, "ln1", "ln1", "ln1g", "ln1b")
                    for k in (0, 2):
                        yield f"v{k}"
                        value_copy(name, s, k)
                elif name == "mid0":
                    yield "v0"
                    value_copy(name, s, 0)
                    yield "ln2"
                    affine(name, s, "ln2", "ln2", "ln2g", "ln2b")
                    for k in (2, 4, 6):
                        if k == 4:
                            yield "audio_t"
                            affine(name, s, "audio", "audio_t", "g2", "beta2", cols=T)
                        yield f"v{k}"
                        value_copy(name, s, k)
                elif name == "mid1":
                    yield "ln3"
                    affine(name, s, "ln3", "ln3", "ln3g", "ln3b")
                    yield "gate"
                    table_for(ACT.Gelu_apprx_tanh)
                    for r in range(2):
                        act.wait_ge(sem["bank_filled"], FILL[name, s, f"g{r}"])
                        for k in range(2):
                            j = 2 * r + k
                            last = nc.scalar.activation(hidden[s][:, j, :], Y[:, k * S:(k + 1) * S],
                                                        ACT.Gelu_apprx_tanh, bias=cols_of["bff1"][:, 4 + j:5 + j])
                        last.then_inc(sem["bank_read"], 1)
                    table_for(ACT.Exp)
                    yield "x1_t"
                    act.wait_ge(sem["bank_filled"], FILL[name, s, "x1_t"])
                    copy(x_hi[s][:, :], Y[:, 0:S]).then_inc(sem["x1_high"], 1)
                    yield "text_t"
                    affine(name, s, "text", "text_t", "g1", "beta1")
                    for qb in range(QB):
                        yield f"e{qb}"
                        act.wait_ge(sem["l1_max"], nth("l1_max", s, qb + 1))
                        nc.scalar.activation(probs1[s][:, qb, :], Y[:, :], ACT.Exp, bias=l1_nmax[:, qb:qb + 1],
                                             accum_out=l1_sums[:, qb:qb + 1]).then_inc(sem["bank_read"], 1)
                    yield "p0"
                    act.wait_ge(sem["bank_filled"], FILL[name, s, "p0"])
                    copy(probs1_t[s][:, :, 0:P], Y[:, :].rearrange("p (k q) -> p k q", k=TB)
                         ).then_inc(sem["bank_read"], 1)
                    yield "sc"
                    act.wait_ge(sem["bank_filled"], FILL[name, s, "pv"])
                    copy(l1_scale[s], Y[:, S:2 * S]).then_inc(sem["l1_scale"], 1)
                    yield "m1_t"
                    affine(name, s, "m1", "m1_t", "m1g", "m1b")
                    yield "high"
                    stack_high(name, s, QB)
                    yield from turned_stacks(name, s, QB)
                elif name == "mid2":
                    yield "m2_t"
                    affine(name, s, "m2", "m2_t", "m2g", "m2b")
                    yield "high"
                    stack_high(name, s, TB)
                    yield from turned_stacks(name, s, TB)
                elif name == "mid3":
                    yield "m3_t"
                    affine(name, s, "m3", "m3_t", "m3g", "m3b")
                    yield "up"
                    table_for(ACT.Gelu)
                    for r in range(2):
                        act.wait_ge(sem["bank_filled"], FILL[name, s, f"up{r}"])
                        for k in range(2):
                            j = 2 * r + k
                            last = nc.scalar.activation(hidden[s][:, j, :], Y[:, k * S:(k + 1) * S], ACT.Gelu,
                                                        bias=cols_of["bmlp1"][:, j:j + 1])
                        last.then_inc(sem["bank_read"], 1)
                    table_for(ACT.Exp)
                    yield "rms_t"
                    affine(name, s, "rms", "rms_t", "normw", None)
                    yield "root"
                    act.wait_ge(sem["squares"], nth("squares", s))
                    nc.scalar.activation(norm[:, :, :], ss[:, :, :], ACT.Sqrt).then_inc(sem["root"], 1)
                    table_for(ACT.Exp)
                    yield "high"
                    stack_high(name, s, TB)
                    yield from turned_stacks(name, s, TB)

            def t_high(ph, h):
                act.wait_ge(sem["attention_t"], ph.at("t", h + 1))
                if h >= 2:
                    act.wait_ge(sem["attention_scores"], ph.at("scores", (h - 1) * ph.per_head))
                copy(t_hi[0:ph.t_rows, h % 2, :], X[0:ph.t_rows, 0:S]).then_inc(sem["attention_t_hi"], 1)

            def exps(ph, u):
                h, part, n = u // ph.per_head, u % ph.per_head, ph.at("turned", u)
                bank = SC[ph.at("scores", u) % 3]
                if ph.key_major:
                    act.wait_ge(sem["attention_scores"], ph.at("scores", u + 1))
                    if h >= ph.slots:
                        act.wait_ge(sem["attention_heads"], ph.at("heads", (h - ph.slots) // ph.group + 1))
                    nc.scalar.activation(probs_t[:, h % ph.slots, 2 * part:2 * part + 2, :],
                                         bank[:, :].rearrange("p (k q) -> p k q", k=2), ACT.Exp,
                                         scale=float(np.sqrt(np.float32(E2)))).then_inc(sem["attention_exp"], 1)
                    return
                act.wait_ge(sem["attention_max"], ph.at("max", u + 1))
                if ph.at("turned", u) >= 3:
                    act.wait_ge(sem["attention_turned"], ph.at("turned", u - 2))
                for k, qb in enumerate(range(QB) if ph.per_head == 1 else (part,)):
                    last = nc.scalar.activation(probs[:, n % 3, k * S:k * S + ph.keys],
                                                bank[:, k * S:k * S + ph.keys], ACT.Exp,
                                                bias=nmax[:, h * QB + qb:h * QB + qb + 1],
                                                accum_out=sums[:, qb, h:h + 1])
                last.then_inc(sem["attention_exp"], 1)

            def turned_copy(ph, u):
                h = u // ph.per_head
                act.wait_ge(sem["attention_turned"], ph.at("turned", u + 1))
                if h >= ph.slots:
                    act.wait_ge(sem["attention_heads"], ph.at("heads", (h - ph.slots) // ph.group + 1))
                copy(turned_place(ph, u), turned_in_bank(ph, 0)).then_inc(sem["attention_copied0"], 1)

            def scale_copy(ph, g):
                act.wait_ge(sem["attention_heads"], ph.at("heads", g + 1))
                if ph.at("out_scaled", g - 1) > 0:
                    act.wait_ge(sem["attention_out_scaled"], ph.at("out_scaled", g - 1))
                copy(scale_t[:, g % 2, :], O[:, S:2 * S]).then_inc(sem["attention_scale"], 1)

            def attention(ph):
                if ph.t_rows:
                    t_high(ph, 0)
                    t_high(ph, 1)
                exps(ph, 0)
                for h in early_t(ph):
                    t_high(ph, h)
                for u in range(ph.units):
                    if u + 1 < ph.units:
                        exps(ph, u + 1)
                    if not ph.key_major and u % 2 == 0:
                        turned_copy(ph, u)
                    if next_t(ph, u):
                        t_high(ph, next_t(ph, u))
                    g = ph.ends_group(u)
                    if g is not None and not ph.key_major:
                        scale_copy(ph, g)
                    if u == ph.units - 1 and not ph.key_major:
                        scale_copy(ph, ph.groups - 1)
                    yield

            def segment(name, ends):
                enter(name)
                run_rounds(name, attention, chain)
                segment_end(act, ends)

            segment("first", 1)
            with act.Fori(0, LOOPS) as b:
                segment("loop", b + 2)
            segment("last", LOOPS + 2)

        @block.vector
        def _(dve):
            chained = {"setup_chain": 0, "segment_chain": 0}

            def then(ins, name="segment_chain"):
                ins.then_inc(sem[name], 1)
                chained[name] += 1
                dve.wait_ge(sem[name], chained[name])

            def low_part(out, full, high):
                return nc.vector.tensor_tensor(out, full, f32(high), ALU.subtract)

            dve.wait_ge(sem["raw_loaded"], 16 * n_raw)
            q_scale = float(E2) ** -0.5
            then(nc.vector.tensor_scalar(raw["wsa"][:, 0:D], raw["wsa"][:, 0:D], q_scale, None, ALU.mult),
                 "setup_chain")
            nc.vector.tensor_scalar(raw["wcaq"], raw["wcaq"], q_scale, None, ALU.mult).then_inc(sem["raw_scaled"], 1)
            dve.wait_ge(sem["raw_scaled"], 1)
            for n, name in enumerate(split):
                dve.wait_ge(sem["w_hi"], n + 1)
                low_part(split[name][1][:, :], raw[name], split[name][0][:, :]).then_inc(sem["w_lo"], 1)
            for fill in range(4):
                layer, half = fill // 2, fill % 2
                width = (D, C)[layer]
                dve.wait_ge(sem["m_hi"], 2 * fill + 2)
                for i in range(2):
                    bank = (SC[0], SC[1], PT[0], PT[1], O, X, Y, SC[2])[2 * fill + i]
                    view = lambda m: m[:, :, :].rearrange("p (j i) n -> p j i n", i=2)[:, 4 * half:4 * half + 4, i, :]
                    src = bank[:, 0:4 * width].rearrange("p (j n) -> p j n", j=4)
                    nc.vector.scalar_tensor_tensor(view(m_lo[layer]), src, E0 ** -0.5, f32(view(m_hi[layer])),
                                                   op0=ALU.mult, op1=ALU.subtract).then_inc(sem["m_split"], 1)
            dve.wait_ge(sem["kept_loaded"], 16 * n_kept)
            for tile in (rows_of["bsa"][:, 0:D], rows_of["bcaq"][:, :]):
                then(nc.vector.tensor_scalar(tile, tile, q_scale, None, ALU.mult), "setup_chain")
            for name in ("g1", "beta1"):
                then(nc.vector.tensor_scalar(cols_of[name][:, :], cols_of[name][:, :], float(D) ** -0.5, None,
                                             ALU.mult), "setup_chain")
            setup_end(dve)

            def in_bank(blocks):
                return Y[:, 0:blocks * D].rearrange("p (b n) -> p b n", b=blocks)

            def statistics(src, blocks):
                for k in range(blocks):
                    last = nc.vector.bn_stats(stats[:, k, :], src[:, k, :])
                then(last)
                for k in range(blocks):
                    last = nc.vector.bn_aggr(moments[:, k, :], stats[:, k, :])
                then(last)
                nc.vector.tensor_scalar(var_eps[:, 0:blocks], moments[:, 0:blocks, 1], EPS, None,
                                        ALU.add).then_inc(sem["var"], 1)

            def normalised(key, src, blocks=QB):
                dve.wait_ge(sem["rstd"], NORM[key])
                for k in range(blocks):
                    last = nc.vector.tensor_scalar(xhat[:, k, :], src[:, k, :], moments[:, k, 0:1], rstd[:, k:k + 1],
                                                   ALU.subtract, ALU.mult)
                last.then_inc(sem["hat"], 1)
                dve.wait_ge(sem["hat"], NORM[key])

            def split_x(chain, s, norm_name, content, hi=None, lo=None, cols=S):
                hi, lo = (x_hi[s][:, :], x_lo[s][:, :]) if hi is None else (hi, lo)
                dve.wait_ge(sem["bank_read"], FILL[chain, s, content])
                then(nc.vector.tensor_copy(hi, xz[:, 0:cols]))
                low_part(lo, xz[:, 0:cols], hi).then_inc(sem["split"], 1)

            def row(name, blocks, cols=slice(None)):
                r = rows_of[name][:, cols].unsqueeze(1)
                return r.to_broadcast([P, blocks, r.shape[2]])

            def add_row(s, name):
                then(nc.vector.tensor_tensor(x[s][:, :, :], x[s][:, :, :], row(name, QB), ALU.add))

            def add_projected(chain, s, content):
                dve.wait_ge(sem["bank_filled"], FILL[chain, s, content])
                nc.vector.tensor_tensor(x[s][:, :, :], in_bank(QB), x[s][:, :, :], ALU.add
                                        ).then_inc(sem["bank_read"], 1)
                dve.wait_ge(sem["bank_read"], FILL[chain, s, content])

            def value_copy(chain, s, k):
                dve.wait_ge(sem["bank_filled"], FILL[chain, s, f"v{k}"])
                nc.vector.tensor_copy(v0[s][:, k // 2, 512 * (k % 2):512 * (k % 2) + 512], Y[:, :]
                                      ).then_inc(sem["bank_read"], 1)

            def stack_low(chain, s, kb_count):
                if chain != "mid2":
                    nc.vector.memset(q_stack[s][:, :, :, 24:32], 0.0)
                dve.wait_ge(sem["high_once"], each_layer(s, chain))
                nc.vector.tensor_tensor(f32r(q_stack[s][:, :, :, 16:24]), heads4(nat_q[:, :, :]),
                                        q_stack[s][:, :, :, 0:8], ALU.subtract)
                nc.vector.tensor_tensor(f32r(k_stack[s][:, 0:kb_count, :, 8:16]), heads4(nat_kv[:, 0:kb_count, 0:D]),
                                        k_stack[s][:, 0:kb_count, :, 0:8], ALU.subtract).then_inc(sem["stacked"], 1)

            def turned_stacks(chain, s, kb_count):
                yield "qt1"
                dve.wait_ge(sem["bank_filled"], FILL[chain, s, "qt1"])
                nc.vector.tensor_copy(q_t[s][:, 2:4, :], Y[:, :].rearrange("p (g q) -> p g q", g=2)
                                      ).then_inc(sem["bank_read"], 1)
                for r in range(1, kb_count, 2):
                    yield f"kt{r}"
                    dve.wait_ge(sem["bank_filled"], FILL[chain, s, f"kt{r}"])
                    nc.vector.tensor_copy(keys_turned(s, r, kb_count), keys_in_bank(kb_count)
                                          ).then_inc(sem["bank_read"], 1)

            def rotate(s, y4, blocks, at):
                cos = rope_cos[:, 0:blocks, :].unsqueeze(2).to_broadcast([P, blocks, H, E2])
                sin = rope_sin[:, 0:blocks, :].unsqueeze(2).to_broadcast([P, blocks, H, E2])
                tmp, prod = rope_tmp[s][:, 0:blocks], rope_prod[s][:, 0:blocks]
                half = E2 // 2
                nc.vector.tensor_tensor(tmp[:, :, :, 0:half], y4[:, :, :, half:E2], sin[:, :, :, 0:half], ALU.mult)
                nc.vector.tensor_tensor(tmp[:, :, :, half:E2], y4[:, :, :, 0:half], sin[:, :, :, half:E2], ALU.mult)
                then(nc.vector.tensor_tensor(prod, y4, cos, ALU.mult))
                then(nc.vector.tensor_tensor(y4, tmp, prod, ALU.add))
                then(nc.vector.tensor_tensor(prod, y4, y4, ALU.mult))
                then(nc.vector.tensor_reduce(ss[:, at:at + blocks, :], prod, AX.X, ALU.add))

            def chain(name, s):
                xs = x[s]
                if name == "start":
                    yield "ctx"
                    dve.wait_ge(sem["ctx_high"], nth("ctx_high", s))
                    low_part(ctx_lo[s][:, :], Y[0:C, :], ctx_hi[s][:, :]).then_inc(sem["bank_read"], 1)
                    yield "stats"
                    dve.wait_ge(sem[f"x_loaded{s}"], 16)
                    statistics(xs, QB)
                    yield "hat"
                    normalised((name, s, "ln1"), xs)
                    add_row(s, "bo1")
                    yield "split"
                    split_x(name, s, "ln1", "ln1")
                    for k in (1, 3):
                        yield f"v{k}"
                        value_copy(name, s, k)
                elif name == "mid0":
                    yield "audio"
                    dve.wait_ge(sem["bank_filled"], FILL[name, s, "audio"])
                    nc.vector.tensor_tensor(v1[s], in_bank(TB), row("baudio", TB), ALU.add
                                            ).then_inc(sem["bank_read"], 1)
                    dve.wait_ge(sem["bank_read"], FILL[name, s, "audio"])
                    yield "wo"
                    add_projected(name, s, "wo")
                    yield "stats"
                    statistics(xs, QB)
                    yield "hat"
                    normalised((name, s, "ln2"), xs)
                    add_row(s, "bo2")
                    yield "astats"
                    statistics(v1[s], TB)
                    yield "v1"
                    value_copy(name, s, 1)
                    yield "split"
                    split_x(name, s, "ln2", "ln2")
                    yield "ahat"
                    normalised((name, s, "audio"), v1[s], TB)
                    yield "v3"
                    value_copy(name, s, 3)
                    yield "asplit"
                    split_x(name, s, "audio", "audio_t", k1_hi[s], k1_lo[s], T)
                    for k in (5, 7):
                        yield f"v{k}"
                        value_copy(name, s, k)
                elif name == "mid1":
                    yield "wo"
                    add_projected(name, s, "wo")
                    yield "stats"
                    statistics(xs, QB)
                    yield "hat"
                    normalised((name, s, "ln3"), xs)
                    add_row(s, "bff2")
                    for r in range(2):
                        yield f"l{r}"
                        dve.wait_ge(sem["bank_filled"], FILL[name, s, f"l{r}"])
                        for k in range(2):
                            j = 2 * r + k
                            last = nc.vector.scalar_tensor_tensor(
                                hidden[s][:, j, :], Y[:, k * S:(k + 1) * S], cols_of["bff1"][:, j:j + 1],
                                hidden[s][:, j, :], op0=ALU.add, op1=ALU.mult)
                        last.then_inc(sem["bank_read"], 1)
                    yield "down"
                    add_projected(name, s, "down")
                    yield "x1_lo"
                    dve.wait_ge(sem["x1_high"], nth("x1_high", s))
                    low_part(x_lo[s][:, :], Y[:, 0:S], x_hi[s][:, :]).then_inc(sem["bank_read"], 1)
                    yield "tstats"
                    dve.wait_ge(sem["bank_filled"], FILL[name, s, "text"])
                    nc.vector.tensor_tensor(nat_q[:, :, :], in_bank(QB), row("btext", QB), ALU.add
                                            ).then_inc(sem["bank_read"], 1)
                    dve.wait_ge(sem["bank_read"], FILL[name, s, "text"])
                    statistics(nat_q, QB)
                    yield "that"
                    normalised((name, s, "text"), nat_q)
                    add_row(s, "bout")
                    yield "tsplit"
                    split_x(name, s, "text", "text_t")
                    for qb in range(QB):
                        yield f"s{qb}"
                        dve.wait_ge(sem["bank_filled"], FILL[name, s, f"s{qb}"])
                        nc.vector.tensor_reduce(l1_nmax[:, qb:qb + 1], Y[:, :], AX.X, ALU.max,
                                                negate=True).then_inc(sem["l1_max"], 1)
                    yield "p1"
                    dve.wait_ge(sem["bank_read"], FILL[name, s, "s1"])
                    then(nc.vector.reciprocal(l1_sums[:, :], l1_sums[:, :]))
                    nc.vector.tensor_copy(l1_rinv[s], l1_sums[:, :].unsqueeze(2).to_broadcast([P, QB, P])
                                          ).then_inc(sem["l1_rinv"], 1)
                    dve.wait_ge(sem["bank_filled"], FILL[name, s, "p1"])
                    nc.vector.tensor_copy(probs1_t[s][:, :, P:2 * P], Y[:, :].rearrange("p (k q) -> p k q", k=TB)
                                          ).then_inc(sem["bank_read"], 1)
                    yield "sc"
                    dve.wait_ge(sem["l1_scale"], nth("l1_scale", s))
                    nc.vector.tensor_tensor(out_t[s][:, 0, :], Y[:, 0:S], l1_scale[s], ALU.mult
                                            ).then_inc(sem["bank_read"], 1)
                    yield "wout"
                    add_projected(name, s, "wout")
                    yield "ostats"
                    statistics(xs, QB)
                    yield "ohat"
                    normalised((name, s, "out1"), xs)
                    then(nc.vector.tensor_tensor(xs[:, :, :], xhat[:, 0:QB, :], row("gout", QB), ALU.mult))
                    add_row(s, "betaout")
                    yield "mstats"
                    statistics(xs, QB)
                    yield "mhat"
                    normalised((name, s, "m1"), xs)
                    add_row(s, "bosa")
                    yield "msplit"
                    split_x(name, s, "m1", "m1_t")
                    for qb in range(QB):
                        yield f"qkv{qb}"
                        dve.wait_ge(sem["bank_filled"], FILL[name, s, f"qkv{qb}"])
                        nc.vector.tensor_tensor(nat_q[:, qb, :], Y[:, 0:D], rows_of["bsa"][:, 0:D], ALU.add)
                        nc.vector.tensor_tensor(nat_kv[:, qb, :], Y[:, D:3 * D], rows_of["bsa"][:, D:3 * D], ALU.add
                                                ).then_inc(sem["bank_read"], 1)
                    dve.wait_ge(sem["bank_read"], FILL[name, s, "qkv1"])
                    nc.vector.memset(k_stack[s][:, :, :, 24:32], 0.0).then_inc(sem["natural"], 1)
                    yield "low"
                    stack_low(name, s, QB)
                    yield from turned_stacks(name, s, QB)
                elif name == "mid2":
                    yield "wo"
                    add_projected(name, s, "wo")
                    yield "stats"
                    statistics(xs, QB)
                    yield "hat"
                    normalised((name, s, "m2"), xs)
                    add_row(s, "boca")
                    for r in range(2):
                        yield f"kv{r}"
                        dve.wait_ge(sem["bank_filled"], FILL[name, s, f"kv{r}"])
                        nc.vector.tensor_tensor(nat_kv[:, 2 * r:2 * r + 2, :], Y[:, :].rearrange("p (b n) -> p b n", b=2),
                                                row("bcakv", 2), ALU.add).then_inc(sem["bank_read"], 1)
                    yield "msplit"
                    split_x(name, s, "m2", "m2_t")
                    yield "q"
                    dve.wait_ge(sem["bank_filled"], FILL[name, s, "q"])
                    nc.vector.tensor_tensor(nat_q[:, :, :], in_bank(QB), row("bcaq", QB), ALU.add
                                            ).then_inc(sem["bank_read"], 1)
                    dve.wait_ge(sem["bank_read"], FILL[name, s, "q"])
                    nc.vector.memset(q_stack[s][:, :, :, 24:32], 0.0).then_inc(sem["natural"], 1)
                    yield "low"
                    stack_low(name, s, TB)
                    yield from turned_stacks(name, s, TB)
                elif name == "mid3":
                    yield "wo"
                    add_projected(name, s, "wo")
                    yield "stats"
                    statistics(xs, QB)
                    yield "hat"
                    normalised((name, s, "m3"), xs)
                    add_row(s, "bmlp2")
                    yield "down"
                    add_projected(name, s, "down")
                    yield "squares"
                    then(nc.vector.tensor_tensor(xhat[:, 0:QB, :], xs[:, :, :], xs[:, :, :], ALU.mult))
                    then(nc.vector.tensor_reduce(moments[:, 0:QB, 0], xhat[:, 0:QB, :], AX.X, ALU.add))
                    nc.vector.tensor_scalar(var_eps[:, 0:QB], moments[:, 0:QB, 0], 1.0 / D, EPS, ALU.mult, ALU.add
                                            ).then_inc(sem["var"], 1)
                    yield "rmshat"
                    dve.wait_ge(sem["rstd"], NORM[name, s, "rms"])
                    for k in range(QB):
                        last = nc.vector.tensor_scalar(xhat[:, k, :], xs[:, k, :], rstd[:, k:k + 1], None, ALU.mult)
                    last.then_inc(sem["hat"], 1)
                    for r in range(2):
                        yield f"kv{r}"
                        dve.wait_ge(sem["bank_filled"], FILL[name, s, f"kv{r}"])
                        nc.vector.tensor_copy(nat_kv[:, 2 * r:2 * r + 2, :], Y[:, :].rearrange("p (b n) -> p b n", b=2)
                                              ).then_inc(sem["bank_read"], 1)
                    dve.wait_ge(sem["bank_read"], FILL[name, s, "kv1"])
                    yield "krope"
                    rotate(s, heads4(nat_kv[:, :, 0:D]), TB, 0)
                    yield "rsplit"
                    split_x(name, s, "rms", "rms_t")
                    yield "q"
                    dve.wait_ge(sem["bank_filled"], FILL[name, s, "q"])
                    nc.vector.tensor_copy(nat_q[:, :, :], in_bank(QB)).then_inc(sem["bank_read"], 1)
                    dve.wait_ge(sem["bank_read"], FILL[name, s, "q"])
                    yield "qrope"
                    rotate(s, heads4(nat_q[:, :, :]), QB, TB)
                    nc.vector.tensor_scalar(ss[:, :, :], ss[:, :, :], EPS_L2 ** 2, None, ALU.max
                                            ).then_inc(sem["squares"], 1)
                    yield "unit"
                    dve.wait_ge(sem["root"], nth("root", s))
                    then(nc.vector.reciprocal(norm[:, :, :], norm[:, :, :]))
                    for y4, at, blocks in ((heads4(nat_kv[:, :, 0:D]), 0, TB), (heads4(nat_q[:, :, :]), TB, QB)):
                        last = nc.vector.tensor_tensor(y4, y4, norm[:, at:at + blocks, :].unsqueeze(3).to_broadcast(
                            [P, blocks, H, E2]), ALU.mult)
                    last.then_inc(sem["natural"], 1)
                    yield "low"
                    stack_low(name, s, TB)
                    yield from turned_stacks(name, s, TB)
                else:
                    yield "wo"
                    dve.wait_ge(sem["bank_filled"], FILL[name, s, "wo"])
                    nc.vector.tensor_tensor(xs[:, :, :], in_bank(QB), xs[:, :, :], ALU.add
                                            ).then_inc(sem["bank_read"], 1)

            def maximum(ph, u):
                h, part = u // ph.per_head, u % ph.per_head
                dve.wait_ge(sem["attention_scores"], ph.at("scores", u + 1))
                bank = SC[ph.at("scores", u) % 3]
                if ph.per_head == 1:
                    out, src = nmax[:, h * QB:h * QB + QB], bank[:, :].rearrange("p (b k) -> p b k", b=QB)
                else:
                    out, src = nmax[:, h * QB + part:h * QB + part + 1], bank[:, :]
                nc.vector.tensor_reduce(out, src, AX.X, ALU.max, negate=True).then_inc(sem["attention_max"], 1)

            def t_low(ph, h):
                dve.wait_ge(sem["attention_t_hi"], ph.at("t_hi", h + 1))
                low_part(t_lo[0:ph.t_rows, h % 2, :], X[0:ph.t_rows, 0:S],
                         t_hi[0:ph.t_rows, h % 2, :]).then_inc(sem["attention_t_lo"], 1)

            def turned_copy(ph, u):
                h = u // ph.per_head
                dve.wait_ge(sem["attention_turned"], ph.at("turned", u + 1))
                if h >= ph.slots:
                    dve.wait_ge(sem["attention_heads"], ph.at("heads", (h - ph.slots) // ph.group + 1))
                nc.vector.tensor_copy(turned_place(ph, u), turned_in_bank(ph, 1)).then_inc(sem["attention_copied1"], 1)

            def inverse_sums(ph, g):
                dve.wait_ge(sem["attention_exp"], ph.at("exp", (g + 1) * ph.group * ph.per_head))
                s = inv[:, :, 0:ph.group]
                then(nc.vector.reciprocal(s, sums[:, :, g * ph.group:(g + 1) * ph.group]))
                nc.vector.tensor_copy(rinv[:, :, :].rearrange("p b (h c) -> p b h c", h=ph.group),
                                      s.unsqueeze(3).to_broadcast([P, QB, ph.group, ph.rows])
                                      ).then_inc(sem["attention_rinv"], 1)

            def scale_out(ph, g):
                dve.wait_ge(sem["attention_scale"], ph.at("scale", g + 1))
                nc.vector.tensor_tensor(out_t[ph.s][:, g, :], O[:, 0:S], scale_t[:, g % 2, :], ALU.mult
                                        ).then_inc(sem["attention_out_scaled"], 1)

            def quad_copy(ph, g):
                dve.wait_ge(sem["attention_heads"], ph.at("heads", g + 1))
                nc.vector.tensor_copy(scale_t[:, g % 2, :], O[:, 0:S]).then_inc(sem["l3_heads_copied"], 1)

            def quad_scale(ph, g):
                dve.wait_ge(sem["attention_scale"], ph.at("scale", g + 1))
                temp = out_t[ph.s][:, QUADS + g % 2, :]
                then(nc.vector.reciprocal(temp, O[:, S:2 * S]))
                nc.vector.tensor_tensor(out_t[ph.s][:, g, :], scale_t[:, g % 2, :], temp, ALU.mult
                                        ).then_inc(sem["attention_out_scaled"], 1)

            def attention(ph):
                if ph.key_major:
                    for u in range(ph.units):
                        if ph.ends_group(u) is not None:
                            quad_copy(ph, ph.ends_group(u))
                        if ph.ends_group(u - 2) is not None:
                            quad_scale(ph, ph.ends_group(u - 2))
                        if u == ph.units - 1:
                            quad_copy(ph, ph.groups - 1)
                            quad_scale(ph, ph.groups - 1)
                        yield
                    return
                if ph.t_rows:
                    t_low(ph, 0)
                    t_low(ph, 1)
                maximum(ph, 0)
                maximum(ph, 1)
                for h in early_t(ph):
                    t_low(ph, h)
                for u in range(ph.units):
                    if u + 2 < ph.units:
                        maximum(ph, u + 2)
                    g = ph.ends_group(u)
                    if g is not None:
                        inverse_sums(ph, g)
                    if u % 2 == 1:
                        turned_copy(ph, u)
                    if next_t(ph, u):
                        t_low(ph, next_t(ph, u))
                    if g is not None:
                        scale_out(ph, g)
                    if u == ph.units - 1:
                        inverse_sums(ph, ph.groups - 1)
                        scale_out(ph, ph.groups - 1)
                    yield

            def segment(name, ends):
                enter(name)
                chained["segment_chain"] = 0
                run_rounds(name, attention, chain)
                segment_end(dve, ends)

            segment("first", 1)
            with dve.Fori(0, LOOPS) as b:
                segment("loop", b + 2)
            segment("last", LOOPS + 2)

        @block.gpsimd
        def _(pool):
            nc.gpsimd.memset(minus_half[:, :], -0.5)
            nc.gpsimd.memset(f32(q_mask[:, :, :]), 0.0)
            for k in range(3):
                nc.gpsimd.memset(wo_pad[k][:, :, :], 0.0).then_inc(sem["pads_clear"], 1)
            setup_end(pool)

            issued = {"attention_mask": 0, "rstd": 0, "pads": 0}

            def power(key, blocks=QB):
                if issued["attention_mask"]:
                    pool.wait_ge(sem["attention_mask"], issued["attention_mask"])
                if issued["pads"]:
                    pool.wait_ge(sem["pads"], issued["pads"])
                if issued["rstd"]:
                    pool.wait_ge(sem["rstd"], issued["rstd"])
                issued["rstd"] += 1
                pool.wait_ge(sem["var"], NORM[key])
                nc.gpsimd.tensor_tensor(rstd[:, 0:blocks], var_eps[:, 0:blocks], minus_half[:, 0:blocks],
                                        ALU.pow).then_inc(sem["rstd"], 1)

            def chain(name, s):
                steps = {"start": [("stats", "ln1")], "mid0": [("stats", "ln2"), ("astats", "audio")],
                         "mid1": [("stats", "ln3"), ("tstats", "text"), ("ostats", "out1"),
                                  ("mstats", "m1")],
                         "mid2": [("stats", "m2")], "mid3": [("stats", "m3"), ("squares", "rms")], "end": []}[name]
                for step, n in steps:
                    yield step
                    power((name, s, n), TB if n == "audio" else QB)
                    if n == "out1":
                        pool.wait_ge(sem["bank_read"], FILL[name, s, "wout"])
                        pool.wait_ge(sem["rstd"], issued["rstd"])
                        nc.gpsimd.memset(v_pad[s][:, :, :, E2 + 1:32], 0.0).then_inc(sem["pads"], 1)
                        pool.wait_ge(sem["pads"], issued["pads"] + 1)
                        nc.gpsimd.memset(v_pad[s][:, :, :, E2:E2 + 1], 1.0).then_inc(sem["pads"], 1)
                        issued["pads"] += 2

            def mask(ph, h):
                g, i = h // 4, h % 4
                if h >= 4:
                    pool.wait_ge(sem["attention_scores"], ph.at("scores", (h - 3) * ph.per_head))
                if issued["rstd"]:
                    pool.wait_ge(sem["rstd"], issued["rstd"])
                if issued["pads"]:
                    pool.wait_ge(sem["pads"], issued["pads"])
                issued["attention_mask"] += 1
                rows = slice(32 * i, 32 * i + 32)
                nc.gpsimd.tensor_copy(q_mask[rows, i, :], f32(q_t[ph.s][rows, g, :])
                                      ).then_inc(sem["attention_mask"], 1)

            def attention(ph):
                if ph.masked:
                    name = {"self2": "mid1", "cross2": "mid2", "l3": "mid3"}[ph.name]
                    if precedes((name, ph.s), (ph.name, ph.s)):
                        pool.wait_ge(sem["bank_read"], FILL[name, ph.s, "qt1"])
                    if ph.before["scores"]:
                        pool.wait_ge(sem["attention_scores"], ph.at("scores", 0))
                for u in range(ph.units):
                    if ph.masked and u == 0:
                        for h in range(3 // ph.per_head + 1):
                            mask(ph, h)
                    elif ph.masked and (u + 3) % ph.per_head == 0 and (u + 3) // ph.per_head < H:
                        mask(ph, (u + 3) // ph.per_head)
                    yield

            def segment(name, ends):
                enter(name)
                issued.update(attention_mask=0, rstd=0, pads=0)
                run_rounds(name, attention, chain)
                segment_end(pool, ends)

            segment("first", 1)
            with pool.Fori(0, LOOPS) as b:
                segment("loop", b + 2)
            segment("last", LOOPS + 2)

        @block.sync
        def _(sp):
            for name, dst in CONSTANTS + RAW:
                sp.dma_start(dst, A[name]).then_inc(sem["raw_loaded"], 16)
            for name, dst in KEPT:
                sp.dma_start(dst, A[name]).then_inc(sem["kept_loaded"], 16)
            sp.wait_ge(sem["pads_clear"], 3)
            for k, name in enumerate(("sawo", "cawo", "l3wo")):
                for i in range(4):
                    sp.dma_start(wo_pad[k][32 * i:32 * i + E2, :, :], A[name][i]).then_inc(sem["wo_loaded"], 16)
            sp.wait_ge(sem["wo_loaded"], 16 * 12)
            setup_end(sp)

            def load(s, b):
                sp.dma_start(ctx_nat[s], A["ctx"][:, bass.ds(b * TB, TB), :]).then_inc(sem[f"ctx_loaded{s}"], 16)
                sp.dma_start(x[s][:, :, :], A["x"][:, bass.ds(b * QB, QB), :]).then_inc(sem[f"x_loaded{s}"], 16)

            def store(s, b):
                sp.wait_ge(sem["bank_read"], FILL["end", s, "wo"])
                sp.dma_start(y_out[:, bass.ds(b * QB, QB), :], x[s][:, :, :]).then_inc(sem[f"y_stored{s}"], 16)
                sp.wait_ge(sem[f"y_stored{s}"], 16)

            def segment_over():
                sp.wait_ge(sem["segment_done"], ENGINES - 1)
                sp.sem_clear(sem.ids()).then_inc(segments_over, 1)

            enter("first")
            load(0, 0)
            segment_over()
            with sp.Fori(0, LOOPS) as b:
                enter("loop")
                load(1, b * STREAMS + 1)
                store(0, b * STREAMS)
                load(0, b * STREAMS + 2)
                store(1, b * STREAMS + 1)
                segment_over()
            enter("last")
            load(1, B - 1)
            store(0, B - 2)
            store(1, B - 1)
            segment_over()


def rope_tables():
    inv = 1.0 / 10000.0 ** (np.arange(0, E2, 2, dtype=np.float32) / E2)
    freqs = np.einsum("i,j->ij", np.arange(T, dtype=np.float32), inv)
    emb = np.concatenate([freqs, freqs], axis=-1)
    sign = np.concatenate([-np.ones(E2 // 2, np.float32), np.ones(E2 // 2, np.float32)])
    by_partition = lambda t: t.astype(np.float32).reshape(TB, P, E2).transpose(1, 0, 2)
    return by_partition(np.cos(emb)), by_partition(np.sin(emb) * sign)


def layout(a):
    l0, l1, l2, l3 = (f"L{n}_xattn_" for n in range(4))
    cols = lambda v: v.reshape(-1, P).T
    out = {"x": a["x"], "ctx": a["ctx_768"]}
    out["ident"] = np.eye(P, dtype=np.float32)
    sum_rows = np.zeros((P, P), np.float32)
    for i in range(4):
        sum_rows[32 * i + E2, 32 * i:32 * i + 32] = 1.0
    out["sum_rows"] = sum_rows
    out["rope_cos"], out["rope_sin"] = rope_tables()
    for n in (1, 2):
        out[f"wqt{n - 1}"] = a[f"{l0}wq{n}"].T
        out[f"wkt{n - 1}"] = a[f"{l0}wk{n}"].T
        out[f"wv{n}"] = a[f"{l0}wv{n}"]
        out[f"wo{n}"] = a[f"{l0}wo{n}"]
        out[f"bo{n}"] = a[f"{l0}bo{n}"]
    for n in (1, 2, 3):
        out[f"ln{n}g"], out[f"ln{n}b"] = cols(a[f"{l0}ln{n}_g"]), cols(a[f"{l0}ln{n}_b"])
        out[f"m{n}g"], out[f"m{n}b"] = cols(a[f"{l2}ln{n}_g"]), cols(a[f"{l2}ln{n}_b"])
    out["wff1"], out["wff2"] = a[l0 + "w_ff1"], a[l0 + "w_ff2"]
    out["bff1"], out["bff2"] = cols(a[l0 + "b_ff1"]), a[l0 + "b_ff2"]
    out["wtext"], out["waudio"], out["wout1"] = a[l1 + "W_text"], a[l1 + "W_audio"], a[l1 + "W_out"]
    out["btext"], out["baudio"], out["bout"] = a[l1 + "b_text"], a[l1 + "b_audio"], a[l1 + "b_out"]
    for n in ("g1", "beta1", "g2", "beta2"):
        out[n] = cols(a[l1 + n])
    out["gout"], out["betaout"] = a[l1 + "g_out"], a[l1 + "beta_out"]
    for k in "qkv":
        out[f"saw{k}"], out[f"caw{k}"] = a[f"{l2}sa_w{k}"].T, a[f"{l2}ca_w{k}"].T
        out[f"sab{k}"], out[f"cab{k}"] = a[f"{l2}sa_b{k}"], a[f"{l2}ca_b{k}"]
    out["wcaq"], out["bcaq"] = out.pop("cawq"), out.pop("cabq")
    out["sawo"], out["cawo"], out["l3wo"] = a[l2 + "sa_wo"].T, a[l2 + "ca_wo"].T, a[l3 + "wout"]
    out["bosa"], out["boca"] = a[l2 + "sa_bo"], a[l2 + "ca_bo"]
    out["wmlp1"], out["wmlp2"] = a[l2 + "mlp_w1"].T, a[l2 + "mlp_w2"].T
    out["bmlp1"], out["bmlp2"] = cols(a[l2 + "mlp_b1"]), a[l2 + "mlp_b2"]
    out["wl3q"], out["wl3kv"], out["normw"] = a[l3 + "wq"], a[l3 + "wkv"], cols(a[l3 + "norm_w"])
    return {n: np.ascontiguousarray(v) for n, v in out.items()}


VIEWS = {"x": "b (q p) n -> p (b q) n", "ctx": "b (q p) n -> p (b q) n"}
VIEWS |= dict.fromkeys(("wqt0", "wkt0", "wqt1", "wkt1", "wo1", "wo2", "wff2", "wmlp2"), "(j p) n -> p j n")
VIEWS |= dict.fromkeys(("sawo", "cawo", "l3wo"), "(g i c) n -> i c g n")
SIZES = {"(j p) n -> p j n": {"p": P}, "(g i c) n -> i c g n": {"i": 4, "c": E2}, VIEWS["x"]: {"p": P}}
ROWS = ("bo1", "bo2", "bff2", "btext", "baudio", "bout", "gout", "betaout", "sabq", "sabk", "sabv", "bcaq",
        "cabk", "cabv", "bosa", "boca", "bmlp2")


def kernel(**inputs):
    from concourse import bacc
    from concourse.bass_utils import run_bass_kernel_spmd

    arrays = layout({n: np.asarray(v) for n, v in inputs.items()})
    nc = bacc.Bacc("TRN2", target_bir_lowering=False, num_devices=1, dynamic_dma_scratch_size=1024)
    A = {}
    for name, a in arrays.items():
        ap = nc.dram_tensor(name + "_dram", a.shape, mybir.dt.from_np(a.dtype), kind="ExternalInput").ap()
        if name in VIEWS:
            ap = ap.rearrange(VIEWS[name], **SIZES[VIEWS[name]])
        elif name in ROWS:
            ap = ap.partition_broadcast(P)
        A[name] = ap
    y = nc.dram_tensor("y_dram", arrays["x"].shape, F32, kind="ExternalOutput").ap().rearrange(VIEWS["x"], p=P)
    program(nc, A, y)
    r = run_bass_kernel_spmd(nc, [{n + "_dram": a for n, a in arrays.items()}], core_ids=[0])
    return r.results[0]["y_dram"]
```

```python
from contextlib import ExitStack

import numpy as np

import concourse.bass as bass
from concourse import mybir

F32 = mybir.dt.float32
F32R = mybir.dt.float32r
ACT = mybir.ActivationFunctionType
ALU = mybir.AluOpType
AX = mybir.AxisListType

B, S, D = 8, 256, 128
T, C = 512, 96
H = 16
E0 = 64
E2 = 8
INNER = H * E0
FF = 4 * D
P = 128
QB = S // P
TB = T // P
PAIRS = H // 2
QUADS = H // 4
STREAMS = 2
PROBS_SLOTS = 5
EPS = 1e-5
EPS_L2 = 1e-12
ENGINES = 5


class Semaphores:

    def __init__(self, nc, ctx):
        self.nc, self.ctx, self.by_name = nc, ctx, {}

    def __getitem__(self, name):
        if name not in self.by_name:
            self.by_name[name] = self.ctx.enter_context(self.nc.semaphore(name))
        return self.by_name[name]

    def ids(self):
        ids = sorted(s.num for s in self.by_name.values())
        assert ids == list(range(ids[0], ids[0] + len(ids)))
        return range(ids[0], ids[0] + len(ids))


class Attention:

    def __init__(self, name, s, group, keys, t_rows=0, masked=False, key_major=False):
        self.name, self.s, self.group, self.keys, self.t_rows = name, s, group, keys, t_rows
        self.masked, self.key_major = masked, key_major
        self.kb = keys // P
        self.per_head = keys // S
        self.units = H * self.per_head
        self.groups = H // group
        self.slots = min(2 * group, PROBS_SLOTS)
        self.rows = P // group
        self.before = {}

    def counts(self):
        t = H if self.t_rows else 0
        qm = 0 if self.key_major else 1
        return {"t": t, "t_hi": t, "t_lo": t, "mask": H if self.masked else 0, "scores": self.units,
                "max": self.units * qm, "exp": self.units, "turned": self.units * qm,
                "copied0": self.units // 2 * qm, "copied1": self.units // 2 * qm, "rinv": self.groups * qm,
                "heads": self.groups, "scale": self.groups, "out_scaled": self.groups}

    def at(self, what, n):
        return self.before[what] + n

    def ends_group(self, u):
        n = self.group * self.per_head
        return u // n - 1 if u % n == 0 and u else None


MAKE = {"self0": lambda s: Attention("self0", s, 2, S, t_rows=D),
        "cross0": lambda s: Attention("cross0", s, 2, T, t_rows=C),
        "self2": lambda s: Attention("self2", s, 4, S, masked=True),
        "cross2": lambda s: Attention("cross2", s, 4, T, masked=True),
        "l3": lambda s: Attention("l3", s, 4, T, masked=True, key_major=True)}

CHAINS = {
    "start": "ctx stats hat ln1 split v0 v1 v2 v3",
    "mid0": "audio wo stats hat v0 astats ln2 v1 split v2 ahat v3 audio_t v4 asplit v5 v6 v7",
    "mid1": "wo stats hat ln3 gate l0 l1 down x1_t x1_lo text "
            "tstats that text_t tsplit s0 e0 s1 e1 p0 p1 pv sc wout ostats ohat mstats mhat m1_t msplit "
            "qkv0 qkv1 high low qt0 qt1 kt0 kt1",
    "mid2": "wo stats hat kv0 kv1 m2_t msplit q high low qt0 qt1 kt0 kt1 kt2 kt3",
    "mid3": "wo stats hat m3_t up down squares rmshat kv0 kv1 krope rms_t rsplit q qrope root unit high "
            "low qt0 qt1 kt0 kt1 kt2 kt3",
    "end": "wo",
}
FILLS = {
    "start": "ctx ln1 v0 v1 v2 v3",
    "mid0": "audio wo v0 ln2 v1 v2 v3 audio_t v4 v5 v6 v7",
    "mid1": "wo ln3 g0 g1 l0 l1 down x1_t text text_t s0 s1 p0 p1 pv wout m1_t qkv0 qkv1 "
            "qt0 qt1 kt0 kt1",
    "mid2": "wo kv0 kv1 m2_t q qt0 qt1 kt0 kt1 kt2 kt3",
    "mid3": "wo m3_t up0 up1 down kv0 kv1 rms_t q qt0 qt1 kt0 kt1 kt2 kt3",
    "end": "wo",
}
NORMS = {"start": "ln1", "mid0": "ln2 audio", "mid1": "ln3 text out1 m1", "mid2": "m2", "mid3": "m3 rms", "end": ""}

SPLITS = {"start": "ln1", "mid0": "ln2 audio", "mid1": "text m1", "mid2": "m2", "mid3": "rms", "end": ""}


PAIR = [("self0", 0, [("start", 1)]), ("self0", 1, [("mid0", 0)]), ("cross0", 0, [("mid0", 1)]),
        ("cross0", 1, [("mid1", 0)]), ("self2", 0, [("mid1", 1)]), ("self2", 1, [("mid2", 0)]),
        ("cross2", 0, [("mid2", 1)]), ("cross2", 1, [("mid3", 0)]), ("l3", 0, [("mid3", 1)])]
SEGMENTS = {
    "first": [("", 0, [("start", 0)])],
    "loop": PAIR + [("l3", 1, [("end", 0), ("start", 0)]), ("", 0, [("end", 1)])],
    "last": PAIR + [("l3", 1, [("end", 0)]), ("", 0, [("end", 1)])],
}
LOOPS = B // STREAMS - 1

TOTAL = {"l1_max": 2, "pads": 2, "l3_heads_copied": QUADS}
CHAIN_OF = {"ctx_high": "start", "x1_high": "mid1", "l1_max": "mid1", "l1_rinv": "mid1", "l1_scale": "mid1",
            "pads": "mid1", "squares": "mid3", "root": "mid3", "l3_heads_copied": "l3"}

ORDER = []
PHASES = {}
FILL = {}
NORM = {}
SPLIT = {}


def bank_name(key):
    chain, s, content = key
    spare = content in ("g1", "l1", "s1", "p1", "qkv1", "up1", "kv1", "qt1", "kt1", "kt3")
    if chain == "start":
        spare = s == 0 and content in ("v1", "v3")
    return "spare" if spare and (chain, s) != ("mid1", 0) else "chain"


def filled(key):
    return f"{bank_name(key)}_bank_filled"


def bank_read(key):
    return f"{bank_name(key)}_bank_read"


def enter(segment):
    for table in (ORDER, PHASES, FILL, NORM, SPLIT):
        table.clear()
    fills = {"chain": 0, "spare": 0}
    total = {}
    for phase, ps, chains in SEGMENTS[segment]:
        if phase:
            ph = PHASES[phase, ps] = MAKE[phase](ps)
            ph.before = dict.fromkeys(ph.counts(), 0) | total
            total = {what: ph.before[what] + n for what, n in ph.counts().items()}
            ORDER.append((phase, ps))
        for chain, s in chains:
            ORDER.append((chain, s))
            for content in FILLS[chain].split():
                fills[bank_name((chain, s, content))] += 1
                FILL[chain, s, content] = fills[bank_name((chain, s, content))]
            for table, of_chain in ((NORM, NORMS), (SPLIT, SPLITS)):
                for content in of_chain[chain].split():
                    table[chain, s, content] = len(table) + 1


def rank(s, name):
    return [key[1] for key in ORDER if key[0] == name].index(s)


def precedes(first, second):
    return first in ORDER and ORDER.index(first) < ORDER.index(second)


def early_t(ph):
    return (range(2, 4) if ph.per_head == 1 else (2,)) if ph.t_rows else ()


def next_t(ph, u):
    ahead = u + (4 if ph.per_head == 1 else 5)
    return ahead // ph.per_head if ph.t_rows and ahead < ph.units and ahead % ph.per_head == 0 else None


PACE = {
    ("mid0", 0): {"hat": 0.5, "v2": 4, "v4": 1.6, "v5": 1.6, "v7": 4},
    ("mid0", 1): {"hat": 0.25, "astats": 0.6, "v1": 1.6, "audio_t": 0.6, "v4": 1.6, "v5": 1.6, "v7": 8},
    ("mid1", 0): {"l0": 0.3},
    ("mid1", 1): {"that": 0.4, "text_t": 0.4, "p1": 0.4, "qkv1": 2.5, "qt1": 0.5, "kt0": 0.5},
    ("mid2", 1): {"stats": 0.3},
    ("mid3", 0): {"unit": 1.6},
    ("mid3", 1): {"unit": 1.6},
    ("start", 1): {"ctx": 0.8, "stats": 4, "ln1": 0.64, "split": 6.25, "v0": 1.6, "v1": 4, "v3": 2.5},
}


def due(steps, units):
    pace = [PACE.get((name, s), {}).get(step, 1.0) for name, s, step in steps]
    return {step: int(sum(pace[:n]) * units / sum(pace)) for n, step in enumerate(steps)}


def run_rounds(segment, attention, chain):
    ending = iter(())
    for phase, ps, chains in SEGMENTS[segment]:
        units = PHASES[phase, ps].units if phase else 1
        at = due([(name, s, step) for name, s in chains for step in CHAINS[name].split()], units)
        work = ((name, s, step) for name, s in chains for step in chain(name, s))
        emitted = attention(PHASES[phase, ps]) if phase else iter((None, None))
        next(emitted)
        assert next(ending, "over") == "over"
        ahead = next(work, None)
        for u in range(units):
            next(emitted)
            while ahead is not None and at[ahead] <= u:
                ahead = next(work, None)
        assert ahead is None
        ending = emitted
    assert next(ending, "over") == "over"


def program(nc, A, y_out):
    ctx = ExitStack()
    with ctx:
        def sb(name, shape, dt=F32):
            return ctx.enter_context(nc.sbuf_tensor(name, shape, dt))

        def ps(name, cols=512):
            return ctx.enter_context(nc.psum_tensor(name, [P, cols], F32))

        def f32r(ap):
            return ap.bitcast(F32R)

        def f32(ap):
            return ap.bitcast(F32)

        def per_stream(name, shape, dt=F32):
            return [sb(f"{name}_{s}", shape, dt) for s in range(STREAMS)]

        ident = sb("ident", [P, P])
        sum_rows = sb("sum_rows", [P, P])
        rope_cos = sb("rope_cos", [P, TB, E2])
        rope_sin = sb("rope_sin", [P, TB, E2])
        minus_half = sb("minus_half", [P, TB])
        m_hi = [sb("m1_hi", [P, H, D], F32R), sb("m2_hi", [P, H, C], F32R)]
        m_lo = [sb("m1_lo", [P, H, D], F32R), sb("m2_lo", [P, H, C], F32R)]
        split = {}
        for name, rows, cols in (("wv1", D, INNER), ("wv2", C, INNER), ("wtext", D, D),
                                 ("waudio", C, D), ("wsa", D, 3 * D), ("wcaq", D, D), ("wcakv", C, 2 * D),
                                 ("wl3q", D, D), ("wl3kv", C, 2 * D)):
            split[name] = (sb(name + "_hi", [rows, cols], F32R), sb(name + "_lo", [rows, cols], F32R))
        wo = [sb("wo1", [P, PAIRS, D]), sb("wo2", [P, PAIRS, D])]
        wff1 = sb("wff1", [D, 2 * FF])
        wff2 = sb("wff2", [P, FF // P, D])
        wout1 = sb("wout1", [P, D])
        wmlp1 = sb("wmlp1", [D, FF])
        wmlp2 = sb("wmlp2", [P, FF // P, D])
        wo_pad = [sb("wo_sa", [P, QUADS, D]), sb("wo_ca", [P, QUADS, D]), sb("wo_l3", [P, QUADS, D])]
        rows_of = {}
        for name, cols in (("bo1", D), ("bo2", D), ("bff2", D), ("btext", D), ("baudio", D), ("bout", D),
                           ("gout", D), ("betaout", D), ("bsa", 3 * D), ("bcaq", D), ("bcakv", 2 * D),
                           ("bosa", D), ("boca", D), ("bmlp2", D)):
            rows_of[name] = sb("row_" + name, [P, cols])
        cols_of = {}
        for name, n in (("ln1g", 1), ("ln1b", 1), ("ln2g", 1), ("ln2b", 1), ("ln3g", 1), ("ln3b", 1),
                        ("bff1", 2 * FF // P), ("g1", 1), ("beta1", 1), ("g2", 1), ("beta2", 1),
                        ("m1g", 1), ("m1b", 1), ("m2g", 1), ("m2b", 1), ("m3g", 1), ("m3b", 1),
                        ("bmlp1", FF // P), ("normw", 1)):
            cols_of[name] = sb("col_" + name, [P, n])

        x = per_stream("x", [P, QB, D])
        ctx_hi, ctx_lo = per_stream("ctx_hi", [C, T], F32R), per_stream("ctx_lo", [C, T], F32R)
        x_hi, x_lo = per_stream("x_hi", [P, S], F32R), per_stream("x_lo", [P, S], F32R)
        v = per_stream("v", [P, TB * INNER])
        out_t = per_stream("out_t", [P, PAIRS, S])
        q_t = per_stream("q_t", [P, QUADS, S], F32R)
        k_t = per_stream("k_t", [P, QUADS, T], F32R)
        v0 = [t[:, :].rearrange("p (b n) -> p b n", b=TB) for t in v]
        probs1 = [t[:, 512:1536].rearrange("p (b k) -> p b k", b=QB) for t in v]
        probs1_t = [t[:, 1536:2560].rearrange("p (k q) -> p k q", k=TB) for t in v]
        l1_rinv = [t[:, 2560:2816].rearrange("p (b n) -> p b n", b=QB) for t in v]
        l1_scale = [t[:, 2816:3072] for t in v]
        k_stack = [t[:, 0:2048].rearrange("p (b h c) -> p b h c", b=TB, h=H) for t in v]
        v_pad = [t[:, 2048:4096].rearrange("p (b h c) -> p b h c", b=TB, h=H) for t in v]
        hidden = [t[:, 0:4, :] for t in out_t]
        q_stack = [t[:, 0:4, :].rearrange("p a c -> p (a c)").rearrange("p (b h c) -> p b h c", b=QB, h=H)
                   for t in out_t]
        rope_tmp = [t[:, 4:6, :].rearrange("p a c -> p (a c)").rearrange("p (b h c) -> p b h c", b=TB, h=H)
                    for t in out_t]
        rope_prod = [t[:, 6:8, :].rearrange("p a c -> p (a c)").rearrange("p (b h c) -> p b h c", b=TB, h=H)
                     for t in out_t]
        ctx_nat = [t[:, 0:2, :].rearrange("p a c -> p (a c)")[:, 0:TB * C].rearrange("p (b n) -> p b n", b=TB)
                   for t in out_t]
        k1_hi, k1_lo = [t[:, 0, :] for t in k_t], [t[:, 1, :] for t in k_t]

        stats = sb("stats", [P, TB, 6])
        moments = sb("moments", [P, TB, 2])
        var_eps = sb("var_eps", [P, TB])
        rstd = sb("rstd", [P, TB])
        xhat = sb("xhat", [P, TB, D])
        xz = sb("xz", [P, T])
        nat_q = xhat[:, TB - QB:TB, :]
        nat_kv = sb("nat_kv", [P, TB, 2 * D])
        ss = sb("ss", [P, TB + QB, H])
        norm = sb("norm", [P, TB + QB, H])
        l1_nmax = sb("l1_nmax", [P, QB])
        l1_sums = sb("l1_sums", [P, QB])
        t_hi, t_lo = sb("t_hi", [P, 2, S], F32R), sb("t_lo", [P, 2, S], F32R)
        probs = sb("probs", [P, 3, 512])
        probs_t = sb("probs_t", [P, PROBS_SLOTS, TB, S])
        v1 = [probs_t[:, PROBS_SLOTS - 1, 2 * s:2 * s + 2, :].rearrange("p a q -> p (a q)").rearrange(
            "p (b n) -> p b n", b=TB) for s in range(STREAMS)]
        sums = sb("sums", [P, QB, H])
        inv = sb("inv", [P, QB, 4])
        rinv = sb("rinv", [P, QB, P])
        nmax = sb("nmax", [P, H * QB])
        scale_t = sb("scale_t", [P, 2, S])
        q_mask = sb("q_mask", [P, 4, S], F32R)
        table_probe = sb("table_probe", [P, 2])

        raw_at, raw = 0, {}
        raw_tile = probs_t[:, :, :, :].rearrange("p a b c -> p (a b c)")
        for name, (hi, _) in split.items():
            rows, cols = hi.shape
            raw[name] = raw_tile[0:rows, raw_at:raw_at + cols]
            raw_at += cols
        wqt = [v[0][:, 0:PAIRS * D].rearrange("p (j n) -> p j n", j=PAIRS),
               v[0][:, 1024:1024 + PAIRS * D].rearrange("p (j n) -> p j n", j=PAIRS)]
        wkt = [v[0][:, 2048:2048 + PAIRS * D].rearrange("p (j n) -> p j n", j=PAIRS),
               v[0][:, 3072:3072 + PAIRS * C].rearrange("p (j n) -> p j n", j=PAIRS)]

        SC = [ps(f"scores{k}") for k in range(3)]
        PT = [ps("turned0"), ps("turned1")]
        O = ps("heads_out")
        X = ps("queries_m")
        Y = ps("chain_bank")

        sem = Semaphores(nc, ctx)
        segments_over = ctx.enter_context(nc.semaphore("segments_over"))

        def bank_of(key):
            return X if bank_name(key) == "spare" else Y

        def nth(name, s, n=1):
            return TOTAL.get(name, 1) * rank(s, CHAIN_OF[name]) + n

        def each_layer(s, chain):
            before = [key for key in ORDER if key[0] in ("mid1", "mid2", "mid3")]
            return before.index((chain, s)) + 1

        def heads4(ap):
            return ap.rearrange("p b (h c) -> p b h c", h=H)

        def three_products(out, a, b):
            (a_hi, a_lo), (b_hi, b_lo) = a, b
            nc.tensor.matmul(out, a_hi, b_hi, start=True, stop=False)
            nc.tensor.matmul(out, a_lo, b_hi, start=False, stop=False)
            return nc.tensor.matmul(out, a_hi, b_lo, start=False, stop=True)

        def probs_block(ph, k):
            kb, qb = (k // 2, k % 2) if ph.per_head == 1 else (k, 0)
            return slice(qb * S + kb * P, qb * S + (kb + 1) * P)

        def turned_place(ph, u):
            h, part = u // ph.per_head, u % ph.per_head
            if ph.per_head == 1:
                return probs_t[:, h % ph.slots, 0:2, :]
            return probs_t[:, h % ph.slots, :, part * P:(part + 1) * P]

        def turned_in_bank(ph, bank):
            return PT[bank][:, :].rearrange("p (k q) -> p k q", k=2 if ph.per_head == 1 else TB)

        def keys_in_bank(kb_count, bank):
            return bank[:, :].rearrange("p (g k) -> p g k", g=1 if kb_count == TB else 2)

        def keys_turned(s, r, kb_count):
            return k_t[s][:, r:r + 1, :] if kb_count == TB else k_t[s][:, 2 * r:2 * r + 2, 0:S]

        CONSTANTS = [("ident", ident[:, :]), ("sum_rows", sum_rows[:, :]), ("rope_cos", rope_cos[:, :, :]),
                     ("rope_sin", rope_sin[:, :, :])]
        RAW = ([("wqt0", wqt[0]), ("wkt0", wkt[0]), ("wqt1", wqt[1]), ("wkt1", wkt[1])]
               + [(n, raw[n]) for n in ("wv1", "wv2", "wtext", "waudio", "wcaq", "wl3q", "wl3kv")]
               + [(n, raw["wsa"][:, k * D:(k + 1) * D]) for k, n in enumerate(("sawq", "sawk", "sawv"))]
               + [(n, raw["wcakv"][:, k * D:(k + 1) * D]) for k, n in enumerate(("cawk", "cawv"))])
        KEPT = ([("wo1", wo[0][:, :, :]), ("wo2", wo[1][:, :, :]), ("wff1", wff1[:, :]), ("wff2", wff2[:, :, :]),
                 ("wout1", wout1[:, :]), ("wmlp1", wmlp1[:, :]), ("wmlp2", wmlp2[:, :, :])]
                + [(n, t[:, :]) for n, t in cols_of.items()]
                + [(n, rows_of[n][:, :]) for n in rows_of if n not in ("bsa", "bcakv")]
                + [(n, rows_of["bsa"][:, k * D:(k + 1) * D]) for k, n in enumerate(("sabq", "sabk", "sabv"))]
                + [(n, rows_of["bcakv"][:, k * D:(k + 1) * D]) for k, n in enumerate(("cabk", "cabv"))])
        n_raw, n_kept = len(RAW) + len(CONSTANTS), len(KEPT)

        def setup_end(eng):
            eng.drain().then_inc(sem["setup_done"], 1)
            eng.wait_ge(sem["setup_done"], ENGINES)

        def segment_end(eng, ends):
            eng.drain().then_inc(sem["segment_done"], 1)
            eng.wait_ge(segments_over, ends)

        block = ctx.enter_context(nc.Block())

        @block.tensor
        def _(pe):
            pe.wait_ge(sem["raw_loaded"], 16 * n_raw)
            for fill in range(4):
                layer, half = fill // 2, fill % 2
                width = (D, C)[layer]
                for jj in range(4):
                    for i in range(2):
                        bank = (SC[0], SC[1], PT[0], PT[1], O, X, Y, SC[2])[2 * fill + i]
                        rows = slice(64 * i, 64 * i + 64)
                        last = nc.tensor.matmul(bank[:, jj * width:(jj + 1) * width],
                                                wqt[layer][rows, 4 * half + jj, :],
                                                wkt[layer][rows, 4 * half + jj, 0:width], start=True, stop=True)
                last.then_inc(sem["m_made"], 1)
            setup_end(pe)

            def transpose(out, in_):
                return nc.tensor.transpose(out, in_, ident[:, :])

            def fill_bank(key):
                if FILL[key] > 1:
                    pe.wait_ge(sem[bank_read(key)], FILL[key] - 1)

            def block_of(pair, k):
                cols = slice(k * P, (k + 1) * P)
                return pair[0][:, cols], pair[1][:, cols]

            def halves(name, cols=slice(None)):
                hi, lo = split[name]
                return hi[:, cols], lo[:, cols]

            def turn_tokens(key, src, blocks):
                fill_bank(key)
                for k in range(blocks):
                    last = transpose(Y[:, k * P:(k + 1) * P], src[:, k, :])
                last.then_inc(sem["chain_bank_filled"], 1)

            def turn_normalised(chain, s, norm_name, content, blocks=QB):
                pe.wait_ge(sem["hat"], NORM[chain, s, norm_name])
                turn_tokens((chain, s, content), xhat, blocks)

            def values(chain, s, k, left, w):
                kb, half = k // 2, k % 2
                key = chain, s, f"v{k}"
                fill_bank(key)
                three_products(bank_of(key)[:, :], block_of(left, kb),
                               halves(w, slice(512 * half, 512 * half + 512))).then_inc(sem[filled(key)], 1)

            def project_out(chain, s, content, blocks, left, weights, phase=None):
                fill_bank((chain, s, content))
                for qb in range(QB):
                    for j in range(blocks):
                        if phase and qb == 0:
                            pe.wait_ge(sem["attention_out_scaled"], PHASES[phase, s].at("out_scaled", j + 1))
                        last = nc.tensor.matmul(Y[:, qb * P:(qb + 1) * P], left[:, j, qb * P:(qb + 1) * P],
                                                weights(j), start=(j == 0), stop=(j == blocks - 1))
                last.then_inc(sem["chain_bank_filled"], 1)

            def keys_values(chain, s, r, w):
                key = chain, s, f"kv{r}"
                fill_bank(key)
                for k in range(2):
                    last = three_products(bank_of(key)[:, k * 2 * D:(k + 1) * 2 * D],
                                          block_of((ctx_hi[s], ctx_lo[s]), 2 * r + k), halves(w))
                last.then_inc(sem[filled(key)], 1)

            def queries(chain, s, w):
                fill_bank((chain, s, "q"))
                for qb in range(QB):
                    last = three_products(Y[:, qb * D:(qb + 1) * D], block_of((x_hi[s], x_lo[s]), qb), halves(w))
                last.then_inc(sem["chain_bank_filled"], 1)

            def turn_stacks(chain, s, kb_count):
                pe.wait_ge(sem["stacked"], each_layer(s, chain))
                pe.wait_ge(sem["high"], each_layer(s, chain))
                for r in range(2):
                    yield f"qt{r}"
                    key = chain, s, f"qt{r}"
                    fill_bank(key)
                    for g in range(2):
                        for qb in range(QB):
                            last = transpose(bank_of(key)[:, g * S + qb * P:g * S + (qb + 1) * P],
                                             q_stack[s][:, qb, 8 * r + 4 * g:8 * r + 4 * g + 4, :])
                    last.then_inc(sem[filled(key)], 1)
                for r in range(kb_count):
                    yield f"kt{r}"
                    key = chain, s, f"kt{r}"
                    fill_bank(key)
                    for k in range(4):
                        quad, kb = (r, k) if kb_count == TB else (2 * r + k // 2, k % 2)
                        last = transpose(bank_of(key)[:, k * P:(k + 1) * P], k_stack[s][:, kb, 4 * quad:4 * quad + 4, :])
                    last.then_inc(sem[filled(key)], 1)

            def chain(name, s):
                xs, cs = (x_hi[s], x_lo[s]), (ctx_hi[s], ctx_lo[s])
                if name == "start":
                    yield "ctx"
                    pe.wait_ge(sem[f"ctx_loaded{s}"], 16)
                    fill_bank((name, s, "ctx"))
                    for kb in range(TB):
                        last = transpose(Y[0:C, kb * P:(kb + 1) * P], ctx_nat[s][:, kb, :])
                    last.then_inc(sem["chain_bank_filled"], 1)
                    yield "ln1"
                    turn_normalised(name, s, "ln1", "ln1")
                    for k in range(4):
                        yield f"v{k}"
                        pe.wait_ge(sem["split"], SPLIT[name, s, "ln1"])
                        values(name, s, k, xs, "wv1")
                elif name == "mid0":
                    yield "audio"
                    fill_bank((name, s, "audio"))
                    for kb in range(TB):
                        last = three_products(Y[:, kb * D:(kb + 1) * D], block_of(cs, kb), halves("waudio"))
                    last.then_inc(sem["chain_bank_filled"], 1)
                    yield "wo"
                    project_out(name, s, "wo", PAIRS, out_t[s], lambda j: wo[0][:, j, :], "self0")
                    yield "v0"
                    values(name, s, 0, cs, "wv2")
                    yield "ln2"
                    turn_normalised(name, s, "ln2", "ln2")
                    for k in range(1, 8):
                        if k == 4:
                            yield "audio_t"
                            turn_normalised(name, s, "audio", "audio_t", TB)
                        yield f"v{k}"
                        values(name, s, k, cs, "wv2")
                elif name == "mid1":
                    yield "wo"
                    project_out(name, s, "wo", PAIRS, out_t[s], lambda j: wo[1][:, j, :], "cross0")
                    yield "ln3"
                    turn_normalised(name, s, "ln3", "ln3")
                    for part, at in (("g", FF), ("l", 0)):
                        for r in range(2):
                            if part == "l" or r == 0:
                                yield f"l{r}" if part == "l" else "gate"
                            key = name, s, f"{part}{r}"
                            fill_bank(key)
                            for k in range(2):
                                cols = slice(at + (2 * r + k) * P, at + (2 * r + k + 1) * P)
                                last = nc.tensor.matmul(bank_of(key)[:, k * S:(k + 1) * S], wff1[:, cols], xz[:, 0:S],
                                                        start=True, stop=True)
                            last.then_inc(sem[filled(key)], 1)
                    yield "down"
                    pe.wait_ge(sem[bank_read((name, s, "l1"))], FILL[name, s, "l1"])
                    project_out(name, s, "down", 4, hidden[s], lambda j: wff2[:, j, :])
                    yield "x1_t"
                    turn_tokens((name, s, "x1_t"), x[s], QB)
                    yield "text"
                    fill_bank((name, s, "text"))
                    for qb in range(QB):
                        last = three_products(Y[:, qb * P:(qb + 1) * P], block_of(xs, qb), halves("wtext"))
                    last.then_inc(sem["chain_bank_filled"], 1)
                    yield "text_t"
                    turn_normalised(name, s, "text", "text_t")
                    for qb in range(QB):
                        yield f"s{qb}"
                        pe.wait_ge(sem["split"], SPLIT[name, s, "text"])
                        key = name, s, f"s{qb}"
                        fill_bank(key)
                        three_products(bank_of(key)[:, :], block_of(xs, qb), (k1_hi[s], k1_lo[s])
                                       ).then_inc(sem[filled(key)], 1)
                    for qb in range(QB):
                        yield f"p{qb}"
                        key = name, s, f"p{qb}"
                        fill_bank(key)
                        for kb in range(TB):
                            last = transpose(bank_of(key)[:, kb * P:(kb + 1) * P], probs1[s][:, qb, kb * P:(kb + 1) * P])
                        last.then_inc(sem[filled(key)], 1)
                    yield "pv"
                    pe.wait_ge(sem[bank_read((name, s, "p1"))], FILL[name, s, "p1"])
                    fill_bank((name, s, "pv"))
                    for kb in range(TB):
                        nc.tensor.matmul(Y[:, 0:S], v1[s][:, kb, :], probs1_t[s][:, kb, :],
                                         start=(kb == 0), stop=(kb == TB - 1))
                    pe.wait_ge(sem["l1_rinv"], nth("l1_rinv", s))
                    for qb in range(QB):
                        last = transpose(Y[:, S + qb * P:S + (qb + 1) * P], l1_rinv[s][:, qb, :])
                    last.then_inc(sem["chain_bank_filled"], 1)
                    yield "wout"
                    project_out(name, s, "wout", 1, out_t[s], lambda j: wout1[:, :])
                    yield "m1_t"
                    turn_normalised(name, s, "m1", "m1_t")
                    for qb in range(QB):
                        yield f"qkv{qb}"
                        pe.wait_ge(sem["split"], SPLIT[name, s, "m1"])
                        key = name, s, f"qkv{qb}"
                        fill_bank(key)
                        three_products(bank_of(key)[:, 0:3 * D], block_of(xs, qb), halves("wsa")
                                       ).then_inc(sem[filled(key)], 1)
                    yield "low"
                    yield from turn_stacks(name, s, QB)
                elif name == "mid2":
                    yield "wo"
                    project_out(name, s, "wo", QUADS, out_t[s], lambda j: wo_pad[0][:, j, :], "self2")
                    for r in range(2):
                        yield f"kv{r}"
                        keys_values(name, s, r, "wcakv")
                    yield "m2_t"
                    turn_normalised(name, s, "m2", "m2_t")
                    yield "q"
                    pe.wait_ge(sem["split"], SPLIT[name, s, "m2"])
                    queries(name, s, "wcaq")
                    yield "low"
                    yield from turn_stacks(name, s, TB)
                elif name == "mid3":
                    yield "wo"
                    project_out(name, s, "wo", QUADS, out_t[s], lambda j: wo_pad[1][:, j, :], "cross2")
                    yield "m3_t"
                    turn_normalised(name, s, "m3", "m3_t")
                    yield "up"
                    for r in range(2):
                        key = name, s, f"up{r}"
                        fill_bank(key)
                        for k in range(2):
                            last = nc.tensor.matmul(bank_of(key)[:, k * S:(k + 1) * S],
                                                    wmlp1[:, (2 * r + k) * P:(2 * r + k + 1) * P], xz[:, 0:S],
                                                    start=True, stop=True)
                        last.then_inc(sem[filled(key)], 1)
                    yield "down"
                    pe.wait_ge(sem[bank_read((name, s, "up1"))], FILL[name, s, "up1"])
                    project_out(name, s, "down", 4, hidden[s], lambda j: wmlp2[:, j, :])
                    for r in range(2):
                        yield f"kv{r}"
                        keys_values(name, s, r, "wl3kv")
                    yield "rms_t"
                    turn_normalised(name, s, "rms", "rms_t")
                    yield "q"
                    pe.wait_ge(sem["split"], SPLIT[name, s, "rms"])
                    queries(name, s, "wl3q")
                    yield "low"
                    yield from turn_stacks(name, s, TB)
                else:
                    yield "wo"
                    project_out(name, s, "wo", QUADS, out_t[s], lambda j: wo_pad[2][:, j, :], "l3")

            def queries_times_m(ph, h):
                layer = 0 if ph.name == "self0" else 1
                if ph.at("t_lo", h) > 0:
                    pe.wait_ge(sem["attention_t_lo"], ph.at("t_lo", h))
                three_products(X[0:ph.t_rows, 0:S], (m_hi[layer][:, h, :], m_lo[layer][:, h, :]),
                               (x_hi[ph.s][:, :], x_lo[ph.s][:, :])).then_inc(sem["attention_t"], 1)

            def scores(ph, u):
                h, part, s = u // ph.per_head, u % ph.per_head, ph.s
                if ph.at("exp", u - 2) > 0:
                    pe.wait_ge(sem["attention_exp"], ph.at("exp", u - 2))
                if ph.masked:
                    pe.wait_ge(sem["attention_mask"], ph.at("mask", h + 1))
                else:
                    pe.wait_ge(sem["attention_t_lo"], ph.at("t_lo", h + 1))
                bank = SC[ph.at("scores", u) % 3]
                if ph.key_major:
                    for k in range(2):
                        kb = 2 * part + k
                        last = nc.tensor.matmul(bank[:, k * S:(k + 1) * S], k_t[s][:, h // 4, kb * P:(kb + 1) * P],
                                                q_mask[:, h % 4, :], start=True, stop=True)
                else:
                    for k, qb in enumerate(range(QB) if ph.per_head == 1 else (part,)):
                        out, q = bank[:, k * S:k * S + ph.keys], slice(qb * P, (qb + 1) * P)
                        if ph.masked:
                            last = nc.tensor.matmul(out, q_mask[:, h % 4, q], k_t[s][:, h // 4, 0:ph.keys],
                                                    start=True, stop=True)
                        else:
                            right = (x_hi[s], x_lo[s]) if ph.name == "self0" else (ctx_hi[s], ctx_lo[s])
                            last = three_products(out, (t_hi[0:ph.t_rows, h % 2, q], t_lo[0:ph.t_rows, h % 2, q]),
                                                  (right[0][:, :], right[1][:, :]))
                last.then_inc(sem["attention_scores"], 1)

            def turn_probs(ph, u):
                pe.wait_ge(sem["attention_exp"], ph.at("exp", u + 1))
                n = ph.at("turned", u)
                if n >= 2:
                    pe.wait_ge(sem[f"attention_copied{n % 2}"], n // 2)
                for k in range(4):
                    last = transpose(PT[n % 2][:, k * P:(k + 1) * P],
                                     probs[:, n % 3, probs_block(ph, k)])
                last.then_inc(sem["attention_turned"], 1)

            def head_outputs(ph, g):
                s, w = ph.s, ph.rows
                n = (g + 1) * ph.group * ph.per_head
                if ph.key_major:
                    pe.wait_ge(sem["attention_exp"], ph.at("exp", n))
                else:
                    pe.wait_ge(sem["attention_copied0"], ph.at("copied0", n // 2))
                    pe.wait_ge(sem["attention_copied1"], ph.at("copied1", n // 2))
                if ph.at("out_scaled", g) > 0:
                    pe.wait_ge(sem["attention_out_scaled"], ph.at("out_scaled", g))
                for kb in range(ph.kb):
                    for i in range(ph.group):
                        h = g * ph.group + i
                        stationary = v_pad[s][:, kb, h, :] if ph.masked else v0[s][:, kb, h * E0:(h + 1) * E0]
                        last = nc.tensor.matmul(O[w * i:w * i + w, 0:S], stationary,
                                                probs_t[:, h % ph.slots, kb, :], start=(kb == 0),
                                                stop=(kb == ph.kb - 1))
                if not ph.key_major:
                    pe.wait_ge(sem["attention_rinv"], ph.at("rinv", g + 1))
                    for qb in range(QB):
                        last = transpose(O[:, S + qb * P:S + (qb + 1) * P], rinv[:, qb, :])
                last.then_inc(sem["attention_heads"], 1)

            def quad_sums(ph, g):
                pe.wait_ge(sem["l3_heads_copied"], nth("l3_heads_copied", ph.s, g + 1))
                nc.tensor.matmul(O[:, S:2 * S], sum_rows[:, :], scale_t[:, g % 2, :], start=True,
                                 stop=True).then_inc(sem["attention_scale"], 1)

            def attention(ph):
                chain, contents = {"self0": ("start", ("v2", "v3")), "cross0": ("mid0", ("v7",)),
                                   "self2": ("mid1", ("kt0", "kt1")), "cross2": ("mid2", ("kt2", "kt3")),
                                   "l3": ("mid3", ("kt2", "kt3"))}[ph.name]
                if precedes((chain, ph.s), (ph.name, ph.s)):
                    for content in contents:
                        pe.wait_ge(sem[bank_read((chain, ph.s, content))], FILL[chain, ph.s, content])
                    if ph.name == "cross0":
                        pe.wait_ge(sem["split"], SPLIT["mid0", ph.s, "audio"])
                    if ph.masked:
                        pe.wait_ge(sem["v_padded"], each_layer(ph.s, chain))
                if ph.t_rows:
                    queries_times_m(ph, 0)
                    queries_times_m(ph, 1)
                scores(ph, 0)
                scores(ph, 1)
                for h in early_t(ph):
                    queries_times_m(ph, h)
                yield
                for u in range(ph.units):
                    if u + 2 < ph.units:
                        scores(ph, u + 2)
                    if not ph.key_major:
                        turn_probs(ph, u)
                    if next_t(ph, u):
                        queries_times_m(ph, next_t(ph, u))
                    g = ph.ends_group(u)
                    if g is not None:
                        head_outputs(ph, g)
                    if ph.key_major and ph.ends_group(u - 2) is not None:
                        quad_sums(ph, ph.ends_group(u - 2))
                    yield
                head_outputs(ph, ph.groups - 1)
                if ph.key_major:
                    quad_sums(ph, ph.groups - 1)

            def segment(name, ends):
                enter(name)
                run_rounds(name, attention, chain)
                segment_end(pe, ends)

            segment("first", 1)
            with pe.Fori(0, LOOPS) as b:
                segment("loop", b + 2)
            segment("last", LOOPS + 2)

        @block.scalar
        def _(act):
            def copy(out, in_, scale=1.0):
                return nc.scalar.activation(out, in_, ACT.Copy, scale=scale)

            act.wait_ge(sem["raw_loaded"], 16 * n_raw)
            act.wait_ge(sem["raw_scaled"], 1)
            for name in split:
                copy(split[name][0][:, :], raw[name]).then_inc(sem["w_hi"], 1)
            for fill in range(4):
                layer, half = fill // 2, fill % 2
                width = (D, C)[layer]
                act.wait_ge(sem["m_made"], fill + 1)
                for i in range(2):
                    bank = (SC[0], SC[1], PT[0], PT[1], O, X, Y, SC[2])[2 * fill + i]
                    out = m_hi[layer][:, :, :].rearrange("p (j i) n -> p j i n", i=2)[:, 4 * half:4 * half + 4, i, :]
                    copy(out, bank[:, 0:4 * width].rearrange("p (j n) -> p j n", j=4),
                         scale=E0 ** -0.5).then_inc(sem["m_hi"], 1)
            setup_end(act)

            def affine(chain, s, norm_name, content, g, beta, cols=S):
                act.wait_ge(sem[filled((chain, s, content))], FILL[chain, s, content])
                nc.scalar.activation(xz[:, 0:cols], Y[:, 0:cols], ACT.Identity,
                                     bias=cols_of[beta][:, 0:1] if beta else 0.0,
                                     scale=cols_of[g][:, 0:1]).then_inc(sem["chain_bank_read"], 1)

            def value_copy(chain, s, k):
                act.wait_ge(sem[filled((chain, s, f"v{k}"))], FILL[chain, s, f"v{k}"])
                copy(v0[s][:, k // 2, 512 * (k % 2):512 * (k % 2) + 512], Y[:, :]).then_inc(sem["chain_bank_read"], 1)

            def stack_high(chain, s, kb_count):
                act.wait_ge(sem["natural"], each_layer(s, chain))
                copy(f32r(q_stack[s][:, :, :, 0:8]), heads4(nat_q[:, :, :]))
                keys = heads4(nat_kv[:, 0:kb_count, 0:D])
                copy(f32r(k_stack[s][:, 0:kb_count, :, 0:8]), keys).then_inc(sem["high_once"], 1)
                copy(f32r(q_stack[s][:, :, :, 8:16]), heads4(nat_q[:, :, :]))
                copy(f32r(k_stack[s][:, 0:kb_count, :, 16:24]), keys).then_inc(sem["high"], 1)
                if chain == "mid1":
                    act.wait_ge(sem["pads"], nth("pads", s, 2))
                copy(v_pad[s][:, 0:kb_count, :, 0:8],
                     heads4(nat_kv[:, 0:kb_count, D:2 * D])).then_inc(sem["v_padded"], 1)

            def turned_stacks(chain, s, kb_count):
                yield "qt0"
                act.wait_ge(sem[filled((chain, s, "qt0"))], FILL[chain, s, "qt0"])
                copy(q_t[s][:, 0:2, :], Y[:, :].rearrange("p (g q) -> p g q", g=2)).then_inc(sem["chain_bank_read"], 1)
                for r in range(0, kb_count, 2):
                    yield f"kt{r}"
                    act.wait_ge(sem[filled((chain, s, f"kt{r}"))], FILL[chain, s, f"kt{r}"])
                    copy(keys_turned(s, r, kb_count), keys_in_bank(kb_count, Y)).then_inc(sem["chain_bank_read"], 1)

            def table_for(func):
                at = 0 if func == ACT.Exp else 1
                nc.scalar.activation(table_probe[:, at:at + 1], ident[:, 0:1], func)

            def chain(name, s):
                if name == "start":
                    yield "ctx"
                    act.wait_ge(sem[filled((name, s, "ctx"))], FILL[name, s, "ctx"])
                    copy(ctx_hi[s][:, :], Y[0:C, :]).then_inc(sem["ctx_high"], 1)
                    yield "ln1"
                    affine(name, s, "ln1", "ln1", "ln1g", "ln1b")
                    for k in (0, 2):
                        yield f"v{k}"
                        value_copy(name, s, k)
                elif name == "mid0":
                    yield "v0"
                    value_copy(name, s, 0)
                    yield "ln2"
                    affine(name, s, "ln2", "ln2", "ln2g", "ln2b")
                    for k in (2, 4, 6):
                        if k == 4:
                            yield "audio_t"
                            affine(name, s, "audio", "audio_t", "g2", "beta2", cols=T)
                        yield f"v{k}"
                        value_copy(name, s, k)
                elif name == "mid1":
                    yield "ln3"
                    affine(name, s, "ln3", "ln3", "ln3g", "ln3b")
                    yield "gate"
                    table_for(ACT.Gelu_apprx_tanh)
                    for r in range(2):
                        act.wait_ge(sem[filled((name, s, f"g{r}"))], FILL[name, s, f"g{r}"])
                        for k in range(2):
                            j = 2 * r + k
                            last = nc.scalar.activation(hidden[s][:, j, :], bank_of((name, s, f"g{r}"))[:, k * S:(k + 1) * S],
                                                        ACT.Gelu_apprx_tanh, bias=cols_of["bff1"][:, 4 + j:5 + j])
                        last.then_inc(sem[bank_read((name, s, f"g{r}"))], 1)
                    table_for(ACT.Exp)
                    yield "x1_t"
                    act.wait_ge(sem[filled((name, s, "x1_t"))], FILL[name, s, "x1_t"])
                    copy(x_hi[s][:, :], Y[:, 0:S]).then_inc(sem["x1_high"], 1)
                    yield "text_t"
                    affine(name, s, "text", "text_t", "g1", "beta1")
                    for qb in range(QB):
                        yield f"e{qb}"
                        act.wait_ge(sem["l1_max"], nth("l1_max", s, qb + 1))
                        nc.scalar.activation(probs1[s][:, qb, :], bank_of((name, s, f"s{qb}"))[:, :], ACT.Exp, bias=l1_nmax[:, qb:qb + 1],
                                             accum_out=l1_sums[:, qb:qb + 1]).then_inc(sem[bank_read((name, s, f"s{qb}"))], 1)
                    yield "p0"
                    act.wait_ge(sem[filled((name, s, "p0"))], FILL[name, s, "p0"])
                    copy(probs1_t[s][:, :, 0:P], Y[:, :].rearrange("p (k q) -> p k q", k=TB)
                         ).then_inc(sem["chain_bank_read"], 1)
                    yield "sc"
                    act.wait_ge(sem[filled((name, s, "pv"))], FILL[name, s, "pv"])
                    copy(l1_scale[s], Y[:, S:2 * S]).then_inc(sem["l1_scale"], 1)
                    yield "m1_t"
                    affine(name, s, "m1", "m1_t", "m1g", "m1b")
                    yield "high"
                    stack_high(name, s, QB)
                    yield from turned_stacks(name, s, QB)
                elif name == "mid2":
                    yield "m2_t"
                    affine(name, s, "m2", "m2_t", "m2g", "m2b")
                    yield "high"
                    stack_high(name, s, TB)
                    yield from turned_stacks(name, s, TB)
                elif name == "mid3":
                    yield "m3_t"
                    affine(name, s, "m3", "m3_t", "m3g", "m3b")
                    yield "up"
                    table_for(ACT.Gelu)
                    for r in range(2):
                        act.wait_ge(sem[filled((name, s, f"up{r}"))], FILL[name, s, f"up{r}"])
                        for k in range(2):
                            j = 2 * r + k
                            last = nc.scalar.activation(hidden[s][:, j, :], bank_of((name, s, f"up{r}"))[:, k * S:(k + 1) * S], ACT.Gelu,
                                                        bias=cols_of["bmlp1"][:, j:j + 1])
                        last.then_inc(sem[bank_read((name, s, f"up{r}"))], 1)
                    table_for(ACT.Exp)
                    yield "rms_t"
                    affine(name, s, "rms", "rms_t", "normw", None)
                    yield "root"
                    act.wait_ge(sem["squares"], nth("squares", s))
                    nc.scalar.activation(norm[:, :, :], ss[:, :, :], ACT.Sqrt).then_inc(sem["root"], 1)
                    table_for(ACT.Exp)
                    yield "high"
                    stack_high(name, s, TB)
                    yield from turned_stacks(name, s, TB)

            def t_high(ph, h):
                act.wait_ge(sem["attention_t"], ph.at("t", h + 1))
                if h >= 2:
                    act.wait_ge(sem["attention_scores"], ph.at("scores", (h - 1) * ph.per_head))
                copy(t_hi[0:ph.t_rows, h % 2, :], X[0:ph.t_rows, 0:S]).then_inc(sem["attention_t_hi"], 1)

            def exps(ph, u):
                h, part, n = u // ph.per_head, u % ph.per_head, ph.at("turned", u)
                bank = SC[ph.at("scores", u) % 3]
                if ph.key_major:
                    act.wait_ge(sem["attention_scores"], ph.at("scores", u + 1))
                    used = (h - ph.slots) // ph.group + 1 if h >= ph.slots else 0
                    if ph.at("heads", used) > 0:
                        act.wait_ge(sem["attention_heads"], ph.at("heads", used))
                    nc.scalar.activation(probs_t[:, h % ph.slots, 2 * part:2 * part + 2, :],
                                         bank[:, :].rearrange("p (k q) -> p k q", k=2), ACT.Exp,
                                         scale=float(np.sqrt(np.float32(E2)))).then_inc(sem["attention_exp"], 1)
                    return
                act.wait_ge(sem["attention_max"], ph.at("max", u + 1))
                if ph.at("turned", u) >= 3:
                    act.wait_ge(sem["attention_turned"], ph.at("turned", u - 2))
                for k, qb in enumerate(range(QB) if ph.per_head == 1 else (part,)):
                    last = nc.scalar.activation(probs[:, n % 3, k * S:k * S + ph.keys],
                                                bank[:, k * S:k * S + ph.keys], ACT.Exp,
                                                bias=nmax[:, h * QB + qb:h * QB + qb + 1],
                                                accum_out=sums[:, qb, h:h + 1])
                last.then_inc(sem["attention_exp"], 1)

            def turned_copy(ph, u):
                h = u // ph.per_head
                act.wait_ge(sem["attention_turned"], ph.at("turned", u + 1))
                if h >= ph.slots:
                    act.wait_ge(sem["attention_heads"], ph.at("heads", (h - ph.slots) // ph.group + 1))
                copy(turned_place(ph, u), turned_in_bank(ph, 0)).then_inc(sem["attention_copied0"], 1)

            def scale_copy(ph, g):
                act.wait_ge(sem["attention_heads"], ph.at("heads", g + 1))
                if ph.at("out_scaled", g - 1) > 0:
                    act.wait_ge(sem["attention_out_scaled"], ph.at("out_scaled", g - 1))
                copy(scale_t[:, g % 2, :], O[:, S:2 * S]).then_inc(sem["attention_scale"], 1)

            def attention(ph):
                if ph.t_rows:
                    t_high(ph, 0)
                    t_high(ph, 1)
                exps(ph, 0)
                for h in early_t(ph):
                    t_high(ph, h)
                yield
                for u in range(ph.units):
                    if u + 1 < ph.units:
                        exps(ph, u + 1)
                    if not ph.key_major and u % 2 == 0:
                        turned_copy(ph, u)
                    if next_t(ph, u):
                        t_high(ph, next_t(ph, u))
                    g = ph.ends_group(u)
                    if g is not None and not ph.key_major:
                        scale_copy(ph, g)
                    yield
                if not ph.key_major:
                    scale_copy(ph, ph.groups - 1)

            def segment(name, ends):
                enter(name)
                run_rounds(name, attention, chain)
                segment_end(act, ends)

            segment("first", 1)
            with act.Fori(0, LOOPS) as b:
                segment("loop", b + 2)
            segment("last", LOOPS + 2)

        @block.vector
        def _(dve):
            chained = {"setup_chain": 0, "segment_chain": 0}

            def then(ins, name="segment_chain"):
                ins.then_inc(sem[name], 1)
                chained[name] += 1
                dve.wait_ge(sem[name], chained[name])

            def low_part(out, full, high):
                return nc.vector.tensor_tensor(out, full, f32(high), ALU.subtract)

            dve.wait_ge(sem["raw_loaded"], 16 * n_raw)
            q_scale = float(E2) ** -0.5
            then(nc.vector.tensor_scalar(raw["wsa"][:, 0:D], raw["wsa"][:, 0:D], q_scale, None, ALU.mult),
                 "setup_chain")
            nc.vector.tensor_scalar(raw["wcaq"], raw["wcaq"], q_scale, None, ALU.mult).then_inc(sem["raw_scaled"], 1)
            dve.wait_ge(sem["raw_scaled"], 1)
            for n, name in enumerate(split):
                dve.wait_ge(sem["w_hi"], n + 1)
                low_part(split[name][1][:, :], raw[name], split[name][0][:, :]).then_inc(sem["w_lo"], 1)
            for fill in range(4):
                layer, half = fill // 2, fill % 2
                width = (D, C)[layer]
                dve.wait_ge(sem["m_hi"], 2 * fill + 2)
                for i in range(2):
                    bank = (SC[0], SC[1], PT[0], PT[1], O, X, Y, SC[2])[2 * fill + i]
                    view = lambda m: m[:, :, :].rearrange("p (j i) n -> p j i n", i=2)[:, 4 * half:4 * half + 4, i, :]
                    src = bank[:, 0:4 * width].rearrange("p (j n) -> p j n", j=4)
                    nc.vector.scalar_tensor_tensor(view(m_lo[layer]), src, E0 ** -0.5, f32(view(m_hi[layer])),
                                                   op0=ALU.mult, op1=ALU.subtract).then_inc(sem["m_split"], 1)
            dve.wait_ge(sem["kept_loaded"], 16 * n_kept)
            for tile in (rows_of["bsa"][:, 0:D], rows_of["bcaq"][:, :]):
                then(nc.vector.tensor_scalar(tile, tile, q_scale, None, ALU.mult), "setup_chain")
            for name in ("g1", "beta1"):
                then(nc.vector.tensor_scalar(cols_of[name][:, :], cols_of[name][:, :], float(D) ** -0.5, None,
                                             ALU.mult), "setup_chain")
            setup_end(dve)

            def in_bank(blocks):
                return Y[:, 0:blocks * D].rearrange("p (b n) -> p b n", b=blocks)

            def statistics(src, blocks):
                for k in range(blocks):
                    last = nc.vector.bn_stats(stats[:, k, :], src[:, k, :])
                then(last)
                for k in range(blocks):
                    last = nc.vector.bn_aggr(moments[:, k, :], stats[:, k, :])
                then(last)
                nc.vector.tensor_scalar(var_eps[:, 0:blocks], moments[:, 0:blocks, 1], EPS, None,
                                        ALU.add).then_inc(sem["var"], 1)

            def normalised(key, src, blocks=QB):
                dve.wait_ge(sem["rstd"], NORM[key])
                for k in range(blocks):
                    last = nc.vector.tensor_scalar(xhat[:, k, :], src[:, k, :], moments[:, k, 0:1], rstd[:, k:k + 1],
                                                   ALU.subtract, ALU.mult)
                last.then_inc(sem["hat"], 1)
                dve.wait_ge(sem["hat"], NORM[key])

            def split_x(chain, s, norm_name, content, hi=None, lo=None, cols=S):
                hi, lo = (x_hi[s][:, :], x_lo[s][:, :]) if hi is None else (hi, lo)
                dve.wait_ge(sem[bank_read((chain, s, content))], FILL[chain, s, content])
                then(nc.vector.tensor_copy(hi, xz[:, 0:cols]))
                low_part(lo, xz[:, 0:cols], hi).then_inc(sem["split"], 1)

            def row(name, blocks, cols=slice(None)):
                r = rows_of[name][:, cols].unsqueeze(1)
                return r.to_broadcast([P, blocks, r.shape[2]])

            def add_row(s, name):
                then(nc.vector.tensor_tensor(x[s][:, :, :], x[s][:, :, :], row(name, QB), ALU.add))

            def add_projected(chain, s, content):
                dve.wait_ge(sem[filled((chain, s, content))], FILL[chain, s, content])
                nc.vector.tensor_tensor(x[s][:, :, :], in_bank(QB), x[s][:, :, :], ALU.add
                                        ).then_inc(sem["chain_bank_read"], 1)
                dve.wait_ge(sem[bank_read((chain, s, content))], FILL[chain, s, content])

            def value_copy(chain, s, k):
                dve.wait_ge(sem[filled((chain, s, f"v{k}"))], FILL[chain, s, f"v{k}"])
                key = chain, s, f"v{k}"
                nc.vector.tensor_copy(v0[s][:, k // 2, 512 * (k % 2):512 * (k % 2) + 512], bank_of(key)[:, :]
                                      ).then_inc(sem[bank_read(key)], 1)

            def stack_low(chain, s, kb_count):
                if chain != "mid2":
                    nc.vector.memset(q_stack[s][:, :, :, 24:32], 0.0)
                dve.wait_ge(sem["high_once"], each_layer(s, chain))
                nc.vector.tensor_tensor(f32r(q_stack[s][:, :, :, 16:24]), heads4(nat_q[:, :, :]),
                                        q_stack[s][:, :, :, 0:8], ALU.subtract)
                nc.vector.tensor_tensor(f32r(k_stack[s][:, 0:kb_count, :, 8:16]), heads4(nat_kv[:, 0:kb_count, 0:D]),
                                        k_stack[s][:, 0:kb_count, :, 0:8], ALU.subtract).then_inc(sem["stacked"], 1)

            def turned_stacks(chain, s, kb_count):
                yield "qt1"
                dve.wait_ge(sem[filled((chain, s, "qt1"))], FILL[chain, s, "qt1"])
                key = chain, s, "qt1"
                nc.vector.tensor_copy(q_t[s][:, 2:4, :], bank_of(key)[:, :].rearrange("p (g q) -> p g q", g=2)
                                      ).then_inc(sem[bank_read(key)], 1)
                for r in range(1, kb_count, 2):
                    yield f"kt{r}"
                    dve.wait_ge(sem[filled((chain, s, f"kt{r}"))], FILL[chain, s, f"kt{r}"])
                    key = chain, s, f"kt{r}"
                    nc.vector.tensor_copy(keys_turned(s, r, kb_count), keys_in_bank(kb_count, bank_of(key))
                                          ).then_inc(sem[bank_read(key)], 1)

            def rotate(s, y4, blocks, at):
                cos = rope_cos[:, 0:blocks, :].unsqueeze(2).to_broadcast([P, blocks, H, E2])
                sin = rope_sin[:, 0:blocks, :].unsqueeze(2).to_broadcast([P, blocks, H, E2])
                tmp, prod = rope_tmp[s][:, 0:blocks], rope_prod[s][:, 0:blocks]
                half = E2 // 2
                nc.vector.tensor_tensor(tmp[:, :, :, 0:half], y4[:, :, :, half:E2], sin[:, :, :, 0:half], ALU.mult)
                nc.vector.tensor_tensor(tmp[:, :, :, half:E2], y4[:, :, :, 0:half], sin[:, :, :, half:E2], ALU.mult)
                then(nc.vector.tensor_tensor(prod, y4, cos, ALU.mult))
                then(nc.vector.tensor_tensor(y4, tmp, prod, ALU.add))
                then(nc.vector.tensor_tensor(prod, y4, y4, ALU.mult))
                then(nc.vector.tensor_reduce(ss[:, at:at + blocks, :], prod, AX.X, ALU.add))

            def chain(name, s):
                xs = x[s]
                if name == "start":
                    yield "ctx"
                    dve.wait_ge(sem["ctx_high"], nth("ctx_high", s))
                    low_part(ctx_lo[s][:, :], Y[0:C, :], ctx_hi[s][:, :]).then_inc(sem["chain_bank_read"], 1)
                    yield "stats"
                    dve.wait_ge(sem[f"x_loaded{s}"], 16)
                    statistics(xs, QB)
                    yield "hat"
                    normalised((name, s, "ln1"), xs)
                    add_row(s, "bo1")
                    yield "split"
                    split_x(name, s, "ln1", "ln1")
                    for k in (1, 3):
                        yield f"v{k}"
                        value_copy(name, s, k)
                elif name == "mid0":
                    yield "audio"
                    dve.wait_ge(sem[filled((name, s, "audio"))], FILL[name, s, "audio"])
                    nc.vector.tensor_tensor(v1[s], in_bank(TB), row("baudio", TB), ALU.add
                                            ).then_inc(sem["chain_bank_read"], 1)
                    dve.wait_ge(sem[bank_read((name, s, "audio"))], FILL[name, s, "audio"])
                    yield "wo"
                    add_projected(name, s, "wo")
                    yield "stats"
                    statistics(xs, QB)
                    yield "hat"
                    normalised((name, s, "ln2"), xs)
                    add_row(s, "bo2")
                    yield "astats"
                    statistics(v1[s], TB)
                    yield "v1"
                    value_copy(name, s, 1)
                    yield "split"
                    split_x(name, s, "ln2", "ln2")
                    yield "ahat"
                    normalised((name, s, "audio"), v1[s], TB)
                    yield "v3"
                    value_copy(name, s, 3)
                    yield "asplit"
                    split_x(name, s, "audio", "audio_t", k1_hi[s], k1_lo[s], T)
                    for k in (5, 7):
                        yield f"v{k}"
                        value_copy(name, s, k)
                elif name == "mid1":
                    yield "wo"
                    add_projected(name, s, "wo")
                    yield "stats"
                    statistics(xs, QB)
                    yield "hat"
                    normalised((name, s, "ln3"), xs)
                    add_row(s, "bff2")
                    for r in range(2):
                        yield f"l{r}"
                        dve.wait_ge(sem[filled((name, s, f"l{r}"))], FILL[name, s, f"l{r}"])
                        for k in range(2):
                            j = 2 * r + k
                            last = nc.vector.scalar_tensor_tensor(
                                hidden[s][:, j, :], bank_of((name, s, f"l{r}"))[:, k * S:(k + 1) * S], cols_of["bff1"][:, j:j + 1],
                                hidden[s][:, j, :], op0=ALU.add, op1=ALU.mult)
                        last.then_inc(sem[bank_read((name, s, f"l{r}"))], 1)
                    yield "down"
                    add_projected(name, s, "down")
                    yield "x1_lo"
                    dve.wait_ge(sem["x1_high"], nth("x1_high", s))
                    low_part(x_lo[s][:, :], Y[:, 0:S], x_hi[s][:, :]).then_inc(sem["chain_bank_read"], 1)
                    yield "tstats"
                    dve.wait_ge(sem[filled((name, s, "text"))], FILL[name, s, "text"])
                    nc.vector.tensor_tensor(nat_q[:, :, :], in_bank(QB), row("btext", QB), ALU.add
                                            ).then_inc(sem["chain_bank_read"], 1)
                    dve.wait_ge(sem[bank_read((name, s, "text"))], FILL[name, s, "text"])
                    statistics(nat_q, QB)
                    yield "that"
                    normalised((name, s, "text"), nat_q)
                    add_row(s, "bout")
                    yield "tsplit"
                    split_x(name, s, "text", "text_t")
                    for qb in range(QB):
                        yield f"s{qb}"
                        dve.wait_ge(sem[filled((name, s, f"s{qb}"))], FILL[name, s, f"s{qb}"])
                        nc.vector.tensor_reduce(l1_nmax[:, qb:qb + 1], bank_of((name, s, f"s{qb}"))[:, :], AX.X, ALU.max,
                                                negate=True).then_inc(sem["l1_max"], 1)
                    yield "p1"
                    dve.wait_ge(sem[bank_read((name, s, "s1"))], FILL[name, s, "s1"])
                    then(nc.vector.reciprocal(l1_sums[:, :], l1_sums[:, :]))
                    nc.vector.tensor_copy(l1_rinv[s], l1_sums[:, :].unsqueeze(2).to_broadcast([P, QB, P])
                                          ).then_inc(sem["l1_rinv"], 1)
                    dve.wait_ge(sem[filled((name, s, "p1"))], FILL[name, s, "p1"])
                    nc.vector.tensor_copy(probs1_t[s][:, :, P:2 * P], bank_of((name, s, "p1"))[:, :].rearrange("p (k q) -> p k q", k=TB)
                                          ).then_inc(sem[bank_read((name, s, "p1"))], 1)
                    yield "sc"
                    dve.wait_ge(sem["l1_scale"], nth("l1_scale", s))
                    nc.vector.tensor_tensor(out_t[s][:, 0, :], Y[:, 0:S], l1_scale[s], ALU.mult
                                            ).then_inc(sem["chain_bank_read"], 1)
                    yield "wout"
                    add_projected(name, s, "wout")
                    yield "ostats"
                    statistics(xs, QB)
                    yield "ohat"
                    normalised((name, s, "out1"), xs)
                    then(nc.vector.tensor_tensor(xs[:, :, :], xhat[:, 0:QB, :], row("gout", QB), ALU.mult))
                    add_row(s, "betaout")
                    yield "mstats"
                    statistics(xs, QB)
                    yield "mhat"
                    normalised((name, s, "m1"), xs)
                    add_row(s, "bosa")
                    yield "msplit"
                    split_x(name, s, "m1", "m1_t")
                    for qb in range(QB):
                        yield f"qkv{qb}"
                        dve.wait_ge(sem[filled((name, s, f"qkv{qb}"))], FILL[name, s, f"qkv{qb}"])
                        nc.vector.tensor_tensor(nat_q[:, qb, :], bank_of((name, s, f"qkv{qb}"))[:, 0:D], rows_of["bsa"][:, 0:D], ALU.add)
                        nc.vector.tensor_tensor(nat_kv[:, qb, :], bank_of((name, s, f"qkv{qb}"))[:, D:3 * D], rows_of["bsa"][:, D:3 * D], ALU.add
                                                ).then_inc(sem[bank_read((name, s, f"qkv{qb}"))], 1)
                    dve.wait_ge(sem[bank_read((name, s, "qkv0"))], FILL[name, s, "qkv0"])
                    dve.wait_ge(sem[bank_read((name, s, "qkv1"))], FILL[name, s, "qkv1"])
                    nc.vector.memset(k_stack[s][:, :, :, 24:32], 0.0).then_inc(sem["natural"], 1)
                    yield "low"
                    stack_low(name, s, QB)
                    yield from turned_stacks(name, s, QB)
                elif name == "mid2":
                    yield "wo"
                    add_projected(name, s, "wo")
                    yield "stats"
                    statistics(xs, QB)
                    yield "hat"
                    normalised((name, s, "m2"), xs)
                    add_row(s, "boca")
                    for r in range(2):
                        yield f"kv{r}"
                        dve.wait_ge(sem[filled((name, s, f"kv{r}"))], FILL[name, s, f"kv{r}"])
                        nc.vector.tensor_tensor(nat_kv[:, 2 * r:2 * r + 2, :], bank_of((name, s, f"kv{r}"))[:, :].rearrange("p (b n) -> p b n", b=2),
                                                row("bcakv", 2), ALU.add).then_inc(sem[bank_read((name, s, f"kv{r}"))], 1)
                    yield "msplit"
                    split_x(name, s, "m2", "m2_t")
                    yield "q"
                    dve.wait_ge(sem[filled((name, s, "q"))], FILL[name, s, "q"])
                    nc.vector.tensor_tensor(nat_q[:, :, :], in_bank(QB), row("bcaq", QB), ALU.add
                                            ).then_inc(sem["chain_bank_read"], 1)
                    dve.wait_ge(sem[bank_read((name, s, "q"))], FILL[name, s, "q"])
                    dve.wait_ge(sem[bank_read((name, s, "kv1"))], FILL[name, s, "kv1"])
                    nc.vector.memset(q_stack[s][:, :, :, 24:32], 0.0).then_inc(sem["natural"], 1)
                    yield "low"
                    stack_low(name, s, TB)
                    yield from turned_stacks(name, s, TB)
                elif name == "mid3":
                    yield "wo"
                    add_projected(name, s, "wo")
                    yield "stats"
                    statistics(xs, QB)
                    yield "hat"
                    normalised((name, s, "m3"), xs)
                    add_row(s, "bmlp2")
                    yield "down"
                    add_projected(name, s, "down")
                    yield "squares"
                    then(nc.vector.tensor_tensor(xhat[:, 0:QB, :], xs[:, :, :], xs[:, :, :], ALU.mult))
                    then(nc.vector.tensor_reduce(moments[:, 0:QB, 0], xhat[:, 0:QB, :], AX.X, ALU.add))
                    nc.vector.tensor_scalar(var_eps[:, 0:QB], moments[:, 0:QB, 0], 1.0 / D, EPS, ALU.mult, ALU.add
                                            ).then_inc(sem["var"], 1)
                    yield "rmshat"
                    dve.wait_ge(sem["rstd"], NORM[name, s, "rms"])
                    for k in range(QB):
                        last = nc.vector.tensor_scalar(xhat[:, k, :], xs[:, k, :], rstd[:, k:k + 1], None, ALU.mult)
                    last.then_inc(sem["hat"], 1)
                    for r in range(2):
                        yield f"kv{r}"
                        dve.wait_ge(sem[filled((name, s, f"kv{r}"))], FILL[name, s, f"kv{r}"])
                        nc.vector.tensor_copy(nat_kv[:, 2 * r:2 * r + 2, :], bank_of((name, s, f"kv{r}"))[:, :].rearrange("p (b n) -> p b n", b=2)
                                              ).then_inc(sem[bank_read((name, s, f"kv{r}"))], 1)
                    dve.wait_ge(sem[bank_read((name, s, "kv1"))], FILL[name, s, "kv1"])
                    dve.wait_ge(sem[bank_read((name, s, "kv0"))], FILL[name, s, "kv0"])
                    yield "krope"
                    rotate(s, heads4(nat_kv[:, :, 0:D]), TB, 0)
                    yield "rsplit"
                    split_x(name, s, "rms", "rms_t")
                    yield "q"
                    dve.wait_ge(sem[filled((name, s, "q"))], FILL[name, s, "q"])
                    nc.vector.tensor_copy(nat_q[:, :, :], in_bank(QB)).then_inc(sem["chain_bank_read"], 1)
                    dve.wait_ge(sem[bank_read((name, s, "q"))], FILL[name, s, "q"])
                    yield "qrope"
                    rotate(s, heads4(nat_q[:, :, :]), QB, TB)
                    nc.vector.tensor_scalar(ss[:, :, :], ss[:, :, :], EPS_L2 ** 2, None, ALU.max
                                            ).then_inc(sem["squares"], 1)
                    yield "unit"
                    dve.wait_ge(sem["root"], nth("root", s))
                    then(nc.vector.reciprocal(norm[:, :, :], norm[:, :, :]))
                    for y4, at, blocks in ((heads4(nat_kv[:, :, 0:D]), 0, TB), (heads4(nat_q[:, :, :]), TB, QB)):
                        last = nc.vector.tensor_tensor(y4, y4, norm[:, at:at + blocks, :].unsqueeze(3).to_broadcast(
                            [P, blocks, H, E2]), ALU.mult)
                    last.then_inc(sem["natural"], 1)
                    yield "low"
                    stack_low(name, s, TB)
                    yield from turned_stacks(name, s, TB)
                else:
                    yield "wo"
                    dve.wait_ge(sem[filled((name, s, "wo"))], FILL[name, s, "wo"])
                    nc.vector.tensor_tensor(xs[:, :, :], in_bank(QB), xs[:, :, :], ALU.add
                                            ).then_inc(sem["chain_bank_read"], 1)

            def maximum(ph, u):
                h, part = u // ph.per_head, u % ph.per_head
                dve.wait_ge(sem["attention_scores"], ph.at("scores", u + 1))
                bank = SC[ph.at("scores", u) % 3]
                if ph.per_head == 1:
                    out, src = nmax[:, h * QB:h * QB + QB], bank[:, :].rearrange("p (b k) -> p b k", b=QB)
                else:
                    out, src = nmax[:, h * QB + part:h * QB + part + 1], bank[:, :]
                nc.vector.tensor_reduce(out, src, AX.X, ALU.max, negate=True).then_inc(sem["attention_max"], 1)

            def t_low(ph, h):
                dve.wait_ge(sem["attention_t_hi"], ph.at("t_hi", h + 1))
                low_part(t_lo[0:ph.t_rows, h % 2, :], X[0:ph.t_rows, 0:S],
                         t_hi[0:ph.t_rows, h % 2, :]).then_inc(sem["attention_t_lo"], 1)

            def turned_copy(ph, u):
                h = u // ph.per_head
                dve.wait_ge(sem["attention_turned"], ph.at("turned", u + 1))
                if h >= ph.slots:
                    dve.wait_ge(sem["attention_heads"], ph.at("heads", (h - ph.slots) // ph.group + 1))
                nc.vector.tensor_copy(turned_place(ph, u), turned_in_bank(ph, 1)).then_inc(sem["attention_copied1"], 1)

            def inverse_sums(ph, g):
                dve.wait_ge(sem["attention_exp"], ph.at("exp", (g + 1) * ph.group * ph.per_head))
                s = inv[:, :, 0:ph.group]
                then(nc.vector.reciprocal(s, sums[:, :, g * ph.group:(g + 1) * ph.group]))
                nc.vector.tensor_copy(rinv[:, :, :].rearrange("p b (h c) -> p b h c", h=ph.group),
                                      s.unsqueeze(3).to_broadcast([P, QB, ph.group, ph.rows])
                                      ).then_inc(sem["attention_rinv"], 1)

            def scale_out(ph, g):
                dve.wait_ge(sem["attention_scale"], ph.at("scale", g + 1))
                nc.vector.tensor_tensor(out_t[ph.s][:, g, :], O[:, 0:S], scale_t[:, g % 2, :], ALU.mult
                                        ).then_inc(sem["attention_out_scaled"], 1)

            def quad_copy(ph, g):
                dve.wait_ge(sem["attention_heads"], ph.at("heads", g + 1))
                nc.vector.tensor_copy(scale_t[:, g % 2, :], O[:, 0:S]).then_inc(sem["l3_heads_copied"], 1)

            def quad_scale(ph, g):
                dve.wait_ge(sem["attention_scale"], ph.at("scale", g + 1))
                temp = out_t[ph.s][:, QUADS + g % 2, :]
                then(nc.vector.reciprocal(temp, O[:, S:2 * S]))
                nc.vector.tensor_tensor(out_t[ph.s][:, g, :], scale_t[:, g % 2, :], temp, ALU.mult
                                        ).then_inc(sem["attention_out_scaled"], 1)

            def attention(ph):
                if ph.key_major:
                    yield
                    for u in range(ph.units):
                        if ph.ends_group(u) is not None:
                            quad_copy(ph, ph.ends_group(u))
                        if ph.ends_group(u - 2) is not None:
                            quad_scale(ph, ph.ends_group(u - 2))
                        yield
                    quad_copy(ph, ph.groups - 1)
                    quad_scale(ph, ph.groups - 1)
                    return
                if ph.t_rows:
                    t_low(ph, 0)
                    t_low(ph, 1)
                maximum(ph, 0)
                maximum(ph, 1)
                for h in early_t(ph):
                    t_low(ph, h)
                yield
                for u in range(ph.units):
                    if u + 2 < ph.units:
                        maximum(ph, u + 2)
                    g = ph.ends_group(u)
                    if g is not None:
                        inverse_sums(ph, g)
                    if u % 2 == 1:
                        turned_copy(ph, u)
                    if next_t(ph, u):
                        t_low(ph, next_t(ph, u))
                    if g is not None:
                        scale_out(ph, g)
                    yield
                inverse_sums(ph, ph.groups - 1)
                scale_out(ph, ph.groups - 1)

            def segment(name, ends):
                enter(name)
                chained["segment_chain"] = 0
                run_rounds(name, attention, chain)
                segment_end(dve, ends)

            segment("first", 1)
            with dve.Fori(0, LOOPS) as b:
                segment("loop", b + 2)
            segment("last", LOOPS + 2)

        @block.gpsimd
        def _(pool):
            nc.gpsimd.memset(minus_half[:, :], -0.5)
            nc.gpsimd.memset(f32(q_mask[:, :, :]), 0.0)
            for k in range(3):
                nc.gpsimd.memset(wo_pad[k][:, :, :], 0.0).then_inc(sem["pads_clear"], 1)
            setup_end(pool)

            issued = {"attention_mask": 0, "rstd": 0, "pads": 0}

            def power(key, blocks=QB):
                if issued["attention_mask"]:
                    pool.wait_ge(sem["attention_mask"], issued["attention_mask"])
                if issued["pads"]:
                    pool.wait_ge(sem["pads"], issued["pads"])
                if issued["rstd"]:
                    pool.wait_ge(sem["rstd"], issued["rstd"])
                issued["rstd"] += 1
                pool.wait_ge(sem["var"], NORM[key])
                nc.gpsimd.tensor_tensor(rstd[:, 0:blocks], var_eps[:, 0:blocks], minus_half[:, 0:blocks],
                                        ALU.pow).then_inc(sem["rstd"], 1)

            def chain(name, s):
                steps = {"start": [("stats", "ln1")], "mid0": [("stats", "ln2"), ("astats", "audio")],
                         "mid1": [("stats", "ln3"), ("tstats", "text"), ("ostats", "out1"),
                                  ("mstats", "m1")],
                         "mid2": [("stats", "m2")], "mid3": [("stats", "m3"), ("squares", "rms")], "end": []}[name]
                for step, n in steps:
                    yield step
                    power((name, s, n), TB if n == "audio" else QB)
                    if n == "out1":
                        pool.wait_ge(sem[bank_read((name, s, "wout"))], FILL[name, s, "wout"])
                        pool.wait_ge(sem["rstd"], issued["rstd"])
                        nc.gpsimd.memset(v_pad[s][:, :, :, E2 + 1:32], 0.0).then_inc(sem["pads"], 1)
                        pool.wait_ge(sem["pads"], issued["pads"] + 1)
                        nc.gpsimd.memset(v_pad[s][:, :, :, E2:E2 + 1], 1.0).then_inc(sem["pads"], 1)
                        issued["pads"] += 2

            def mask(ph, h):
                g, i = h // 4, h % 4
                if h >= 4:
                    pool.wait_ge(sem["attention_scores"], ph.at("scores", (h - 3) * ph.per_head))
                if issued["rstd"]:
                    pool.wait_ge(sem["rstd"], issued["rstd"])
                if issued["pads"]:
                    pool.wait_ge(sem["pads"], issued["pads"])
                issued["attention_mask"] += 1
                rows = slice(32 * i, 32 * i + 32)
                nc.gpsimd.tensor_copy(q_mask[rows, i, :], f32(q_t[ph.s][rows, g, :])
                                      ).then_inc(sem["attention_mask"], 1)

            def attention(ph):
                if ph.masked:
                    name = {"self2": "mid1", "cross2": "mid2", "l3": "mid3"}[ph.name]
                    if precedes((name, ph.s), (ph.name, ph.s)):
                        pool.wait_ge(sem[bank_read((name, ph.s, "qt0"))], FILL[name, ph.s, "qt0"])
                        pool.wait_ge(sem[bank_read((name, ph.s, "qt1"))], FILL[name, ph.s, "qt1"])
                    if ph.before["scores"]:
                        pool.wait_ge(sem["attention_scores"], ph.at("scores", 0))
                    for h in range(3 // ph.per_head + 1):
                        mask(ph, h)
                yield
                for u in range(ph.units):
                    if u > 0 and ph.masked and (u + 3) % ph.per_head == 0 and (u + 3) // ph.per_head < H:
                        mask(ph, (u + 3) // ph.per_head)
                    yield

            def segment(name, ends):
                enter(name)
                issued.update(attention_mask=0, rstd=0, pads=0)
                run_rounds(name, attention, chain)
                segment_end(pool, ends)

            segment("first", 1)
            with pool.Fori(0, LOOPS) as b:
                segment("loop", b + 2)
            segment("last", LOOPS + 2)

        @block.sync
        def _(sp):
            for name, dst in CONSTANTS + RAW:
                sp.dma_start(dst, A[name]).then_inc(sem["raw_loaded"], 16)
            for name, dst in KEPT:
                sp.dma_start(dst, A[name]).then_inc(sem["kept_loaded"], 16)
            sp.wait_ge(sem["pads_clear"], 3)
            for k, name in enumerate(("sawo", "cawo", "l3wo")):
                for i in range(4):
                    sp.dma_start(wo_pad[k][32 * i:32 * i + E2, :, :], A[name][i]).then_inc(sem["wo_loaded"], 16)
            sp.wait_ge(sem["wo_loaded"], 16 * 12)
            setup_end(sp)

            def load(s, b):
                sp.dma_start(ctx_nat[s], A["ctx"][:, bass.ds(b * TB, TB), :]).then_inc(sem[f"ctx_loaded{s}"], 16)
                sp.dma_start(x[s][:, :, :], A["x"][:, bass.ds(b * QB, QB), :]).then_inc(sem[f"x_loaded{s}"], 16)

            def store(s, b):
                sp.wait_ge(sem[bank_read(("end", s, "wo"))], FILL["end", s, "wo"])
                sp.dma_start(y_out[:, bass.ds(b * QB, QB), :], x[s][:, :, :]).then_inc(sem[f"y_stored{s}"], 16)
                sp.wait_ge(sem[f"y_stored{s}"], 16)

            def segment_over():
                sp.wait_ge(sem["segment_done"], ENGINES - 1)
                sp.sem_clear(sem.ids()).then_inc(segments_over, 1)

            enter("first")
            load(0, 0)
            segment_over()
            with sp.Fori(0, LOOPS) as b:
                enter("loop")
                load(1, b * STREAMS + 1)
                store(0, b * STREAMS)
                load(0, b * STREAMS + 2)
                store(1, b * STREAMS + 1)
                segment_over()
            enter("last")
            load(1, B - 1)
            store(0, B - 2)
            store(1, B - 1)
            segment_over()


def rope_tables():
    inv = 1.0 / 10000.0 ** (np.arange(0, E2, 2, dtype=np.float32) / E2)
    freqs = np.einsum("i,j->ij", np.arange(T, dtype=np.float32), inv)
    emb = np.concatenate([freqs, freqs], axis=-1)
    sign = np.concatenate([-np.ones(E2 // 2, np.float32), np.ones(E2 // 2, np.float32)])
    by_partition = lambda t: t.astype(np.float32).reshape(TB, P, E2).transpose(1, 0, 2)
    return by_partition(np.cos(emb)), by_partition(np.sin(emb) * sign)


def layout(a):
    l0, l1, l2, l3 = (f"L{n}_xattn_" for n in range(4))
    cols = lambda v: v.reshape(-1, P).T
    out = {"x": a["x"], "ctx": a["ctx_768"]}
    out["ident"] = np.eye(P, dtype=np.float32)
    sum_rows = np.zeros((P, P), np.float32)
    for i in range(4):
        sum_rows[32 * i + E2, 32 * i:32 * i + 32] = 1.0
    out["sum_rows"] = sum_rows
    out["rope_cos"], out["rope_sin"] = rope_tables()
    for n in (1, 2):
        out[f"wqt{n - 1}"] = a[f"{l0}wq{n}"].T
        out[f"wkt{n - 1}"] = a[f"{l0}wk{n}"].T
        out[f"wv{n}"] = a[f"{l0}wv{n}"]
        out[f"wo{n}"] = a[f"{l0}wo{n}"]
        out[f"bo{n}"] = a[f"{l0}bo{n}"]
    for n in (1, 2, 3):
        out[f"ln{n}g"], out[f"ln{n}b"] = cols(a[f"{l0}ln{n}_g"]), cols(a[f"{l0}ln{n}_b"])
        out[f"m{n}g"], out[f"m{n}b"] = cols(a[f"{l2}ln{n}_g"]), cols(a[f"{l2}ln{n}_b"])
    out["wff1"], out["wff2"] = a[l0 + "w_ff1"], a[l0 + "w_ff2"]
    out["bff1"], out["bff2"] = cols(a[l0 + "b_ff1"]), a[l0 + "b_ff2"]
    out["wtext"], out["waudio"], out["wout1"] = a[l1 + "W_text"], a[l1 + "W_audio"], a[l1 + "W_out"]
    out["btext"], out["baudio"], out["bout"] = a[l1 + "b_text"], a[l1 + "b_audio"], a[l1 + "b_out"]
    for n in ("g1", "beta1", "g2", "beta2"):
        out[n] = cols(a[l1 + n])
    out["gout"], out["betaout"] = a[l1 + "g_out"], a[l1 + "beta_out"]
    for k in "qkv":
        out[f"saw{k}"], out[f"caw{k}"] = a[f"{l2}sa_w{k}"].T, a[f"{l2}ca_w{k}"].T
        out[f"sab{k}"], out[f"cab{k}"] = a[f"{l2}sa_b{k}"], a[f"{l2}ca_b{k}"]
    out["wcaq"], out["bcaq"] = out.pop("cawq"), out.pop("cabq")
    out["sawo"], out["cawo"], out["l3wo"] = a[l2 + "sa_wo"].T, a[l2 + "ca_wo"].T, a[l3 + "wout"]
    out["bosa"], out["boca"] = a[l2 + "sa_bo"], a[l2 + "ca_bo"]
    out["wmlp1"], out["wmlp2"] = a[l2 + "mlp_w1"].T, a[l2 + "mlp_w2"].T
    out["bmlp1"], out["bmlp2"] = cols(a[l2 + "mlp_b1"]), a[l2 + "mlp_b2"]
    out["wl3q"], out["wl3kv"], out["normw"] = a[l3 + "wq"], a[l3 + "wkv"], cols(a[l3 + "norm_w"])
    return {n: np.ascontiguousarray(v) for n, v in out.items()}


VIEWS = {"x": "b (q p) n -> p (b q) n", "ctx": "b (q p) n -> p (b q) n"}
VIEWS |= dict.fromkeys(("wqt0", "wkt0", "wqt1", "wkt1", "wo1", "wo2", "wff2", "wmlp2"), "(j p) n -> p j n")
VIEWS |= dict.fromkeys(("sawo", "cawo", "l3wo"), "(g i c) n -> i c g n")
SIZES = {"(j p) n -> p j n": {"p": P}, "(g i c) n -> i c g n": {"i": 4, "c": E2}, VIEWS["x"]: {"p": P}}
ROWS = ("bo1", "bo2", "bff2", "btext", "baudio", "bout", "gout", "betaout", "sabq", "sabk", "sabv", "bcaq",
        "cabk", "cabv", "bosa", "boca", "bmlp2")


def kernel(**inputs):
    from concourse import bacc
    from concourse.bass_utils import run_bass_kernel_spmd

    arrays = layout({n: np.asarray(v) for n, v in inputs.items()})
    nc = bacc.Bacc("TRN2", target_bir_lowering=False, num_devices=1, dynamic_dma_scratch_size=1024)
    A = {}
    for name, a in arrays.items():
        ap = nc.dram_tensor(name + "_dram", a.shape, mybir.dt.from_np(a.dtype), kind="ExternalInput").ap()
        if name in VIEWS:
            ap = ap.rearrange(VIEWS[name], **SIZES[VIEWS[name]])
        elif name in ROWS:
            ap = ap.partition_broadcast(P)
        A[name] = ap
    y = nc.dram_tensor("y_dram", arrays["x"].shape, F32, kind="ExternalOutput").ap().rearrange(VIEWS["x"], p=P)
    program(nc, A, y)
    r = run_bass_kernel_spmd(nc, [{n + "_dram": a for n, a in arrays.items()}], core_ids=[0])
    return r.results[0]["y_dram"]
```
